# Optimizing a Trainium2 kernel written in Bass

```python
import numpy as np
import jax
import jax.numpy as jnp

def _softmax(x, axis=-1):
    return jax.nn.softmax(x, axis=axis)

def _gelu(x):
    return jax.nn.gelu(x, approximate=True)

def _silu(x):
    return jax.nn.silu(x)

def _sigmoid(x):
    return jax.nn.sigmoid(x)

def _layernorm(x, axis=-1, eps=1e-05):
    m = jnp.mean(x, axis=axis, keepdims=True)
    v = jnp.var(x, axis=axis, keepdims=True)
    return (x - m) / jnp.sqrt(v + eps)

def _scatter_add(tgt, idx, src, axis=0):
    return tgt.at[idx].add(src)

def _segment_sum(src, seg, n):
    return jax.ops.segment_sum(src, seg, n)
kernel_name = 'mk_gnn_preln_d2_gnn_r8_7a28c6'

def setup_inputs(seed: int=0):
    np.random.seed(seed)
    _w = jnp.asarray

    def _rec_inputs():
        import jax
        import jax.numpy as jnp
        _gk = jax.random.key(seed)
        x = -0.0005121 + 1.001 * jax.random.normal(jax.random.fold_in(_gk, 1), (6250, 64), jnp.float32)
        _s = jax.random.randint(jax.random.fold_in(_gk, 2), (100000,), 0, 6250, jnp.int32)
        _d = jax.random.randint(jax.random.fold_in(_gk, 3), (100000,), 0, 6250, jnp.int32)
        _loop = jnp.arange(6250, dtype=jnp.int32)
        src = jnp.concatenate([_s, _d, _loop])
        dst = jnp.concatenate([_d, _s, _loop])
        _o = jnp.argsort(dst, stable=True)
        src = src[_o]
        dst = dst[_o]
        edge_attr_32 = -5.3897e-05 + 0.999841 * jax.random.normal(jax.random.fold_in(_gk, 12), (206250, 32), jnp.float32)
        return (x, src, dst, edge_attr_32)
    x, src, dst, edge_attr_32 = _rec_inputs()

    def _L0_gnn_setup():
        import jax, jax.numpy as jnp
        import numpy as np
        N_NODES = 6250
        N_EDGES = 100000
        IN_F = 64
        EDGE_F = 32
        OUT_F = 64
        LN_EPS = 1e-05
        key = jax.random.key(seed)
        ks = jax.random.split(key, 8)
        node_feat = jax.random.normal(ks[0], (N_NODES, IN_F), dtype=jnp.float32)
        edge_feat = jax.random.normal(ks[1], (N_EDGES, EDGE_F), dtype=jnp.float32)
        src = jax.random.randint(ks[2], (N_EDGES,), 0, N_NODES)
        dst = jax.random.randint(ks[3], (N_EDGES,), 0, N_NODES)
        W1 = jax.random.normal(ks[4], (IN_F + EDGE_F, OUT_F), dtype=jnp.float32) * (1.0 / np.sqrt(IN_F + EDGE_F))
        b1 = jnp.zeros((OUT_F,), jnp.float32)
        W2 = jax.random.normal(ks[5], (OUT_F, OUT_F), dtype=jnp.float32) * (1.0 / np.sqrt(OUT_F))
        b2 = jnp.zeros((OUT_F,), jnp.float32)
        gamma = jnp.ones((OUT_F,), jnp.float32)
        beta = jnp.zeros((OUT_F,), jnp.float32)
        return {'node_feat': node_feat, 'edge_feat': edge_feat, 'src': src, 'dst': dst, 'W1': W1, 'b1': b1, 'W2': W2, 'b2': b2, 'gamma': gamma, 'beta': beta}
    _L0_gnn_all = _L0_gnn_setup()
    _L0_gnn_in = {k: v for k, v in _L0_gnn_all.items() if k in ('W1', 'b1', 'W2', 'b2', 'gamma', 'beta')}
    del _L0_gnn_all

    def _L1_gnn_setup():
        import jax, jax.numpy as jnp
        import numpy as np
        N_NODES = 6250
        N_EDGES = 100000
        EMB = 64
        HEADS = 4
        key = jax.random.key(seed)
        k1, k2, k3, k4, k5, k6 = jax.random.split(key, 6)
        scale = 1.0 / np.sqrt(EMB)
        return {'embeds': jax.random.normal(k1, (N_NODES, EMB), dtype=jnp.float32), 'rows': jax.random.randint(k2, (N_EDGES,), 0, N_NODES, dtype=jnp.int64), 'cols': jax.random.randint(k3, (N_EDGES,), 0, N_NODES, dtype=jnp.int64), 'qTrans': jax.random.normal(k4, (EMB, EMB), dtype=jnp.float32) * scale, 'kTrans': jax.random.normal(k5, (EMB, EMB), dtype=jnp.float32) * scale, 'vTrans': jax.random.normal(k6, (EMB, EMB), dtype=jnp.float32) * scale}
    _L1_gnn_all = _L1_gnn_setup()
    _L1_gnn_in = {k: v for k, v in _L1_gnn_all.items() if k in ('qTrans', 'kTrans', 'vTrans')}
    del _L1_gnn_all
    return {'x': x, 'src': src, 'dst': dst, 'edge_attr_32': edge_attr_32, 'L0_gnn_W1': _L0_gnn_in['W1'], 'L0_gnn_b1': _L0_gnn_in['b1'], 'L0_gnn_W2': _L0_gnn_in['W2'], 'L0_gnn_b2': _L0_gnn_in['b2'], 'L0_gnn_gamma': _L0_gnn_in['gamma'], 'L0_gnn_beta': _L0_gnn_in['beta'], 'L1_gnn_qTrans': _L1_gnn_in['qTrans'], 'L1_gnn_kTrans': _L1_gnn_in['kTrans'], 'L1_gnn_vTrans': _L1_gnn_in['vTrans']}

def reference(x, src, dst, edge_attr_32, L0_gnn_W1, L0_gnn_b1, L0_gnn_W2, L0_gnn_b2, L0_gnn_gamma, L0_gnn_beta, L1_gnn_qTrans, L1_gnn_kTrans, L1_gnn_vTrans):
    import jax
    import jax.numpy as jnp

    def _L0_gnn_ref(node_feat, edge_feat, src, dst, W1, b1, W2, b2, gamma, beta):
        import jax, jax.numpy as jnp
        import numpy as np
        N_NODES = 6250
        N_EDGES = 100000
        IN_F = 64
        EDGE_F = 32
        OUT_F = 64
        LN_EPS = 1e-05
        n_nodes = node_feat.shape[0]
        z = jnp.concatenate([node_feat[src], edge_feat], axis=-1)
        m = jax.nn.relu(z @ W1 + b1) @ W2 + b2
        msum = jax.ops.segment_sum(m, dst, num_segments=n_nodes)
        deg = jax.ops.segment_sum(jnp.ones((dst.shape[0],), m.dtype), dst, num_segments=n_nodes)
        h_new = msum / jnp.maximum(deg, 1.0)[:, None]
        x = h_new + node_feat
        mu = jnp.mean(x, axis=-1, keepdims=True)
        var = jnp.mean((x - mu) ** 2, axis=-1, keepdims=True)
        return gamma * (x - mu) * jax.lax.rsqrt(var + LN_EPS) + beta

    def _L1_gnn_ref(embeds, rows, cols, qTrans, kTrans, vTrans):
        import jax, jax.numpy as jnp
        import numpy as np
        N_NODES = 6250
        N_EDGES = 100000
        EMB = 64
        HEADS = 4
        n_nodes = embeds.shape[0]
        head_dim = EMB // HEADS
        rowEmb = embeds[rows]
        colEmb = embeds[cols]
        q = (rowEmb @ qTrans).reshape(-1, HEADS, head_dim)
        k = (colEmb @ kTrans).reshape(-1, HEADS, head_dim)
        v = (colEmb @ vTrans).reshape(-1, HEADS, head_dim)
        att = jnp.einsum('ehd,ehd->eh', q, k)
        att = jnp.clip(att, -10.0, 10.0)
        expAtt = jnp.exp(att)
        attNorm = jax.ops.segment_sum(expAtt, rows, num_segments=n_nodes)[rows]
        att = expAtt / (attNorm + 1e-08)
        res = (att[:, :, None] * v).reshape(-1, EMB)
        out = jax.ops.segment_sum(res, rows, num_segments=n_nodes)
        return out
    h = jnp.maximum(_layernorm(x, axis=-1), 0.0)
    x = x + _L0_gnn_ref(h, edge_attr_32, src, dst, L0_gnn_W1, L0_gnn_b1, L0_gnn_W2, L0_gnn_b2, L0_gnn_gamma, L0_gnn_beta)
    h = jnp.maximum(_layernorm(x, axis=-1), 0.0)
    x = x + _L1_gnn_ref(h, src, dst, L1_gnn_qTrans, L1_gnn_kTrans, L1_gnn_vTrans)
    return x

_drawn_inputs = setup_inputs


def setup_inputs(seed=0):
    import zlib

    import numpy as np

    out = dict(_drawn_inputs(seed))
    spreads = {'L0_gnn_b1': (0.0, 0.1),
     'L0_gnn_b2': (0.0, 0.1),
     'L0_gnn_gamma': (1.0, 0.2),
     'L0_gnn_beta': (0.0, 0.1)}
    factors = {}
    for name, (base, spread) in spreads.items():
        noise = np.random.default_rng([zlib.crc32(name.encode()), seed]).standard_normal(out[name].shape)
        drawn = base * np.exp(spread * noise) if base else spread * noise
        out[name] = jnp.asarray(drawn.astype(out[name].dtype))
    for name, factor in factors.items():
        out[name] = (out[name] * factor).astype(out[name].dtype)
    return out
```

```python
from contextlib import ExitStack

import concourse.bass as bass
from concourse import mybir

F32 = mybir.dt.float32
BF16 = mybir.dt.bfloat16
I32 = mybir.dt.int32
ALU = mybir.AluOpType
ACT = mybir.ActivationFunctionType
AX = mybir.AxisListType
ds = bass.ds

P = 128
N_NODES = 6250
N_EDGES = 206250
F = 64
FE = 32
HEADS = 4
HD = F // HEADS
NT = -(-N_NODES // P)
LAST = N_NODES - (NT - 1) * P
NG = NT + 1
SI = 64

QT = 4
BODY = 13
ET = -(-N_EDGES // P)
GROUPS = ET // QT
BODIES = GROUPS // BODY
assert GROUPS * QT == ET and BODIES * BODY == GROUPS
EP = ET + 2 * QT
CHUNKS = [(0, 3), (3, 6), (6, 9), (9, 13)]

REC = FE + 4
MAIN = NG * P * SI
ROWS = MAIN + ET * P
LN_EPS = 1e-5
HB = 26
HBN = ET // HB
assert HBN * HB == ET


def col(ap, n):
    return ap.to_broadcast([P, n])


def apart(eng, t):
    eng.sem_inc(t["passed"], 1)


def gnn(nc, x, src, dst, edge, w1, b1, w2, b2, gamma, beta, wq, wk, wv, out, stop=99):
    binned = nc.dram_tensor("binned", [ROWS, REC], F32).ap()
    with ExitStack() as keep:
        def sb(name, shape, dt=F32, at=keep):
            return at.enter_context(nc.sbuf_tensor(name, shape, dt))

        t = {"passed": keep.enter_context(nc.semaphore("passed"))}
        t["x"] = sb("x_nodes", [P, NT, F])
        t["h"] = sb("h_nodes", [P, NT, F])
        t["row"] = sb("iota_row", [P, P])
        t["rowb"] = sb("iota_rowb", [P, P], BF16)
        t["part"] = sb("iota_part", [P, 1])
        t["idf"] = sb("identity_f32", [P, P])
        t["idb"] = sb("identity_bf16", [P, P], BF16)
        t["w1a"] = sb("w1a_b1", [F + 1, F])
        t["w1b"] = sb("w1b", [P, F])
        t["w2"] = sb("w2_b2", [F + 1, F])
        t["wqkv"] = sb("wqkv", [F, 3 * F])
        t["gb"] = sb("gamma_beta", [P, 2, F])
        t["eps"] = sb("eps", [P, 1])
        t["nover"] = sb("n_over", [1, 1], I32)
        t["A3"] = sb("a_parts", [P, NT, 3, F], BF16)
        with ExitStack() as ctx:
            t["hs"] = sb("src_tile", [P, EP], BF16, ctx)
            t["hd"] = sb("dst_tile", [P, EP], BF16, ctx)
            t["bin"] = sb("bin", [P, EP], F32, ctx)
            t["base"] = sb("bin_base", [P, ET], F32, ctx)
            t["meta"] = sb("meta", [P, ET, 4], F32, ctx)
            t["RD"] = sb("counts_over", [NG, 2, 2 * NG], F32, ctx)
            prepare(nc, t, x, src, dst, w1, b1, w2, b2, gamma, beta, wq, wk, wv, binned)
            if stop > 1:
                place(nc, t, edge, binned)
        if stop > 2:
            t["sum"] = sb("node_sums", [P, NT + 1, F + 1])
            t["ids"] = sb("places", [P, 2, NG * NT], BF16)
            layer0(nc, t, binned)
            if stop == 3:
                dump(nc, t["sum"][:, 1:NT + 1, :])
        if stop > 3:
            t["qkv"] = sb("qkv_parts", [P, NG, 3, 3 * F], BF16)
            nodes(nc, t)
            if stop == 4:
                dump(nc, t["x"][:, :, :])
        if stop > 4:
            t["out"] = sb("attention_sums", [P, NT, F + HEADS])
            layer1(nc, t, binned, out)


def dump(nc, what):
    dbg = nc.dram_tensor("dbg", list(what.shape), F32).ap()
    with nc.semaphore("dbg") as s, nc.Block() as block:
        @block.sync
        def _(sp):
            sp.dma_start(dbg, what).then_inc(s, 16)
            sp.wait_ge(s, 16)


def prepare(nc, t, x, src, dst, w1, b1, w2, b2, gamma, beta, wq, wk, wv, binned):
    FW = 12 * NT * REC // 12
    OW = ET * REC
    with ExitStack() as ctx:
        sb = lambda n, s, d=F32: ctx.enter_context(nc.sbuf_tensor(n, s, d))
        pb = lambda n, s, d=F32: ctx.enter_context(nc.psum_tensor(n, s, d))
        sem = lambda n: ctx.enter_context(nc.semaphore(n))
        fill = sb("fill", [P, OW // 13])
        ids = sb("ids", [P, 2, ET], I32)
        hi = sb("hi", [P, 2, ET], I32)
        lo = sb("lo", [P, 2, ET], I32)
        OH = sb("tile_onehots", [P, 2, 2, HB, NG], BF16)
        hist = pb("hist", [NG, NG])
        pref = pb("pref", [NG, 1])
        tot = pb("tot", [1, 1])
        tr = [pb(f"h_turned{i}", [F, 4 * P]) for i in range(2)]
        pa = [pb(f"a_sum{i}", [P, 4 * F]) for i in range(2)]
        hT = sb("hT", [F + 1, 2, 4 * P])
        ni = sb("ni", [NG, NG], I32)
        nf = sb("nf", [NG, NG])
        n0 = sb("n0", [NG, NG])
        z = sb("zeros", [NG, NG])
        inc = sb("inc", [NG, NG])
        upper = sb("upper", [NG, NG])
        ones = sb("ones", [NG, 1])
        prefs = sb("prefs", [NG, 1])
        sq = sb("sq", [P, NT, F])
        st = sb("st", [P, 3, NT])
        rest = sb("rest", [P, 2, 4 * F])
        s_fillset, s_fill, s_ids, s_x, s_w = (sem(n) for n in ("fill_set", "filled", "ids_in", "x_in", "weights_in"))
        s_iota, s_v, s_c, s_oh, s_hist, s_tab, s_t = (sem(n) for n in ("iotas", "v", "constants", "onehots", "counted", "table", "tab"))
        s_sqrt, s_h, s_tr, s_hT, s_pa, s_hi, s_rest, s_mid, s_a = (sem(n) for n in ("rooted", "h_ready", "turned", "hT_ready", "a_summed", "a_hi", "a_rest", "a_mid", "a_done"))
        s_xz = sem("x_zeroed")
        block = ctx.enter_context(nc.Block())

        @block.sync
        def _(sp):
            sp.dma_start(ids[:, 0, :], src).then_inc(s_ids, 16)
            sp.dma_start(ids[:, 1, :], dst).then_inc(s_ids, 16)
            sp.wait_ge(s_xz, 1)
            sp.dma_start(t["x"][:, 0:NT - 1, :], x[0:(NT - 1) * P, :].rearrange("(t p) f -> p t f", p=P)).then_inc(s_x, 16)
            sp.dma_start(t["x"][0:LAST, NT - 1, :], x[(NT - 1) * P:N_NODES, :]).then_inc(s_x, 16)
            sp.wait_ge(s_fillset, 1)
            for j in range(NG):
                sp.dma_start(binned[j * P * SI:(j + 1) * P * SI, :].rearrange("(p i) w -> p (i w)", i=SI)[:, 0:NT * REC],
                             fill[:, 0:NT * REC]).then_inc(s_fill, 16)
            over = binned[MAIN:ROWS, :].rearrange("(p i) w -> p (i w)", p=P)
            for c in range(13):
                sp.dma_start(over[:, c * (OW // 13):(c + 1) * (OW // 13)], fill[:, :]).then_inc(s_fill, 16)
            sp.wait_ge(s_fill, 16 * (NG + 13))

        @block.scalar
        def _(act):
            one = lambda v: v.rearrange("(a f) -> a f", a=1)
            act.dma_start(t["w1a"][0:F, :], w1[0:F, :]).then_inc(s_w, 16)
            act.dma_start(t["w1a"][F:F + 1, :], one(b1)).then_inc(s_w, 16)
            for k in range(4):
                act.dma_start(t["w1b"][FE * k:FE * k + FE, :], w1[F:F + FE, :]).then_inc(s_w, 16)
            act.dma_start(t["w2"][0:F, :], w2).then_inc(s_w, 16)
            act.dma_start(t["w2"][F:F + 1, :], one(b2)).then_inc(s_w, 16)
            for k, w in enumerate((wq, wk, wv)):
                act.dma_start(t["wqkv"][:, F * k:F * k + F], w).then_inc(s_w, 16)
            act.dma_start(t["gb"][:, 0, :], one(gamma).to_broadcast([P, F])).then_inc(s_w, 16)
            act.dma_start(t["gb"][:, 1, :], one(beta).to_broadcast([P, F])).then_inc(s_w, 16)
            act.wait_ge(s_h, 4)
            act.activation(st[:, 2, :], st[:, 1, :], ACT.Sqrt, bias=t["eps"][:, 0:1], scale=1.0 / F).then_inc(s_sqrt, 1)
            for g in range(NB_A):
                n = min(4, NT - 4 * g)
                act.wait_ge(s_tr, g + 1)
                if g >= 2:
                    act.wait_ge(s_pa, g - 1)
                act.copy(hT[0:F, g % 2, 0:n * P], tr[g % 2][:, 0:n * P]).then_inc(s_hT, 1)
                act.wait_ge(s_pa, g + 1)
                act.copy(t["A3"][:, 4 * g:4 * g + n, 0, :], pa[g % 2][:, 0:n * F].rearrange("p (t f) -> p t f", f=F)).then_inc(s_hi, 1)
                act.wait_ge(s_rest, g + 1)
                act.copy(t["A3"][:, 4 * g:4 * g + n, 1, :], rest[:, g % 2, 0:n * F].rearrange("p (t f) -> p t f", f=F)).then_inc(s_mid, 1)
            act.wait_ge(s_w, 16 * 13)

        @block.gpsimd
        def _(pool):
            pool.memset(t["x"][:, NT - 1, :], 0.0).then_inc(s_xz, 1)
            pool.iota(t["row"][:, :], [[1, P]], base=0, channel_multiplier=0, allow_small_or_imprecise_dtypes=True).then_inc(s_iota, 1)
            pool.iota(t["part"][:, :], [[1, 1]], base=0, channel_multiplier=1, allow_small_or_imprecise_dtypes=True).then_inc(s_iota, 1)
            pool.memset(fill[:, :], -1.0).then_inc(s_fillset, 1)
            pool.memset(t["eps"][:, :], LN_EPS).then_inc(s_iota, 1)
            pool.memset(t["hs"][:, ET:EP], float(NT)).then_inc(s_iota, 1)
            pool.memset(t["hd"][:, ET:EP], float(NT)).then_inc(s_iota, 1)

        @block.vector
        def _(v):
            n = [0]

            def link(ins):
                n[0] += 1
                ins.then_inc(s_v, 1)
                v.wait_ge(s_v, n[0])

            v.memset(z[:, :], 0.0)
            v.memset(t["bin"][:, ET:EP], 0.0)
            v.memset(ones[:, :], 1.0)
            v.memset(hT[F:F + 1, :, :], 1.0)
            v.wait_ge(s_iota, 5)
            v.tensor_copy(t["rowb"][:, :], t["row"][:, :])
            v.tensor_scalar(t["idf"][:, :], t["row"][:, :], t["part"][:, 0:1], None, ALU.is_equal)
            v.tensor_scalar(upper[:, :], t["row"][0:NG, 0:NG], t["part"][0:NG, 0:1], None, ALU.is_gt)
            v.tensor_scalar(t["idb"][:, :], t["row"][:, :], t["part"][:, 0:1], None, ALU.is_equal).then_inc(s_c, 1)
            v.wait_ge(s_ids, 32)
            v.tensor_scalar(hi[:, :, :], ids[:, :, :], 7, None, ALU.logical_shift_right)
            link(v.tensor_scalar(lo[:, :, :], ids[:, :, :], P - 1, None, ALU.bitwise_and))
            v.tensor_copy(t["hs"][:, 0:ET], hi[:, 0, :])
            v.tensor_copy(t["hd"][:, 0:ET], hi[:, 1, :])
            for k, a in enumerate((lo[:, 0, :], lo[:, 1, :], hi[:, 0, :], hi[:, 1, :])):
                last = v.tensor_copy(t["meta"][:, :, k], a)
            link(last)
            v.scalar_tensor_tensor(t["bin"][:, 0:ET], t["meta"][:, :, 3], float(SI), t["meta"][:, :, 2], ALU.mult, ALU.add)
            link(v.tensor_scalar(t["base"][:, :], t["meta"][:, :, 2], 1.0 / SI, None, ALU.mult))
            link(v.scalar_tensor_tensor(t["base"][:, :], t["meta"][:, :, 3], float(P), t["base"][:, :], ALU.mult, ALU.add))
            with v.Fori(0, HBN // 2) as i:
                for b in range(2):
                    v.wait_ge(s_hist, i * 2 + b + 1)
                    for k, a in enumerate((t["hs"], t["hd"])):
                        last = v.tensor_tensor(OH[:, b, k, :, :],
                                               a[:, ds((i * 2 + b) * HB, HB)].rearrange("p (t a) -> p t a", a=1).to_broadcast([P, HB, NG]),
                                               t["rowb"][:, 0:NG].rearrange("p (a n) -> p a n", a=1).to_broadcast([P, HB, NG]), ALU.is_equal)
                    last.then_inc(s_oh, 1)
            v.wait_ge(s_hist, HBN + 2)
            v.tensor_scalar(n0[:, :], hist[:, :], -1.0, 0.0, ALU.add, ALU.max)
            link(v.tensor_scalar(ni[:, :], hist[:, :], -1.0, 0.0, ALU.add, ALU.max))
            link(v.tensor_scalar(ni[:, :], ni[:, :], 7, None, ALU.logical_shift_right))
            link(v.tensor_copy(nf[:, :], ni[:, :]))
            link(v.tensor_tensor_scan(inc[:, :], nf[:, :], z[:, :], 0.0, ALU.add, ALU.add))
            v.tensor_tensor(n0[:, :], inc[:, :], nf[:, :], ALU.subtract).then_inc(s_tab, 1)
            v.wait_ge(s_t, 1)
            link(v.tensor_copy(prefs[:, :], pref[:, :]))
            link(v.tensor_scalar(n0[:, :], n0[:, :], prefs[:, 0:1], float(P), ALU.add, ALU.mult))
            for b in range(2):
                v.tensor_scalar(t["RD"][:, b, NG:], n0[:, :], float(MAIN - P), None, ALU.add)
                v.memset(t["RD"][:, b, 0:NG], 0.0)
            link(v.tensor_scalar(t["nover"][:, :], tot[:, :], float(QT - 1), float(QT), ALU.add, ALU.max))
            link(v.tensor_scalar(t["nover"][:, :], t["nover"][:, :], 2, None, ALU.logical_shift_right))
            v.wait_ge(s_x, 32)
            layer_norm(v, link, t["x"], t["h"], sq, st, s_h, s_sqrt, 1)
            v.tensor_scalar(t["h"][:, :, :], t["h"][:, :, :], 0.0, None, ALU.max).then_inc(s_h, 1)
            for g in range(NB_A):
                m = min(4, NT - 4 * g)
                v.wait_ge(s_hi, g + 1)
                v.tensor_tensor(rest[:, g % 2, 0:m * F], pa[g % 2][:, 0:m * F],
                                t["A3"][:, 4 * g:4 * g + m, 0, :], ALU.subtract).then_inc(s_rest, 1)
                v.wait_ge(s_mid, g + 1)
                v.tensor_tensor(t["A3"][:, 4 * g:4 * g + m, 2, :], rest[:, g % 2, 0:m * F].rearrange("p (t f) -> p t f", f=F),
                                t["A3"][:, 4 * g:4 * g + m, 1, :], ALU.subtract).then_inc(s_a, 1)

        @block.tensor
        def _(pe):
            pe.wait_ge(s_c, 1)
            pe.matmul(hist[:, :], z[:, :], z[:, :], start=True, stop=False, skip_group_check=True).then_inc(s_hist, 2)
            with pe.Fori(0, HBN // 2) as i:
                for b in range(2):
                    pe.wait_ge(s_oh, i * 2 + b + 1)
                    for k in range(HB):
                        last = pe.matmul(hist[:, :], OH[:, b, 1, k, :], OH[:, b, 0, k, :], start=False, stop=False, skip_group_check=True)
                    last.then_inc(s_hist, 1)
            pe.wait_ge(s_tab, 1)
            pe.matmul(pref[:, :], upper[:, :], inc[:, NG - 1:NG], start=True, stop=True)
            pe.matmul(tot[:, :], ones[:, :], inc[:, NG - 1:NG], start=True, stop=True).then_inc(s_t, 1)
            pe.wait_ge(s_h, 5)
            pe.wait_ge(s_w, 16 * 13)
            for g in range(NB_A + 1):
                if g < NB_A:
                    m = min(4, NT - 4 * g)
                    if g >= 2:
                        pe.wait_ge(s_hT, g - 1)
                    for k in range(m):
                        last = pe.transpose(tr[g % 2][:, k * P:k * P + P], t["h"][:, 4 * g + k, :], t["idf"][:, :])
                    last.then_inc(s_tr, 1)
                if g >= 1:
                    q = g - 1
                    m = min(4, NT - 4 * q)
                    pe.wait_ge(s_hT, q + 1)
                    if q >= 2:
                        pe.wait_ge(s_rest, q - 1)
                    for k in range(m):
                        last = pe.matmul(pa[q % 2][:, k * F:k * F + F], hT[:, q % 2, k * P:k * P + P], t["w1a"][:, :], start=True, stop=True)
                    last.then_inc(s_pa, 1)


NB_A = -(-NT // 4)


def layer_norm(v, link, x, y, sq, st, s_h, s_sqrt, roots):
    full = [P, NT, F]
    b = lambda a: a.rearrange("p (t a) -> p t a", a=1).to_broadcast(full)
    link(v.tensor_reduce(st[:, 0, :], x[:, :, :], AX.X, ALU.add))
    link(v.tensor_scalar(st[:, 0, :], st[:, 0, :], 1.0 / F, None, ALU.mult))
    link(v.tensor_tensor(y[:, :, :], x[:, :, :], b(st[:, 0, :]), ALU.subtract))
    link(v.tensor_tensor(sq[:, :, :], y[:, :, :], y[:, :, :], ALU.mult))
    v.tensor_reduce(st[:, 1, :], sq[:, :, :], AX.X, ALU.add).then_inc(s_h, 4)
    v.wait_ge(s_sqrt, roots)
    link(v.reciprocal(st[:, 0, :], st[:, 2, :]))
    link(v.tensor_tensor(y[:, :, :], y[:, :, :], b(st[:, 0, :]), ALU.mult))


def place(nc, t, edge, binned):
    with ExitStack() as ctx:
        sb = lambda n, s, d=F32: ctx.enter_context(nc.sbuf_tensor(n, s, d))
        pb = lambda n, s, d=F32: ctx.enter_context(nc.psum_tensor(n, s, d))
        sem = lambda n: ctx.enter_context(nc.semaphore(n))
        rec = sb("records", [P, BODY * QT, REC])
        rows = sb("rows", [P, BODY * QT], I32)
        OHs = sb("src_onehots", [P, BODY, QT, NG], BF16)
        OHd = sb("dst_onehots", [P, BODY, QT, NG], BF16)
        OHdT = sb("dst_onehots_turned", [NG, 2, QT * P])
        mask = sb("earlier", [P, QT * P])
        junk = sb("junk", [P, QT, QT * P], BF16)
        both = sb("both", [P, 2, QT, 2, NG])
        found = sb("found", [P, BODY, QT, 2])
        inside = sb("inside", [P, BODY, QT])
        rank = sb("rank", [P, BODY, QT])
        main = sb("main", [P, BODY, QT])
        over = sb("over", [P, BODY, QT])
        id64 = sb("id64", [P, P], BF16)
        zb = sb("zb", [P, NG], BF16)
        pbin = [pb(f"bins{i}", [P, QT * P]) for i in range(2)]
        ptr = [pb(f"turned{i}", [NG, 2 * QT * P], BF16) for i in range(2)]
        pg = [pb(f"gathered{i}", [P, QT, 2 * NG]) for i in range(2)]
        cnt = pb("counts", [NG, NG])
        s_c, s_oh, s_bin, s_tr, s_trc, s_g, s_cnt, s_rd, s_in, s_v, s_row, s_meta = (sem(n) for n in (
            "constants", "onehots_ready", "bins_ready", "turned_ready", "turned_copied", "gathered_ready", "group_counted",
            "counts_copied", "inside_ready", "v", "rows_ready", "meta_ready"))
        s_edge = [sem(f"edge_in{c}") for c in range(4)]
        s_scat = [sem(f"scattered{c}") for c in range(4)]
        full = [16 * QT * (b - a) for a, b in CHUNKS]
        chunk_of = [c for c, (a, b) in enumerate(CHUNKS) for _ in range(a, b)]
        s_fin = sem("fin")
        block = ctx.enter_context(nc.Block())

        @block.sync
        def _(sp):
            for c, (a, b) in enumerate(CHUNKS):
                sp.dma_start(rec[:, a * QT:b * QT, 0:FE], edge[:, a * QT:b * QT, :]).then_inc(s_edge[c], 16)
            with sp.Fori(1, BODIES) as i:
                for c, (a, b) in enumerate(CHUNKS):
                    sp.wait_ge(s_scat[c], i * full[c])
                    sp.dma_start(rec[:, a * QT:b * QT, 0:FE],
                                 edge[:, ds(i * BODY * QT + a * QT, (b - a) * QT), :]).then_inc(s_edge[c], 16)
            for c in range(4):
                sp.wait_ge(s_scat[c], BODIES * full[c])

        @block.scalar
        def _(act):
            act.wait_ge(s_tr, 1)
            act.copy(OHdT[:, 0, :], ptr[0][:, 0:QT * P]).then_inc(s_trc, 1)
            with act.Fori(0, BODIES) as i:
                for k in range(BODY):
                    g = i * BODY + k
                    if k in [a for a, _ in CHUNKS]:
                        c = chunk_of[k]
                        a, b = CHUNKS[c]
                        act.wait_ge(s_edge[c], (i + 1) * 16)
                        act.copy(rec[:, a * QT:b * QT, FE:REC], t["meta"][:, ds((i * BODY + a) * QT, (b - a) * QT), :]).then_inc(s_meta, 1)
                    act.wait_ge(s_cnt, g + 1 + 1)
                    act.wait_ge(s_g, (g if k < BODY - 1 else g + 1) + 1)
                    act.copy(t["RD"][:, (k + 1) % BODY % 2, 0:NG], cnt[:, :]).then_inc(s_rd, 1)
                    act.wait_ge(s_tr, g + 2)
                    act.wait_ge(s_g, (g if k < BODY - 1 else g + 1) + 1)
                    act.copy(OHdT[:, (k + 1) % BODY % 2, :], ptr[(k + 1) % BODY % 2][:, 0:QT * P]).then_inc(s_trc, 1)

        @block.tensor
        def _(pe):
            def turn(k):
                for q in range(QT):
                    last = pe.transpose(ptr[k % 2][:, q * P:q * P + P], OHd[:, k, q, :], t["idb"][:, :])
                last.then_inc(s_tr, 1)

            def bins(k, g):
                for q in range(QT):
                    at = g * QT + q
                    c = pbin[k % 2][:, q * P:q * P + P]
                    pe.matmul(c, col(t["hd"][:, ds(at, 1)], P), id64[:, :], start=True, stop=False)
                    last = pe.matmul(c, col(t["hs"][:, ds(at, 1)], P), t["idb"][:, :], start=False, stop=True)
                last.then_inc(s_bin, 1)

            for s in (s_in, s_trc, s_g, s_rd, s_v, s_cnt):
                pe.sem_inc(s, 1)
            pe.wait_ge(s_c, 1)
            pe.matmul(cnt[:, :], zb[:, :], zb[:, :], start=True, stop=False, skip_group_check=True)
            pe.wait_ge(s_oh, 1)
            turn(0)
            bins(0, 0)
            with pe.Fori(0, BODIES) as i:
                for k in range(BODY):
                    g = i * BODY + k
                    k1 = (k + 1) % BODY
                    pe.wait_ge(s_trc, g + 1 + 1)
                    pe.wait_ge(s_rd, g + 1)
                    pe.wait_ge(s_v, (6 * g if k == 0 else 6 * (g - 1) if k == 1 else 6 * (g - 2) + 1) + 1)
                    for q in range(QT):
                        last = pe.matmul(pg[k % 2][:, q, :], OHdT[:, k % 2, q * P:q * P + P], t["RD"][:, k % 2, :], start=True, stop=True)
                    last.then_inc(s_g, 1)
                    pe.wait_ge(s_rd, g + 1)
                    for q in range(QT):
                        last = pe.matmul(cnt[:, :], OHd[:, k, q, :], OHs[:, k, q, :], start=False, stop=False, skip_group_check=True)
                    last.then_inc(s_cnt, 1)
                    pe.wait_ge(s_oh, g + 2)
                    pe.wait_ge(s_trc, (g if k1 else g + 1) + 1)
                    apart(pe, t)
                    turn(k1)
                    pe.wait_ge(s_in, (g if k1 else g + 1) + 1)
                    bins(k1, g + 1)

        @block.gpsimd
        def _(pool):
            with pool.Fori(0, BODIES) as i:
                for k in range(BODY):
                    g = i * BODY + k
                    c = chunk_of[k]
                    if k == CHUNKS[c][0]:
                        pool.wait_ge(s_edge[c], (i + 1) * 16)
                        pool.wait_ge(s_meta, i * 4 + c + 1)
                    pool.wait_ge(s_row, g + 1)
                    apart(pool, t)
                    for q in range(QT):
                        e = k * QT + q
                        pool.indirect_dma_start(binned, bass.IndirectOffsetOnAxis(rows[:, e:e + 1], 0),
                                                rec[:, e, :], None).then_inc(s_scat[c], 16)

        @block.vector
        def _(v):
            def onehot(o, a, k, g):
                return v.tensor_tensor(o[:, k, :, :], a[:, ds(g * QT, QT)].rearrange("p (t a) -> p t a", a=1).to_broadcast([P, QT, NG]),
                                       t["rowb"][:, 0:NG].rearrange("p (a n) -> p a n", a=1).to_broadcast([P, QT, NG]), ALU.is_equal)

            def compare(k, g, q):
                n = (q + 1) * P
                return v.scalar_tensor_tensor(junk[:, q, 0:n], pbin[k % 2][:, 0:n], t["bin"][:, ds(g * QT + q, 1)], mask[:, (QT - 1 - q) * P:],
                                              ALU.is_equal, ALU.mult, accum_out=inside[:, k, q:q + 1])

            v.tensor_scalar(id64[:, :], t["idf"][:, :], float(SI), None, ALU.mult)
            v.memset(mask[:, 0:(QT - 1) * P], 1.0)
            v.tensor_scalar(mask[:, (QT - 1) * P:], t["row"][:, :], t["part"][:, 0:1], None, ALU.is_lt)
            v.memset(zb[:, :], 0.0).then_inc(s_c, 1)
            v.wait_ge(s_c, 1)
            for g in range(2):
                onehot(OHs, t["hs"], g, g)
                onehot(OHd, t["hd"], g, g).then_inc(s_oh, 1)
            v.wait_ge(s_oh, 2)
            v.wait_ge(s_bin, 1)
            for q in range(QT):
                last = compare(0, 0, q)
            last.then_inc(s_in, 1)
            with v.Fori(0, BODIES) as i:
                for k in range(BODY):
                    g = i * BODY + k
                    s, k1, k2 = k % 2, (k + 1) % BODY, (k + 2) % BODY
                    v.wait_ge(s_g, g + 1 + 1)
                    v.tensor_tensor(both[:, s, :, :, :], pg[s][:, :, :].rearrange("p t (a n) -> p t a n", a=2),
                                    OHs[:, k, :, :].rearrange("p t (a n) -> p t a n", a=1).to_broadcast([P, QT, 2, NG]), ALU.mult).then_inc(s_v, 1)
                    v.wait_ge(s_cnt, g + 1)
                    onehot(OHs, t["hs"], k2, g + 2)
                    v.wait_ge(s_v, g * 6 + 1 + 1)
                    v.tensor_reduce(found[:, k, :, :], both[:, s, :, :, :], AX.X, ALU.add).then_inc(s_v, 1)
                    onehot(OHd, t["hd"], k2, g + 2).then_inc(s_oh, 1)
                    v.wait_ge(s_v, g * 6 + 2 + 1)
                    v.wait_ge(s_in, g + 1 + 1)
                    v.tensor_tensor(rank[:, k, :], inside[:, k, :], found[:, k, :, 0], ALU.add).then_inc(s_v, 1)
                    v.wait_ge(s_bin, g + 2)
                    compare(k1, g + 1, 0)
                    v.wait_ge(s_v, g * 6 + 3 + 1)
                    v.scalar_tensor_tensor(main[:, k, :], rank[:, k, :], float(P - 1), t["base"][:, ds(g * QT, QT)], ALU.min, ALU.add).then_inc(s_v, 1)
                    v.tensor_tensor(over[:, k, :], rank[:, k, :], found[:, k, :, 1], ALU.add).then_inc(s_v, 1)
                    compare(k1, g + 1, 1)
                    v.wait_ge(s_v, g * 6 + 5 + 1)
                    v.scalar_tensor_tensor(over[:, k, :], rank[:, k, :], P - 0.5, over[:, k, :], ALU.is_gt, ALU.mult).then_inc(s_v, 1)
                    compare(k1, g + 1, 2)
                    v.wait_ge(s_v, g * 6 + 6 + 1)
                    c = chunk_of[k]
                    if k == CHUNKS[c][0]:
                        v.wait_ge(s_edge[c], (i + 1) * 16)
                    v.scalar_tensor_tensor(rows[:, k * QT:k * QT + QT], main[:, k, :], float(SI), over[:, k, :],
                                           ALU.mult, ALU.max).then_inc(s_row, 1)
                    compare(k1, g + 1, 3).then_inc(s_in, 1)


LB = -(-NT // QT)
LAST_K = LB - 1
assert NT == LAST_K * QT + 1 and LAST_K % 2 == 0
LCHUNKS = [(0, 4), (4, 8), (8, LB)]


def tiles(k):
    return range(k * QT, min(k * QT + QT, NT))


def slot(k):
    return 2 if k == LAST_K else k % 2


def before(k):
    return -1 if k == LAST_K else k - 2 if k >= 2 else k - 3


def bank_before(k):
    return k - 2 if k >= 1 else -1


CREDIT = LB


def deep(k):
    return 3 if k == LAST_K else k % 3


def before_deep(k):
    return -1 if k == LAST_K else k - 3 if k >= 3 else k - 4


WIDE = (QT, QT, 1)
DEEP = (QT, QT, QT, 1)
MW = 3 * F + 1


def layer0(nc, t, binned):
    with ExitStack() as ctx:
        sb = lambda n, s, d=F32: ctx.enter_context(nc.sbuf_tensor(n, s, d))
        pb = lambda n, s, d=F32: ctx.enter_context(nc.psum_tensor(n, s, d))
        sem = lambda n: ctx.enter_context(nc.semaphore(n))
        rec = sb("bin_row", [P, NT, REC])
        close = sb("edge_features", [P, NT, FE])
        places = [sb(f"places_spread{n}", [P, w * P], BF16) for n, w in enumerate(WIDE)]
        GT = [sb(f"gather{n}", [P, w * P], BF16) for n, w in enumerate(WIDE)]
        eT = [sb(f"edge_turned{n}", [w * FE, P]) for n, w in enumerate(WIDE)]
        S = [sb(f"scatter{n}", [P, w, P], BF16) for n, w in enumerate(DEEP)]
        msg = [sb(f"messages{n}", [P, w, MW], BF16) for n, w in enumerate(DEEP)]
        rest = [sb(f"rest_of_messages{n}", [P, w * F]) for n, w in enumerate(DEEP)]
        wd = sb("w1b_diagonal", [P, QT, F])
        pid = [pb(f"places{n}", [P, QT * P]) for n in range(2)]
        ptr = [pb(f"edges_turned{n}", [P, P]) for n in range(2)]
        pre = [pb(f"before_relu{n}", [P, QT * F]) for n in range(2)]
        acc = pb("sums", [P, MW])
        s_ld = [sem(f"row_in{c}") for c in range(3)]
        s_c, s_ids, s_pid, s_pl, s_tr, s_gt, s_et, s_pre, s_hi, s_rest, s_mid, s_msg, s_s, s_acc, s_out = (sem(n) for n in (
            "constants", "ids_ready", "places_up", "places_ready", "edges_turned", "gather_ready", "edges_ready", "sums_ready",
            "messages_hi", "rest_ready", "messages_mid", "messages_ready", "scatter_ready", "group_added", "row_kept"))
        block = ctx.enter_context(nc.Block())
        tiled = lambda a, n: a[:, 0:n * F].rearrange("p (t f) -> p t f", f=F)

        def load(sp, c, j):
            a, b = LCHUNKS[c][0] * QT, min(LCHUNKS[c][1] * QT, NT)
            sp.dma_start(rec[:, a:b, :], binned[ds(j * (P * SI), P * SI), :].rearrange("(p i) w -> p i w", i=SI)[:, a:b, :]).then_inc(s_ld[c], 16)

        @block.sync
        def _(sp):
            for c in range(3):
                load(sp, c, 0)
            with sp.Fori(1, NT) as j:
                for c, (a, b) in enumerate(LCHUNKS):
                    sp.wait_ge(s_s, (j - 1) * LB + CREDIT + b)
                    apart(sp, t)
                    sp.wait_ge(s_ids, (j - 1) * 3 + c + 1)
                    apart(sp, t)
                    load(sp, c, j)
            for c in range(2):
                sp.wait_ge(s_s, (NT - 1) * LB + CREDIT + LCHUNKS[c][1])
                sp.wait_ge(s_ids, (NT - 1) * 3 + c + 1)
                load(sp, c, NT)
            for c in range(2):
                sp.wait_ge(s_ld[c], 16 * (NT + 1))

        @block.gpsimd
        def _(pool):
            def keep_ids(c, j):
                a, b = LCHUNKS[c][0] * QT, min(LCHUNKS[c][1] * QT, NT)
                pool.wait_ge(s_ld[c], (j + 1) * 16)
                apart(pool, t)
                pool.tensor_copy(t["ids"][:, :, ds(j * NT + a, b - a)], rec[:, a:b, FE:FE + 2].rearrange("p t c -> p c t"))

            def draw_close(c, half, j):
                a, b = LCHUNKS[c][0] * QT, min(LCHUNKS[c][1] * QT, NT)
                a, b = ((a, a + 2 * QT), (a + 2 * QT, b))[half]
                pool.wait_ge(s_tr, (j - 1) * LB + CREDIT + LCHUNKS[c][1])
                apart(pool, t)
                last = pool.tensor_copy(close[:, a:b, :], rec[:, a:b, 0:FE])
                if half:
                    last.then_inc(s_ids, 1)

            pieces = {1: (2, 0), 2: (2, 1), 3: (2, 2), 5: (0, 0), 6: (0, 1), 7: (0, 2), 8: (1, 0), 9: (1, 1), 10: (1, 2)}

            def piece(c, part, j):
                if part:
                    draw_close(c, part - 1, j)
                else:
                    keep_ids(c, j)

            for c, part in ((0, 0), (0, 1), (0, 2), (1, 0), (1, 1), (1, 2)):
                piece(c, part, 0)
            with pool.Fori(0, NT) as j:
                for k in range(LB):
                    n = len(tiles(k))
                    pool.wait_ge(s_mid, j * LB + k + 1)
                    apart(pool, t)
                    pool.tensor_tensor(msg[deep(k)][:, :, 2 * F:3 * F], tiled(rest[deep(k)], n), msg[deep(k)][:, :, F:2 * F], ALU.subtract).then_inc(s_msg, 1)
                    if k in pieces:
                        piece(*pieces[k], j if k < 5 else j + 1)

        @block.vector
        def _(v):
            v.memset(wd[:, :, :], 0.0).then_inc(s_c, 1)
            for k in (LAST_K - 1, LAST_K):
                v.memset(S[deep(k)][:, :, :], 0.0)
            for m in msg:
                v.memset(m[:, :, 0:3 * F], 0.0)
                last = v.memset(m[:, :, 3 * F:MW], 1.0)
            v.wait_ge(s_c, 1)
            for q in range(QT):
                last = v.tensor_copy(wd[FE * q:FE * q + FE, q, :], t["w1b"][FE * q:FE * q + FE, :])
            last.then_inc(s_c, 1)
            v.wait_ge(s_c, 2)

            def gather(k, n):
                w = len(tiles(k)) * P
                v.wait_ge(s_pl, n + CREDIT + 1)
                v.wait_ge(s_pre, n + CREDIT - k + before(k) + 1)
                v.tensor_scalar(GT[slot(k)][:, 0:w], places[slot(k)][:, 0:w], t["part"][:, 0:1], None, ALU.is_equal).then_inc(s_gt, 1)

            def scatter(k, j):
                q = tiles(k)
                n = len(q)
                for c, (a, _) in enumerate(LCHUNKS):
                    if k == a:
                        v.wait_ge(s_ld[c], (j + 1) * 16)
                v.wait_ge(s_acc, j * LB + CREDIT + before_deep(k) + 1)
                v.tensor_tensor(S[deep(k)][:, 0:n, :], t["row"][:, :].rearrange("p (a n) -> p a n", a=1).to_broadcast([P, n, P]),
                                rec[:, q[0]:q[0] + n, FE + 1:FE + 2].to_broadcast([P, n, P]), ALU.is_equal).then_inc(s_s, 1)

            def keep_row(j):
                v.wait_ge(s_acc, (j + 1) * LB + CREDIT)
                to = t["sum"][:, ds(j + 1, 1), :].rearrange("p a f -> p (a f)")
                v.tensor_copy(to[:, F:F + 1], acc[:, 3 * F:MW])
                v.tensor_reduce(to[:, 0:F], acc[:, 0:3 * F].rearrange("p (c f) -> p f c", c=3), AX.X, ALU.add).then_inc(s_out, 1)

            gather(0, 0)
            with v.Fori(0, NT) as j:
                for k in range(LB):
                    n = len(tiles(k))
                    scatter(k, j)
                    gather((k + 1) % LB, j * LB + k + 1)
                    v.wait_ge(s_hi, j * LB + k + 1)
                    v.scalar_tensor_tensor(tiled(rest[deep(k)], n), tiled(pre[k % 2], n), 0.0, msg[deep(k)][:, :, 0:F], ALU.max, ALU.subtract).then_inc(s_rest, 1)
                    if k == 1:
                        keep_row(j - 1)
            keep_row(NT - 1)

        @block.scalar
        def _(act):
            def spread(k, n):
                w = len(tiles(k)) * P
                act.wait_ge(s_pid, n + 1)
                act.wait_ge(s_gt, n + CREDIT - k + before(k) + 1)
                act.copy(places[slot(k)][:, 0:w], pid[k % 2][:, 0:w]).then_inc(s_pl, 1)

            def edges(k, n):
                w = len(tiles(k)) * FE
                act.wait_ge(s_tr, n + CREDIT + 1)
                act.wait_ge(s_pre, n + CREDIT - k + before(k) + 1)
                act.copy(eT[slot(k)][0:w, :], ptr[k % 2][0:w, :]).then_inc(s_et, 1)

            def middle(k, j):
                n = len(tiles(k))
                act.wait_ge(s_rest, j * LB + CREDIT + k + 1)
                act.copy(msg[deep(k)][:, :, F:2 * F], tiled(rest[deep(k)], n)).then_inc(s_mid, 1)

            spread(0, 0)
            edges(0, 0)
            with act.Fori(0, NT) as j:
                for k in range(LB):
                    n = len(tiles(k))
                    k1 = (k + 1) % LB
                    spread(k1, j * LB + k + 1)
                    if k:
                        middle(k - 1, j)
                    edges(k1, j * LB + k + 1)
                    act.wait_ge(s_pre, j * LB + CREDIT + k + 1)
                    act.wait_ge(s_acc, j * LB + CREDIT + before_deep(k) + 1)
                    act.activation(msg[deep(k)][:, :, 0:F], tiled(pre[k % 2], n), ACT.Relu).then_inc(s_hi, 1)
                middle(LAST_K, j)

        @block.tensor
        def _(pe):
            def ids_up(k, n, j):
                q = tiles(k)
                for c, (a, _) in enumerate(LCHUNKS):
                    if k == a:
                        pe.wait_ge(s_ids, j * 3 + c + 1)
                pe.wait_ge(s_pl, n - k + CREDIT + bank_before(k) + 1)
                for m, i in enumerate(q):
                    last = pe.matmul(pid[k % 2][:, m * P:m * P + P], col(t["ids"][:, 0, ds(j * NT + i, 1)], P), t["idb"][:, :], start=True, stop=True)
                last.then_inc(s_pid, 1)
                pe.wait_ge(s_et, n - k + CREDIT + bank_before(k) + 1)
                pe.transpose(ptr[k % 2][0:len(q) * FE, :], close[:, q[0]:q[0] + len(q), :].rearrange("p t f -> p (t f)"), t["idf"][:, :]).then_inc(s_tr, 1)

            def sums(k, j):
                q = tiles(k)
                g = j * LB + k
                pe.wait_ge(s_et, g + CREDIT + 1)
                pe.wait_ge(s_rest, j * LB + CREDIT + bank_before(k) + 1)
                pe.matmul(pre[k % 2][:, 0:len(q) * F], eT[slot(k)][0:len(q) * FE, :], wd[0:len(q) * FE, 0:len(q), :], start=True, stop=False, skip_group_check=True)
                pe.wait_ge(s_gt, g + CREDIT + 1)
                for m, i in enumerate(q):
                    for part in range(3):
                        last = pe.matmul(pre[k % 2][:, m * F:m * F + F], GT[slot(k)][:, m * P:m * P + P], t["A3"][:, i, part, :],
                                         start=False, stop=(part == 2), skip_group_check=True)
                last.then_inc(s_pre, 1)

            def add(k, j):
                q = tiles(k)
                g = j * LB + k
                pe.wait_ge(s_msg, g + CREDIT + 1)
                pe.wait_ge(s_s, g + CREDIT + 1)
                if k == 0:
                    pe.wait_ge(s_out, j + 1)
                for m, i in enumerate(q):
                    last = pe.matmul(acc[:, :], S[deep(k)][:, m, :], msg[deep(k)][:, m, :], start=(i == 0), stop=(i == NT - 1), skip_group_check=True)
                last.then_inc(s_acc, 1)

            pe.wait_ge(s_c, 2)
            for s in (s_pl, s_tr, s_gt, s_et, s_pre, s_rest, s_msg, s_s):
                pe.sem_inc(s, CREDIT)
            pe.sem_inc(s_acc, CREDIT - 2)
            pe.matmul(acc[:, :], S[3][:, 0, :], msg[3][:, 0, :], start=True, stop=False, skip_group_check=True)
            ids_up(0, 0, 0)
            with pe.Fori(0, NT) as j:
                for k in range(LB):
                    k1 = (k + 1) % LB
                    ids_up(k1, j * LB + k + 1, j if k1 else j + 1)
                    sums(k, j)
                    add((k - 2) % LB, j if k >= 2 else j - 1)
            add(LAST_K - 1, NT - 1)
            add(LAST_K, NT - 1)

    beyond0(nc, t, binned)


def groups_beyond(eng, t):
    return eng.value_load(t["nover"][0:1, 0:1], min_val=1, max_val=ET // QT)


def beyond0(nc, t, binned):
    with ExitStack() as ctx:
        sb = lambda n, s, d=F32: ctx.enter_context(nc.sbuf_tensor(n, s, d))
        pb = lambda n, s, d=F32: ctx.enter_context(nc.psum_tensor(n, s, d))
        sem = lambda n: ctx.enter_context(nc.semaphore(n))
        rec = sb("beyond", [P, QT, REC])
        close = sb("beyond_features", [P, QT * FE])
        ids = sb("beyond_places", [P, QT], BF16)
        at = sb("beyond_tiles", [1, QT, 2], I32)
        GT = sb("beyond_gather", [P, QT * P], BF16)
        S = sb("beyond_scatter", [P, QT, P])
        eT = sb("beyond_edges_turned", [P, P])
        msg = sb("beyond_messages", [P, QT, F + 1])
        wd = sb("beyond_w1b", [P, QT, F])
        pid, ptr, pre, acc = (pb(f"beyond_{n}", [P, w]) for n, w in (("places_up", QT * P), ("edges_up", P), ("before", QT * F), ("sums", QT * (F + 1))))
        s_ld, s_c, s_close, s_ids, s_at, s_pid, s_tr, s_gt, s_et, s_pre, s_msg, s_s, s_acc, s_out = (sem(n) for n in (
            "beyond_in", "constants", "features_ready", "ids_ready", "tiles_known", "places_up", "edges_turned", "gather_ready", "edges_ready",
            "sums_ready", "messages_ready", "scatter_ready", "group_added", "group_kept"))
        block = ctx.enter_context(nc.Block())

        @block.sync
        def _(sp):
            with sp.Fori(0, groups_beyond(sp, t)) as o:
                sp.wait_ge(s_out, o * QT + 1)
                apart(sp, t)
                sp.dma_start(rec[:, :, :], binned[ds(o * (QT * P) + MAIN, QT * P), :].rearrange("(q p) w -> p q w", p=P)).then_inc(s_ld, 16)

        @block.gpsimd
        def _(pool):
            with pool.Fori(0, groups_beyond(pool, t)) as o:
                pool.wait_ge(s_ld, (o + 1) * 16)
                apart(pool, t)
                pool.tensor_copy(close[:, :].rearrange("p (t f) -> p t f", f=FE), rec[:, :, 0:FE]).then_inc(s_close, 1)

        @block.vector
        def _(v):
            v.memset(wd[:, :, :], 0.0).then_inc(s_c, 1)
            v.memset(msg[:, :, F:F + 1], 1.0)
            v.wait_ge(s_c, 1)
            for q in range(QT):
                last = v.tensor_copy(wd[FE * q:FE * q + FE, q, :], t["w1b"][FE * q:FE * q + FE, :])
            last.then_inc(s_c, 1)
            with v.Fori(0, groups_beyond(v, t)) as o:
                v.wait_ge(s_ld, (o + 1) * 16)
                v.tensor_copy(ids[:, :], rec[:, :, FE]).then_inc(s_ids, 1)
                v.tensor_scalar(at[:, :, :], rec[0:1, :, FE + 2:FE + 4], 0.0, None, ALU.max).then_inc(s_at, 1)
                v.tensor_tensor(S[:, :, :], t["row"][:, :].rearrange("p (a n) -> p a n", a=1).to_broadcast([P, QT, P]),
                                rec[:, :, FE + 1:FE + 2].to_broadcast([P, QT, P]), ALU.is_equal).then_inc(s_s, 1)
                v.wait_ge(s_pid, o + 1)
                v.tensor_scalar(GT[:, :], pid[:, :], t["part"][:, 0:1], None, ALU.is_equal).then_inc(s_gt, 1)
                v.wait_ge(s_at, o + 1)
                apart(v, t)
                to = [v.value_load(at[0:1, q, 1:2], min_val=0, max_val=NT - 1) for q in range(QT)]
                v.wait_ge(s_acc, o + 1)
                for q in range(QT):
                    row = t["sum"][:, ds(to[q] + 1, 1), :].rearrange("p a f -> p (a f)")
                    v.wait_ge(s_out, o * QT + q + 1)
                    v.tensor_tensor(row, row, acc[:, q * (F + 1):(q + 1) * (F + 1)], ALU.add).then_inc(s_out, 1)

        @block.scalar
        def _(act):
            with act.Fori(0, groups_beyond(act, t)) as o:
                act.wait_ge(s_tr, o + 1)
                act.copy(eT[:, :], ptr[:, :]).then_inc(s_et, 1)
                act.wait_ge(s_pre, o + 1)
                act.activation(msg[:, :, 0:F], pre[:, :].rearrange("p (t f) -> p t f", f=F), ACT.Relu).then_inc(s_msg, 1)

        @block.tensor
        def _(pe):
            pe.wait_ge(s_c, 2)
            pe.sem_inc(s_out, 1)
            with pe.Fori(0, groups_beyond(pe, t)) as o:
                pe.wait_ge(s_ids, o + 1)
                for q in range(QT):
                    last = pe.matmul(pid[:, q * P:q * P + P], col(ids[:, q:q + 1], P), t["idb"][:, :], start=True, stop=True)
                last.then_inc(s_pid, 1)
                pe.wait_ge(s_close, o + 1)
                pe.transpose(ptr[:, :], close[:, :], t["idf"][:, :]).then_inc(s_tr, 1)
                pe.wait_ge(s_at, o + 1)
                apart(pe, t)
                of = [pe.value_load(at[0:1, q, 0:1], min_val=0, max_val=NT - 1) for q in range(QT)]
                pe.wait_ge(s_et, o + 1)
                pe.matmul(pre[:, :], eT[:, :], wd[:, :, :], start=True, stop=False, skip_group_check=True)
                pe.wait_ge(s_gt, o + 1)
                for q in range(QT):
                    for part in range(3):
                        last = pe.matmul(pre[:, q * F:q * F + F], GT[:, q * P:q * P + P], t["A3"][:, ds(of[q], 1), part, :].rearrange("p a f -> p (a f)"),
                                         start=False, stop=(part == 2), skip_group_check=True)
                last.then_inc(s_pre, 1)
                pe.wait_ge(s_msg, o + 1)
                pe.wait_ge(s_s, o + 1)
                for q in range(QT):
                    last = pe.matmul(acc[:, q * (F + 1):(q + 1) * (F + 1)], S[:, q, :], msg[:, q, :], start=True, stop=True)
                last.then_inc(s_acc, 1)


def nodes(nc, t):
    with ExitStack() as ctx:
        sb = lambda n, s, d=F32: ctx.enter_context(nc.sbuf_tensor(n, s, d))
        pb = lambda n, s, d=F32: ctx.enter_context(nc.psum_tensor(n, s, d))
        sem = lambda n: ctx.enter_context(nc.semaphore(n))
        sq = sb("sq2", [P, NT, F])
        y = sb("y", [P, NT, F])
        st = sb("st2", [P, 3, NT])
        deg = sb("degree", [P, NT])
        mT = sb("sums_turned", [F + 1, 2, QT * P])
        hT = sb("h_turned2", [F, 2, QT * P])
        rest = sb("rest2", [P, 2, 2, 3 * F])
        ptr = [pb(f"turned2_{i}", [P, QT * P]) for i in range(2)]
        pm = [pb(f"times_w2_{i}", [P, QT * F]) for i in range(2)]
        pq = [pb(f"qkv_sum{i}", [P, 2 * 3 * F]) for i in range(2)]
        s_v, s_tr, s_mT, s_pm, s_y, s_h, s_sqrt, s_tr2, s_hT, s_pq, s_hi, s_rest, s_mid, s_q = (sem(n) for n in (
            "v", "sums_turned", "sums_copied", "times_w2", "y_ready", "h_ready", "rooted", "h_turned", "h_copied", "qkv_up", "qkv_hi",
            "qkv_rest", "qkv_mid", "qkv_done"))
        block = ctx.enter_context(nc.Block())
        GB = -(-NT // QT)
        GQ = -(-NT // 2)

        @block.tensor
        def _(pe):
            for g in range(GB + 1):
                if g < GB:
                    m = min(QT, NT - QT * g)
                    if g >= 2:
                        pe.wait_ge(s_mT, g - 1)
                    for k in range(m):
                        last = pe.transpose(ptr[g % 2][0:F + 1, k * P:k * P + P], t["sum"][:, QT * g + k + 1, :], t["idf"][:, :])
                    last.then_inc(s_tr, 1)
                if g >= 1:
                    q = g - 1
                    m = min(QT, NT - QT * q)
                    pe.wait_ge(s_mT, q + 1)
                    if q >= 2:
                        pe.wait_ge(s_y, q - 1)
                    for k in range(m):
                        last = pe.matmul(pm[q % 2][:, k * F:k * F + F], mT[:, q % 2, k * P:k * P + P], t["w2"][:, :], start=True, stop=True)
                    last.then_inc(s_pm, 1)
            pe.wait_ge(s_h, 9)
            for g in range(GQ + 1):
                if g < GQ:
                    m = min(2, NT - 2 * g)
                    if g >= 2:
                        pe.wait_ge(s_hT, g - 1)
                    for k in range(m):
                        last = pe.transpose(ptr[g % 2][0:F, k * P:k * P + P], t["h"][:, 2 * g + k, :], t["idf"][:, :])
                    last.then_inc(s_tr2, 1)
                if g >= 1:
                    q = g - 1
                    m = min(2, NT - 2 * q)
                    pe.wait_ge(s_hT, q + 1)
                    if q >= 2:
                        pe.wait_ge(s_rest, q - 1)
                    for k in range(m):
                        last = pe.matmul(pq[q % 2][:, k * 3 * F:(k + 1) * 3 * F], hT[:, q % 2, k * P:k * P + P], t["wqkv"][:, :], start=True, stop=True)
                    last.then_inc(s_pq, 1)

        @block.scalar
        def _(act):
            for g in range(GB):
                n = min(QT, NT - QT * g)
                act.wait_ge(s_tr, g + 1)
                if g >= 2:
                    act.wait_ge(s_pm, g - 1)
                act.copy(mT[:, g % 2, 0:n * P], ptr[g % 2][0:F + 1, 0:n * P]).then_inc(s_mT, 1)
            for r in range(2):
                act.wait_ge(s_h, 4 * (r + 1))
                act.activation(st[:, 2, :], st[:, 1, :], ACT.Sqrt, bias=t["eps"][:, 0:1], scale=1.0 / F).then_inc(s_sqrt, 1)
            for g in range(GQ):
                n = min(2, NT - 2 * g)
                at = slice(2 * g, 2 * g + n)
                act.wait_ge(s_tr2, g + 1)
                if g >= 2:
                    act.wait_ge(s_pq, g - 1)
                act.copy(hT[:, g % 2, 0:n * P], ptr[g % 2][0:F, 0:n * P]).then_inc(s_hT, 1)
                act.wait_ge(s_pq, g + 1)
                act.copy(t["qkv"][:, at, 0, :], pq[g % 2][:, 0:n * 3 * F].rearrange("p (t f) -> p t f", t=n)).then_inc(s_hi, 1)
                act.wait_ge(s_rest, g + 1)
                act.copy(t["qkv"][:, at, 1, :], rest[:, g % 2, 0:n, :]).then_inc(s_mid, 1)

        @block.gpsimd
        def _(pool):
            pool.memset(t["qkv"][:, NT, :, :], 0.0)

        @block.vector
        def _(v):
            n = [0]

            def link(ins):
                n[0] += 1
                ins.then_inc(s_v, 1)
                v.wait_ge(s_v, n[0])

            b = lambda a: a.rearrange("p (t a) -> p t a", a=1).to_broadcast([P, NT, F])
            w = lambda a: a.rearrange("p (a f) -> p a f", a=1).to_broadcast([P, NT, F])
            link(v.tensor_scalar(deg[:, :], t["sum"][:, 1:NT + 1, F], 1.0, None, ALU.max))
            link(v.reciprocal(deg[:, :], deg[:, :]))
            for g in range(GB):
                m = min(QT, NT - QT * g)
                at = slice(QT * g, QT * g + m)
                v.wait_ge(s_pm, g + 1)
                v.tensor_tensor(y[:, at, :], pm[g % 2][:, 0:m * F].rearrange("p (t f) -> p t f", f=F),
                                deg[:, at].rearrange("p (t a) -> p t a", a=1).to_broadcast([P, m, F]), ALU.mult).then_inc(s_y, 1)
            v.wait_ge(s_y, GB)
            link(v.tensor_tensor(y[:, :, :], y[:, :, :], t["h"][:, :, :], ALU.add))
            layer_norm(v, link, y, y, sq, st, s_h, s_sqrt, 1)
            link(v.tensor_tensor(y[:, :, :], y[:, :, :], w(t["gb"][:, 0, :]), ALU.mult))
            link(v.tensor_tensor(y[:, :, :], y[:, :, :], w(t["gb"][:, 1, :]), ALU.add))
            link(v.tensor_tensor(t["x"][:, :, :], t["x"][:, :, :], y[:, :, :], ALU.add))
            layer_norm(v, link, t["x"], t["h"], sq, st, s_h, s_sqrt, 2)
            v.tensor_scalar(t["h"][:, :, :], t["h"][:, :, :], 0.0, None, ALU.max).then_inc(s_h, 1)
            for g in range(GQ):
                m = min(2, NT - 2 * g)
                at = slice(2 * g, 2 * g + m)
                v.wait_ge(s_hi, g + 1)
                v.tensor_tensor(rest[:, g % 2, 0:m, :], pq[g % 2][:, 0:m * 3 * F].rearrange("p (t f) -> p t f", t=m),
                                t["qkv"][:, at, 0, :], ALU.subtract).then_inc(s_rest, 1)
                v.wait_ge(s_mid, g + 1)
                v.tensor_tensor(t["qkv"][:, at, 2, :], rest[:, g % 2, 0:m, :], t["qkv"][:, at, 1, :], ALU.subtract).then_inc(s_q, 1)


W = F + HEADS


def layer1(nc, t, binned, out):
    with ExitStack() as ctx:
        sb = lambda n, s, d=F32: ctx.enter_context(nc.sbuf_tensor(n, s, d))
        pb = lambda n, s, d=F32: ctx.enter_context(nc.psum_tensor(n, s, d))
        sem = lambda n: ctx.enter_context(nc.semaphore(n))
        wide = (QT, QT, 1)
        GTs = [sb(f"gather_src{n}", [P, w * P], BF16) for n, w in enumerate(wide)]
        GTd = [sb(f"gather_dst{n}", [P, w * P], BF16) for n, w in enumerate(wide)]
        away = [sb(f"away{n}", [P, w * P]) for n, w in enumerate(wide)]
        S = [sb(f"scatter1_{n}", [P, w, P]) for n, w in enumerate(wide)]
        qs = [sb(f"queries{n}", [P, w, F]) for n, w in enumerate(wide)]
        prod = [sb(f"products{n}", [P, w, F]) for n, w in enumerate(wide)]
        att = [sb(f"scores{n}", [P, w, HEADS]) for n, w in enumerate(wide)]
        msg = [sb(f"messages1_{n}", [P, w, W]) for n, w in enumerate(wide)]
        idf = sb("src_places", [P, NT * NT + 1])
        minus = sb("minus_part", [P, 1])
        row = sb("row_places", [P, NT])
        pis, pid = pb("src_places_up", [P, QT * P]), pb("dst_places_up", [P, QT * P])
        pq = [pb(f"q_up{n}", [P, QT * F]) for n in range(2)]
        pkv = [pb(f"kv_up{n}", [P, w * 2 * F]) for n, w in enumerate(wide)]
        acc = pb("sums1", [P, W])
        names = ("constants", "src_up", "dst_up", "src_gather", "away_ready", "dst_gather", "scatter_part", "scatter_ready", "q_up", "kv_up",
                 "q_ready", "products_ready", "scores_ready", "clipped", "exp_ready", "messages_ready", "group_added", "row_kept")
        s_c, s_is, s_id, s_gs, s_aw, s_gd, s_sp, s_s, s_pq, s_kv, s_q, s_pr, s_sc, s_cl, s_ex, s_msg, s_acc, s_out = (sem(n) for n in names)
        block = ctx.enter_context(nc.Block())
        POOLED = 3

        @block.gpsimd
        def _(pool):
            pool.wait_ge(s_c, 1)
            with pool.Fori(0, NT) as i:
                pool.wait_ge(s_sp, i * (LAST_K + 1) + 1)
                apart(pool, t)
                pool.tensor_copy(row[:, :], idf[:, 0:NT * NT].rearrange("p (j i) -> p i j", i=NT)[:, ds(i, 1), :].rearrange("p a j -> p (a j)")).then_inc(s_sp, 1)
                pool.wait_ge(s_sp, i * (LAST_K + 1) + 2)
                apart(pool, t)
                for k in range(LAST_K):
                    q = tiles(k)
                    pool.wait_ge(s_acc, i * LB + CREDIT + before(k) + 1)
                    apart(pool, t)
                    for m, j in enumerate(q[:POOLED]):
                        last = pool.tensor_scalar(S[slot(k)][:, m, :], t["row"][:, :], row[:, j:j + 1], None, ALU.is_equal)
                    last.then_inc(s_sp, 1)

        @block.vector
        def _(v):
            v.tensor_scalar(minus[:, :], t["part"][:, :], -1.0, None, ALU.mult)
            v.tensor_copy(idf[:, :], t["ids"][:, 0, 0:NT * NT + 1]).then_inc(s_c, 1)
            v.wait_ge(s_c, 1)

            def gather(k, n):
                w = len(tiles(k)) * P
                v.wait_ge(s_is, n + 1)
                v.wait_ge(s_kv, n + CREDIT - k + before(k) + 1)
                v.tensor_scalar(GTs[slot(k)][:, 0:w], pis[:, 0:w], t["part"][:, 0:1], None, ALU.is_equal).then_inc(s_gs, 1)

            def scatter(k, i):
                v.wait_ge(s_acc, i * LB + CREDIT + before(k) + 1)
                m = min(POOLED, len(tiles(k)) - 1)
                v.tensor_scalar(S[slot(k)][:, m, :], t["row"][:, :], idf[:, ds(i + tiles(k)[-1] * NT, 1)], None, ALU.is_equal).then_inc(s_s, 1)

            gather(0, 0)
            gather(1, 1)
            with v.Fori(0, NT) as i:
                for k in range(LB):
                    n = len(tiles(k))
                    g = i * LB + k
                    o = slot(k)
                    kv = pkv[o][:, :].rearrange("p (t f) -> p t f", f=2 * F)
                    heads = lambda a: a.rearrange("p t (h d) -> p t h d", h=HEADS)
                    v.wait_ge(s_q, g + CREDIT + 1)
                    v.wait_ge(s_kv, g + CREDIT + 1)
                    v.tensor_tensor(prod[o][:, :, :], qs[o][:, :, :], kv[:, :, 0:F], ALU.mult).then_inc(s_pr, 1)
                    gather((k + 2) % LB, g + 2)
                    v.wait_ge(s_pr, g + 1)
                    v.tensor_reduce(att[o][:, :, :], heads(prod[o][:, :, :]), AX.X, ALU.add).then_inc(s_sc, 1)
                    scatter(k, i)
                    v.wait_ge(s_sc, g + 1)
                    v.tensor_scalar(att[o][:, :, :], att[o][:, :, :], 10.0, -10.0, ALU.min, ALU.max).then_inc(s_cl, 1)
                    v.wait_ge(s_ex, g + 1)
                    v.tensor_tensor(heads(msg[o][:, :, 0:F]), heads(kv[:, :, F:2 * F]),
                                    msg[o][:, :, F:W].rearrange("p t (h a) -> p t h a", a=1).to_broadcast([P, n, HEADS, HD]), ALU.mult).then_inc(s_msg, 1)
                v.wait_ge(s_acc, (i + 1) * LB + CREDIT)
                v.tensor_copy(t["out"][:, ds(i, 1), :].rearrange("p a f -> p (a f)"), acc[:, :]).then_inc(s_out, 1)

        @block.scalar
        def _(act):
            def gather(k, n):
                w = len(tiles(k)) * P
                act.wait_ge(s_id, n + 1)
                act.activation(away[slot(k)][:, 0:w], pid[:, 0:w], ACT.Abs, bias=minus[:, 0:1]).then_inc(s_aw, 1)
                act.wait_ge(s_kv, n + CREDIT - k + before(k) + 1)
                act.wait_ge(s_aw, n + 1)
                act.activation(GTd[slot(k)][:, 0:w], away[slot(k)][:, 0:w], ACT.Relu, bias=1.0, scale=-1.0).then_inc(s_gd, 1)

            act.wait_ge(s_c, 1)
            gather(0, 0)
            gather(1, 1)
            with act.Fori(0, NT) as i:
                for k in range(LB):
                    n = len(tiles(k))
                    o = slot(k)
                    g = i * LB + k
                    act.wait_ge(s_pq, g + 1)
                    act.wait_ge(s_msg, i * LB + CREDIT + before(k) + 1)
                    act.copy(qs[o][:, :, :], pq[k % 2][:, 0:n * F].rearrange("p (t f) -> p t f", f=F)).then_inc(s_q, 1)
                    gather((k + 2) % LB, g + 2)
                    act.wait_ge(s_cl, g + 1)
                    act.wait_ge(s_acc, i * LB + CREDIT + before(k) + 1)
                    act.activation(msg[o][:, :, F:W], att[o][:, :, :], ACT.Exp).then_inc(s_ex, 1)

        @block.tensor
        def _(pe):
            def ids_up(k, n, i):
                w = len(tiles(k)) * P
                for side, bank, made, up in ((0, pis, s_gs, s_is), (1, pid, s_aw, s_id)):
                    if not isinstance(n, int) or n:
                        pe.wait_ge(made, n)
                    for m, j in enumerate(tiles(k)):
                        last = pe.matmul(bank[:, m * P:m * P + P], col(t["ids"][:, side, ds(i + j * NT, 1)], P), t["idb"][:, :], start=True, stop=True)
                    last.then_inc(up, 1)

            def gathered(k, g, i):
                n = len(tiles(k))
                pe.wait_ge(s_gs, g + 1)
                pe.wait_ge(s_q, g - k + CREDIT + bank_before(k) + 1)
                for m in range(n):
                    for part in range(3):
                        last = pe.matmul(pq[k % 2][:, m * F:m * F + F], GTs[slot(k)][:, m * P:m * P + P],
                                         t["qkv"][:, ds(i, 1), part, 0:F].rearrange("p a f -> p (a f)"), start=(part == 0), stop=(part == 2))
                last.then_inc(s_pq, 1)
                pe.wait_ge(s_gd, g + 1)
                pe.wait_ge(s_msg, g - k + CREDIT + before(k) + 1)
                for m, j in enumerate(tiles(k)):
                    for part in range(3):
                        last = pe.matmul(pkv[slot(k)][:, m * 2 * F:(m + 1) * 2 * F], GTd[slot(k)][:, m * P:m * P + P], t["qkv"][:, j, part, F:3 * F],
                                         start=(part == 0), stop=(part == 2))
                last.then_inc(s_kv, 1)

            def add(k, i):
                g = i * LB + k
                pe.wait_ge(s_msg, g + CREDIT + 1)
                pe.wait_ge(s_s, g + 1)
                if k != LAST_K:
                    pe.wait_ge(s_sp, i * (LAST_K + 1) + k + 3)
                if k == 0:
                    pe.wait_ge(s_out, i + 1)
                for m, j in enumerate(tiles(k)):
                    last = pe.matmul(acc[:, :], S[slot(k)][:, m, :], msg[slot(k)][:, m, :], start=(j == 0), stop=(j == NT - 1), skip_group_check=True)
                last.then_inc(s_acc, 1)

            for s in (s_kv, s_q, s_msg, s_acc):
                pe.sem_inc(s, CREDIT)
            pe.sem_inc(s_out, 1)
            pe.sem_inc(s_sp, 1)
            pe.wait_ge(s_c, 1)
            ids_up(0, 0, 0)
            ids_up(1, 1, 0)
            gathered(0, 0, 0)
            with pe.Fori(0, NT) as i:
                for k in range(LB):
                    k1, k2 = (k + 1) % LB, (k + 2) % LB
                    g = i * LB + k
                    ids_up(k2, g + 2, i if k2 == k + 2 else i + 1)
                    gathered(k1, g + 1, i if k1 else i + 1)
                    if k:
                        add(k - 1, i)
                add(LAST_K, i)

    beyond1(nc, t, binned)
    finish(nc, t, out)


def beyond1(nc, t, binned):
    with ExitStack() as ctx:
        sb = lambda n, s, d=F32: ctx.enter_context(nc.sbuf_tensor(n, s, d))
        pb = lambda n, s, d=F32: ctx.enter_context(nc.psum_tensor(n, s, d))
        sem = lambda n: ctx.enter_context(nc.semaphore(n))
        rec = sb("beyond_places1", [P, QT, 4])
        ids = sb("beyond_ids1", [P, 2, QT], BF16)
        at = sb("beyond_tiles1", [1, QT, 2], I32)
        GT = sb("beyond_gather1", [P, 2, QT * P], BF16)
        S = sb("beyond_scatter1", [P, QT, P])
        qs = sb("beyond_queries", [P, QT, F])
        prod = sb("beyond_products", [P, QT, F])
        att = sb("beyond_scores", [P, QT, HEADS])
        msg = sb("beyond_messages1", [P, QT, W])
        pis, pid, pq, pkv, acc = (pb(f"beyond1_{n}", [P, w]) for n, w in (
            ("src_up", QT * P), ("dst_up", QT * P), ("q_up", QT * F), ("kv_up", QT * 2 * F), ("sums", QT * W)))
        names = ("beyond_in1", "ids_ready1", "tiles_known1", "places_up1", "gathers_ready", "scatter_ready1", "q_up1", "kv_up1", "q_ready1",
                 "products_ready1", "scores_ready1", "clipped1", "exp_ready1", "messages_ready1", "group_added1", "group_kept1")
        s_ld, s_ids, s_at, s_up, s_gt, s_s, s_pq, s_kv, s_q, s_pr, s_sc, s_cl, s_ex, s_msg, s_acc, s_out = (sem(n) for n in names)
        block = ctx.enter_context(nc.Block())
        heads = lambda a: a.rearrange("p t (h d) -> p t h d", h=HEADS)
        kv = pkv[:, :].rearrange("p (t f) -> p t f", f=2 * F)

        @block.sync
        def _(sp):
            with sp.Fori(0, groups_beyond(sp, t)) as o:
                sp.wait_ge(s_out, o * QT + 1)
                apart(sp, t)
                sp.dma_start(rec[:, :, :], binned[ds(o * (QT * P) + MAIN, QT * P), FE:REC].rearrange("(q p) w -> p q w", p=P)).then_inc(s_ld, 16)

        @block.vector
        def _(v):
            with v.Fori(0, groups_beyond(v, t)) as o:
                v.wait_ge(s_ld, (o + 1) * 16)
                v.tensor_copy(ids[:, :, :], rec[:, :, 0:2].rearrange("p t c -> p c t")).then_inc(s_ids, 1)
                v.tensor_scalar(at[:, :, :], rec[0:1, :, 2:4], 0.0, None, ALU.max).then_inc(s_at, 1)
                v.tensor_tensor(S[:, :, :], t["row"][:, :].rearrange("p (a n) -> p a n", a=1).to_broadcast([P, QT, P]),
                                rec[:, :, 0:1].to_broadcast([P, QT, P]), ALU.is_equal).then_inc(s_s, 1)
                v.wait_ge(s_up, o + 1)
                v.tensor_scalar(GT[:, 0, :], pis[:, :], t["part"][:, 0:1], None, ALU.is_equal)
                v.tensor_scalar(GT[:, 1, :], pid[:, :], t["part"][:, 0:1], None, ALU.is_equal).then_inc(s_gt, 1)
                v.wait_ge(s_at, o + 1)
                apart(v, t)
                to = [v.value_load(at[0:1, q, 0:1], min_val=0, max_val=NT - 1) for q in range(QT)]
                v.wait_ge(s_q, o + 1)
                v.wait_ge(s_kv, o + 1)
                v.tensor_tensor(prod[:, :, :], qs[:, :, :], kv[:, :, 0:F], ALU.mult).then_inc(s_pr, 1)
                v.wait_ge(s_pr, o + 1)
                v.tensor_reduce(att[:, :, :], heads(prod[:, :, :]), AX.X, ALU.add).then_inc(s_sc, 1)
                v.wait_ge(s_sc, o + 1)
                v.tensor_scalar(att[:, :, :], att[:, :, :], 10.0, -10.0, ALU.min, ALU.max).then_inc(s_cl, 1)
                v.wait_ge(s_ex, o + 1)
                v.tensor_tensor(heads(msg[:, :, 0:F]), heads(kv[:, :, F:2 * F]),
                                msg[:, :, F:W].rearrange("p t (h a) -> p t h a", a=1).to_broadcast([P, QT, HEADS, HD]), ALU.mult).then_inc(s_msg, 1)
                v.wait_ge(s_acc, o + 1)
                for q in range(QT):
                    row = t["out"][:, ds(to[q], 1), :].rearrange("p a f -> p (a f)")
                    v.wait_ge(s_out, o * QT + q + 1)
                    v.tensor_tensor(row, row, acc[:, q * W:(q + 1) * W], ALU.add).then_inc(s_out, 1)

        @block.scalar
        def _(act):
            with act.Fori(0, groups_beyond(act, t)) as o:
                act.wait_ge(s_pq, o + 1)
                act.copy(qs[:, :, :], pq[:, :].rearrange("p (t f) -> p t f", f=F)).then_inc(s_q, 1)
                act.wait_ge(s_cl, o + 1)
                act.activation(msg[:, :, F:W], att[:, :, :], ACT.Exp).then_inc(s_ex, 1)

        @block.tensor
        def _(pe):
            pe.sem_inc(s_out, 1)
            with pe.Fori(0, groups_beyond(pe, t)) as o:
                pe.wait_ge(s_ids, o + 1)
                for side, bank in ((0, pis), (1, pid)):
                    for q in range(QT):
                        last = pe.matmul(bank[:, q * P:q * P + P], col(ids[:, side, q:q + 1], P), t["idb"][:, :], start=True, stop=True)
                last.then_inc(s_up, 1)
                pe.wait_ge(s_at, o + 1)
                apart(pe, t)
                tile = [[pe.value_load(at[0:1, q, s:s + 1], min_val=0, max_val=NT - 1) for q in range(QT)] for s in range(2)]
                pe.wait_ge(s_gt, o + 1)
                for side, bank, a, b, up in ((0, pq, 0, F, s_pq), (1, pkv, F, 3 * F, s_kv)):
                    for q in range(QT):
                        for part in range(3):
                            last = pe.matmul(bank[:, q * (b - a):(q + 1) * (b - a)], GT[:, side, q * P:q * P + P],
                                             t["qkv"][:, ds(tile[side][q], 1), part, a:b].rearrange("p a f -> p (a f)"), start=(part == 0), stop=(part == 2))
                    last.then_inc(up, 1)
                pe.wait_ge(s_msg, o + 1)
                pe.wait_ge(s_s, o + 1)
                for q in range(QT):
                    last = pe.matmul(acc[:, q * W:(q + 1) * W], S[:, q, :], msg[:, q, :], start=True, stop=True)
                last.then_inc(s_acc, 1)


def finish(nc, t, out):
    with ExitStack() as ctx:
        den = ctx.enter_context(nc.sbuf_tensor("denominators", [P, NT, HEADS], F32))
        s_v, s_o = (ctx.enter_context(nc.semaphore(n)) for n in ("v_out", "written"))
        block = ctx.enter_context(nc.Block())

        @block.vector
        def _(v):
            n = [0]

            def link(ins):
                n[0] += 1
                ins.then_inc(s_v, 1)
                v.wait_ge(s_v, n[0])

            link(v.tensor_scalar(den[:, :, :], t["out"][:, :, F:W], 1e-8, None, ALU.add))
            link(v.reciprocal(den[:, :, :], den[:, :, :]))
            for h in range(HEADS):
                a = t["out"][:, :, h * HD:(h + 1) * HD]
                last = v.tensor_tensor(a, a, den[:, :, h:h + 1].to_broadcast([P, NT, HD]), ALU.mult)
            link(last)
            v.tensor_tensor(t["x"][:, :, :], t["x"][:, :, :], t["out"][:, :, 0:F], ALU.add).then_inc(s_v, 1)

        @block.sync
        def _(sp):
            sp.wait_ge(s_v, 4)
            sp.dma_start(out[0:(NT - 1) * P, :].rearrange("(t p) f -> p t f", p=P), t["x"][:, 0:NT - 1, :]).then_inc(s_o, 16)
            sp.dma_start(out[(NT - 1) * P:N_NODES, :], t["x"][0:LAST, NT - 1, :]).then_inc(s_o, 16)
            sp.wait_ge(s_o, 32)


def kernel(x, src, dst, edge_attr_32, L0_gnn_W1, L0_gnn_b1, L0_gnn_W2, L0_gnn_b2, L0_gnn_gamma, L0_gnn_beta,
           L1_gnn_qTrans, L1_gnn_kTrans, L1_gnn_vTrans):
    import numpy as np
    import concourse.bacc as bacc
    from concourse.bass_utils import run_bass_kernel_spmd

    pad = ET * P - N_EDGES
    across = lambda a: np.ascontiguousarray(a.reshape(ET, P, *a.shape[1:]).swapaxes(0, 1))

    def node_ids(a):
        a = np.asarray(a)
        return across(np.concatenate([a, np.full(pad, NT * P, a.dtype)]))

    arrays = {
        "x_in": np.asarray(x), "src": node_ids(src), "dst": node_ids(dst),
        "edge": across(np.concatenate([np.asarray(edge_attr_32), np.zeros((pad, FE), np.float32)])),
        "w1": np.asarray(L0_gnn_W1), "b1": np.asarray(L0_gnn_b1), "w2": np.asarray(L0_gnn_W2), "b2": np.asarray(L0_gnn_b2),
        "gamma": np.asarray(L0_gnn_gamma), "beta": np.asarray(L0_gnn_beta),
        "wq": np.asarray(L1_gnn_qTrans), "wk": np.asarray(L1_gnn_kTrans), "wv": np.asarray(L1_gnn_vTrans),
    }
    nc = bacc.Bacc("TRN2", target_bir_lowering=False, num_devices=1)
    args = [nc.dram_tensor(n, a.shape, mybir.dt.from_np(a.dtype), kind="ExternalInput").ap() for n, a in arrays.items()]
    out = nc.dram_tensor("out", (N_NODES, F), F32, kind="ExternalOutput").ap()
    gnn(nc, *args, out)
    r = run_bass_kernel_spmd(nc, [arrays], core_ids=[0])
    return r.results[0]["out"]
```

```python
from contextlib import ExitStack

import concourse.bass as bass
from concourse import mybir

F32 = mybir.dt.float32
BF16 = mybir.dt.bfloat16
I32 = mybir.dt.int32
ALU = mybir.AluOpType
ACT = mybir.ActivationFunctionType
AX = mybir.AxisListType
ds = bass.ds

P = 128
N_NODES = 6250
N_EDGES = 206250
F = 64
FE = 32
HEADS = 4
HD = F // HEADS
NT = -(-N_NODES // P)
LAST = N_NODES - (NT - 1) * P
NG = NT + 1
SI = 64

QT = 4
BODY = 13
ET = -(-N_EDGES // P)
GROUPS = ET // QT
BODIES = GROUPS // BODY
assert GROUPS * QT == ET and BODIES * BODY == GROUPS
EP = ET + 2 * QT
CHUNKS = [(0, 3), (3, 6), (6, 9), (9, 13)]

REC = FE + 4
MAIN = NG * P * SI
QB = 2
STEP = QB * QT
EO = -(-ET // STEP) * STEP
ROWS = MAIN + EO * P
LN_EPS = 1e-5
NA = -(-NT // QT)
HB = 31
HU = 4
assert NA * HU * HB == ET


def col(ap, n):
    return ap.to_broadcast([P, n])


def apart(eng, t):
    eng.sem_inc(t["passed"], 1)


def gnn(nc, x, src, dst, edge, w1, b1, w2, b2, gamma, beta, wq, wk, wv, out, stop=99):
    binned = nc.dram_tensor("binned", [ROWS, REC], F32).ap()
    with ExitStack() as keep:
        def sb(name, shape, dt=F32, at=keep):
            return at.enter_context(nc.sbuf_tensor(name, shape, dt))

        t = {"passed": keep.enter_context(nc.semaphore("passed"))}
        t["x"] = sb("x_nodes", [P, NT, F])
        t["h"] = sb("h_nodes", [P, NA * QT, F])
        t["row"] = sb("iota_row", [P, P])
        t["rowb"] = sb("iota_rowb", [P, P], BF16)
        t["part"] = sb("iota_part", [P, 1])
        t["idf"] = sb("identity_f32", [P, P])
        t["idb"] = sb("identity_bf16", [P, P], BF16)
        t["w1a"] = sb("w1a_b1", [F + 1, F])
        t["w1b"] = sb("w1b", [P, F])
        t["w2"] = sb("w2_b2", [F + 1, F])
        t["wqkv"] = sb("wqkv", [F, 3 * F])
        t["gb"] = sb("gamma_beta", [P, 2, F])
        t["eps"] = sb("eps", [P, 1])
        t["nover"] = sb("steps_over", [1, 1], I32)
        t["A3"] = sb("a_parts", [P, NA * QT, 3, F], BF16)
        with ExitStack() as ctx:
            t["hs"] = sb("src_tile", [P, EP], BF16, ctx)
            t["hd"] = sb("dst_tile", [P, EP], BF16, ctx)
            t["bin"] = sb("bin", [P, EP], F32, ctx)
            t["base"] = sb("bin_base", [P, ET], F32, ctx)
            t["meta"] = sb("meta", [P, ET, 4], F32, ctx)
            t["RD"] = sb("counts_over", [NG, 2, 2 * NG], F32, ctx)
            prepare(nc, t, x, src, dst, w1, b1, w2, b2, gamma, beta, wq, wk, wv, binned)
            if stop > 1:
                place(nc, t, edge, binned)
        if stop > 2:
            t["sum"] = sb("node_sums", [P, NT + 1, F + 1])
            t["ids"] = sb("places", [P, 2, NG * NT], BF16)
            layer0(nc, t, binned)
            if stop == 3:
                dump(nc, t["sum"][:, 1:NT + 1, :])
        if stop > 3:
            t["qkv"] = sb("qkv_parts", [P, NG, 3, 3 * F], BF16)
            nodes(nc, t)
            if stop == 4:
                dump(nc, t["x"][:, :, :])
        if stop > 4:
            t["out"] = sb("attention_sums", [P, NT, F + HEADS])
            layer1(nc, t, binned, out)


def dump(nc, what):
    dbg = nc.dram_tensor("dbg", list(what.shape), F32).ap()
    with nc.semaphore("dbg") as s, nc.Block() as block:
        @block.sync
        def _(sp):
            sp.dma_start(dbg, what).then_inc(s, 16)
            sp.wait_ge(s, 16)


def prepare(nc, t, x, src, dst, w1, b1, w2, b2, gamma, beta, wq, wk, wv, binned):
    with ExitStack() as ctx:
        sb = lambda n, s, d=F32: ctx.enter_context(nc.sbuf_tensor(n, s, d))
        pb = lambda n, s, d=F32: ctx.enter_context(nc.psum_tensor(n, s, d))
        sem = lambda n: ctx.enter_context(nc.semaphore(n))
        fill = sb("fill", [P, NT * REC])
        ids = sb("ids", [P, 2, ET], I32)
        hi = sb("hi", [P, 2, ET], I32)
        lo = sb("lo", [P, 2, ET], I32)
        OH = sb("tile_onehots", [P, 2, 2, HB, NG], BF16)
        hist = pb("hist", [NG, NG])
        pref = pb("pref", [NG, 1])
        tot = pb("tot", [1, 1])
        tr = pb("h_turned", [F, QT * P])
        pa = pb("a_sum", [P, QT * F])
        close = sb("h_group", [P, QT, F])
        hT = sb("hT", [F + 1, QT * P])
        ni = sb("ni", [NG, NG], I32)
        nf = sb("nf", [NG, NG])
        n0 = sb("n0", [NG, NG])
        z = sb("zeros", [NG, NG])
        inc = sb("inc", [NG, NG])
        upper = sb("upper", [NG, NG])
        ones = sb("ones", [NG, 1])
        prefs = sb("prefs", [NG, 1])
        sq = sb("sq", [P, NT, F])
        st = sb("st", [P, 3, NT])
        rest = sb("rest", [P, QT * F])
        s_fillset, s_fill, s_ids, s_x, s_w = (sem(n) for n in ("fill_set", "filled", "ids_in", "x_in", "weights_in"))
        s_iota, s_v, s_c, s_oh, s_hist, s_tab, s_t = (sem(n) for n in ("iotas", "v", "constants", "onehots", "counted", "table", "tab"))
        s_sqrt, s_h, s_tr, s_hT, s_pa, s_hi, s_rest, s_mid, s_a = (sem(n) for n in ("rooted", "h_ready", "turned", "hT_ready", "a_summed", "a_hi", "a_rest", "a_mid", "a_done"))
        s_xz, s_close, s_steps = (sem(n) for n in ("x_zeroed", "h_drawn", "steps_known"))
        s_over, s_lo, s_meta = (sem(n) for n in ("filled_beyond", "tiles_and_places", "meta_ready"))
        block = ctx.enter_context(nc.Block())

        @block.sync
        def _(sp):
            sp.dma_start(ids[:, 0, :], src).then_inc(s_ids, 16)
            sp.dma_start(ids[:, 1, :], dst).then_inc(s_ids, 16)
            sp.wait_ge(s_xz, 1)
            sp.dma_start(t["x"][:, 0:NT - 1, :], x[0:(NT - 1) * P, :].rearrange("(t p) f -> p t f", p=P)).then_inc(s_x, 16)
            sp.dma_start(t["x"][0:LAST, NT - 1, :], x[(NT - 1) * P:N_NODES, :]).then_inc(s_x, 16)
            sp.wait_ge(s_fillset, 1)
            for j in range(NG):
                sp.dma_start(binned[j * P * SI:(j + 1) * P * SI, :].rearrange("(p i) w -> p (i w)", i=SI)[:, 0:NT * REC],
                             fill[:, :]).then_inc(s_fill, 16)
            sp.wait_ge(s_fill, 16 * NG)
            sp.wait_ge(s_steps, 1)
            apart(sp, t)
            steps = steps_beyond(sp, t)
            with sp.Fori(0, steps) as o:
                sp.dma_start(binned[ds(o * (STEP * P) + MAIN, STEP * P), :].rearrange("(p i) w -> p (i w)", p=P),
                             fill[:, 0:STEP * REC]).then_inc(s_over, 16)
            sp.wait_ge(s_over, steps * 16)
            apart(sp, t)

        @block.scalar
        def _(act):
            one = lambda v: v.rearrange("(a f) -> a f", a=1)
            act.dma_start(t["w1a"][0:F, :], w1[0:F, :]).then_inc(s_w, 16)
            act.dma_start(t["w1a"][F:F + 1, :], one(b1)).then_inc(s_w, 16)
            for k in range(4):
                act.dma_start(t["w1b"][FE * k:FE * k + FE, :], w1[F:F + FE, :]).then_inc(s_w, 16)
            act.dma_start(t["w2"][0:F, :], w2).then_inc(s_w, 16)
            act.dma_start(t["w2"][F:F + 1, :], one(b2)).then_inc(s_w, 16)
            for k, w in enumerate((wq, wk, wv)):
                act.dma_start(t["wqkv"][:, F * k:F * k + F], w).then_inc(s_w, 16)
            act.dma_start(t["gb"][:, 0, :], one(gamma).to_broadcast([P, F])).then_inc(s_w, 16)
            act.dma_start(t["gb"][:, 1, :], one(beta).to_broadcast([P, F])).then_inc(s_w, 16)
            act.wait_ge(s_lo, 1)
            for k, a in enumerate((hi[:, 0, :], hi[:, 1, :], lo[:, 0, :], lo[:, 1, :])):
                last = act.copy(t["meta"][:, :, (k + 2) % 4], a)
            last.then_inc(s_meta, 1)
            act.wait_ge(s_h, 4)
            act.activation(st[:, 2, :], st[:, 1, :], ACT.Sqrt, bias=t["eps"][:, 0:1], scale=1.0 / F).then_inc(s_sqrt, 1)
            act.wait_ge(s_h, 5)
            with act.Fori(0, NA) as g:
                act.wait_ge(s_tr, g + 1)
                act.copy(close[:, :, :], t["h"][:, ds(g * QT, QT), :]).then_inc(s_close, 1)
                act.wait_ge(s_tr, g + 2)
                act.wait_ge(s_pa, g + 1)
                act.copy(hT[0:F, :], tr[:, :]).then_inc(s_hT, 1)
                act.wait_ge(s_pa, g + 2)
                act.copy(t["A3"][:, ds(g * QT, QT), 0, :], pa[:, :].rearrange("p (t f) -> p t f", f=F)).then_inc(s_hi, 1)
                act.wait_ge(s_rest, g + 2)
                act.copy(t["A3"][:, ds(g * QT, QT), 1, :], rest[:, :].rearrange("p (t f) -> p t f", f=F)).then_inc(s_mid, 1)
            act.wait_ge(s_w, 16 * 13)

        @block.gpsimd
        def _(pool):
            pool.memset(t["x"][:, NT - 1, :], 0.0).then_inc(s_xz, 1)
            pool.iota(t["row"][:, :], [[1, P]], base=0, channel_multiplier=0, allow_small_or_imprecise_dtypes=True).then_inc(s_iota, 1)
            pool.iota(t["part"][:, :], [[1, 1]], base=0, channel_multiplier=1, allow_small_or_imprecise_dtypes=True).then_inc(s_iota, 1)
            pool.memset(fill[:, :], -1.0).then_inc(s_fillset, 1)
            pool.memset(t["h"][:, NT:NA * QT, :], 0.0).then_inc(s_iota, 1)
            pool.memset(t["eps"][:, :], LN_EPS).then_inc(s_iota, 1)
            pool.memset(t["hs"][:, ET:EP], float(NT)).then_inc(s_iota, 1)
            pool.memset(t["hd"][:, ET:EP], float(NT)).then_inc(s_iota, 1)

        @block.vector
        def _(v):
            n = [0]

            def link(ins):
                n[0] += 1
                ins.then_inc(s_v, 1)
                v.wait_ge(s_v, n[0])

            v.memset(z[:, :], 0.0)
            v.memset(t["bin"][:, ET:EP], 0.0)
            v.memset(ones[:, :], 1.0)
            v.memset(hT[F:F + 1, :], 1.0)
            v.wait_ge(s_iota, 6)
            v.tensor_copy(t["rowb"][:, :], t["row"][:, :])
            v.tensor_scalar(t["idf"][:, :], t["row"][:, :], t["part"][:, 0:1], None, ALU.is_equal)
            v.tensor_scalar(upper[:, :], t["row"][0:NG, 0:NG], t["part"][0:NG, 0:1], None, ALU.is_gt)
            v.tensor_scalar(t["idb"][:, :], t["row"][:, :], t["part"][:, 0:1], None, ALU.is_equal).then_inc(s_c, 1)
            v.wait_ge(s_ids, 32)
            v.tensor_scalar(hi[:, :, :], ids[:, :, :], 7, None, ALU.logical_shift_right)
            v.tensor_scalar(lo[:, :, :], ids[:, :, :], P - 1, None, ALU.bitwise_and).then_inc(s_lo, 1)
            v.wait_ge(s_lo, 1)
            v.tensor_copy(t["hs"][:, 0:ET], hi[:, 0, :])
            v.tensor_copy(t["hd"][:, 0:ET], hi[:, 1, :])
            v.wait_ge(s_x, 32)
            layer_norm(v, link, t["x"], t["h"], sq, st, s_h, s_sqrt, 1)
            v.tensor_scalar(t["h"][:, 0:NT, :], t["h"][:, 0:NT, :], 0.0, None, ALU.max).then_inc(s_h, 1)
            v.wait_ge(s_meta, 1)
            v.scalar_tensor_tensor(t["bin"][:, 0:ET], t["meta"][:, :, 3], float(SI), t["meta"][:, :, 2], ALU.mult, ALU.add)
            link(v.tensor_scalar(t["base"][:, :], t["meta"][:, :, 2], 1.0 / SI, None, ALU.mult))
            link(v.scalar_tensor_tensor(t["base"][:, :], t["meta"][:, :, 3], float(P), t["base"][:, :], ALU.mult, ALU.add))
            with v.Fori(0, NA) as g:
                for b in range(HU):
                    v.wait_ge(s_hist, g * HU + b + 1)
                    for k, a in enumerate((t["hs"], t["hd"])):
                        last = v.tensor_tensor(OH[:, b % 2, k, :, :],
                                               a[:, ds((g * HU + b) * HB, HB)].rearrange("p (t a) -> p t a", a=1).to_broadcast([P, HB, NG]),
                                               t["rowb"][:, 0:NG].rearrange("p (a n) -> p a n", a=1).to_broadcast([P, HB, NG]), ALU.is_equal)
                    last.then_inc(s_oh, 1)
                    if b == 2:
                        v.wait_ge(s_hi, g + 1)
                        v.tensor_tensor(rest[:, :].rearrange("p (t f) -> p t f", f=F), pa[:, :].rearrange("p (t f) -> p t f", f=F),
                                        t["A3"][:, ds(g * QT, QT), 0, :], ALU.subtract).then_inc(s_rest, 1)
                    if b == 3:
                        v.wait_ge(s_mid, g + 1)
                        v.tensor_tensor(t["A3"][:, ds(g * QT, QT), 2, :], rest[:, :].rearrange("p (t f) -> p t f", f=F),
                                        t["A3"][:, ds(g * QT, QT), 1, :], ALU.subtract).then_inc(s_a, 1)
            v.wait_ge(s_hist, NA * HU + 2)
            v.tensor_scalar(n0[:, :], hist[:, :], -1.0, 0.0, ALU.add, ALU.max)
            link(v.tensor_scalar(ni[:, :], hist[:, :], -1.0, 0.0, ALU.add, ALU.max))
            link(v.tensor_scalar(ni[:, :], ni[:, :], 7, None, ALU.logical_shift_right))
            link(v.tensor_copy(nf[:, :], ni[:, :]))
            link(v.tensor_tensor_scan(inc[:, :], nf[:, :], z[:, :], 0.0, ALU.add, ALU.add))
            v.tensor_tensor(n0[:, :], inc[:, :], nf[:, :], ALU.subtract).then_inc(s_tab, 1)
            v.wait_ge(s_t, 1)
            link(v.tensor_copy(prefs[:, :], pref[:, :]))
            link(v.tensor_scalar(n0[:, :], n0[:, :], prefs[:, 0:1], float(P), ALU.add, ALU.mult))
            for b in range(2):
                v.tensor_scalar(t["RD"][:, b, NG:], n0[:, :], float(MAIN - P), None, ALU.add)
                v.memset(t["RD"][:, b, 0:NG], 0.0)
            link(v.tensor_scalar(t["nover"][:, :], tot[:, :], float(STEP - 1), float(STEP), ALU.add, ALU.max))
            v.tensor_scalar(t["nover"][:, :], t["nover"][:, :], 3, None, ALU.logical_shift_right).then_inc(s_steps, 1)

        @block.tensor
        def _(pe):
            pe.wait_ge(s_c, 1)
            pe.matmul(hist[:, :], z[:, :], z[:, :], start=True, stop=False, skip_group_check=True).then_inc(s_hist, 2)
            pe.sem_inc(s_tr, 1)
            pe.sem_inc(s_pa, 1)
            pe.sem_inc(s_rest, 1)
            pe.wait_ge(s_w, 16 * 13)
            with pe.Fori(0, NA) as g:
                for b in range(HU):
                    pe.wait_ge(s_oh, g * HU + b + 1)
                    for k in range(HB):
                        last = pe.matmul(hist[:, :], OH[:, b % 2, 1, k, :], OH[:, b % 2, 0, k, :], start=False, stop=False, skip_group_check=True)
                    last.then_inc(s_hist, 1)
                    if b == 0:
                        pe.wait_ge(s_close, g + 1)
                        apart(pe, t)
                        for k in range(QT):
                            last = pe.transpose(tr[:, k * P:k * P + P], close[:, k, :], t["idf"][:, :])
                        last.then_inc(s_tr, 1)
                    if b == 1:
                        pe.wait_ge(s_hT, g + 1)
                        pe.wait_ge(s_rest, g + 1)
                        for k in range(QT):
                            last = pe.matmul(pa[:, k * F:k * F + F], hT[:, k * P:k * P + P], t["w1a"][:, :], start=True, stop=True)
                        last.then_inc(s_pa, 1)
            pe.wait_ge(s_tab, 1)
            pe.matmul(pref[:, :], upper[:, :], inc[:, NG - 1:NG], start=True, stop=True)
            pe.matmul(tot[:, :], ones[:, :], inc[:, NG - 1:NG], start=True, stop=True).then_inc(s_t, 1)


def layer_norm(v, link, x, y, sq, st, s_h, s_sqrt, roots):
    full = [P, NT, F]
    b = lambda a: a.rearrange("p (t a) -> p t a", a=1).to_broadcast(full)
    link(v.tensor_reduce(st[:, 0, :], x[:, :, :], AX.X, ALU.add))
    link(v.tensor_scalar(st[:, 0, :], st[:, 0, :], 1.0 / F, None, ALU.mult))
    link(v.tensor_tensor(y[:, 0:NT, :], x[:, :, :], b(st[:, 0, :]), ALU.subtract))
    link(v.tensor_tensor(sq[:, :, :], y[:, 0:NT, :], y[:, 0:NT, :], ALU.mult))
    v.tensor_reduce(st[:, 1, :], sq[:, :, :], AX.X, ALU.add).then_inc(s_h, 4)
    v.wait_ge(s_sqrt, roots)
    link(v.reciprocal(st[:, 0, :], st[:, 2, :]))
    link(v.tensor_tensor(y[:, 0:NT, :], y[:, 0:NT, :], b(st[:, 0, :]), ALU.mult))


def place(nc, t, edge, binned):
    with ExitStack() as ctx:
        sb = lambda n, s, d=F32: ctx.enter_context(nc.sbuf_tensor(n, s, d))
        pb = lambda n, s, d=F32: ctx.enter_context(nc.psum_tensor(n, s, d))
        sem = lambda n: ctx.enter_context(nc.semaphore(n))
        rec = sb("records", [P, BODY * QT, REC])
        rows = sb("rows", [P, BODY * QT], I32)
        OHs = sb("src_onehots", [P, BODY, QT, NG], BF16)
        OHd = sb("dst_onehots", [P, BODY, QT, NG], BF16)
        OHdT = sb("dst_onehots_turned", [NG, 2, QT * P])
        mask = sb("earlier", [P, QT * P])
        junk = sb("junk", [P, QT, QT * P], BF16)
        both = sb("both", [P, 2, QT, 2, NG])
        found = sb("found", [P, BODY, QT, 2])
        inside = sb("inside", [P, BODY, QT])
        rank = sb("rank", [P, BODY, QT])
        main = sb("main", [P, BODY, QT])
        over = sb("over", [P, BODY, QT])
        id64 = sb("id64", [P, P], BF16)
        zb = sb("zb", [P, NG], BF16)
        pbin = [pb(f"bins{i}", [P, QT * P]) for i in range(2)]
        ptr = [pb(f"turned{i}", [NG, 2 * QT * P], BF16) for i in range(2)]
        pg = [pb(f"gathered{i}", [P, QT, 2 * NG]) for i in range(2)]
        cnt = pb("counts", [NG, NG])
        s_c, s_oh, s_bin, s_tr, s_trc, s_g, s_cnt, s_rd, s_in, s_v, s_row, s_meta = (sem(n) for n in (
            "constants", "onehots_ready", "bins_ready", "turned_ready", "turned_copied", "gathered_ready", "group_counted",
            "counts_copied", "inside_ready", "v", "rows_ready", "meta_ready"))
        s_edge = [sem(f"edge_in{c}") for c in range(4)]
        s_scat = [sem(f"scattered{c}") for c in range(4)]
        full = [16 * QT * (b - a) for a, b in CHUNKS]
        chunk_of = [c for c, (a, b) in enumerate(CHUNKS) for _ in range(a, b)]
        s_fin = sem("fin")
        block = ctx.enter_context(nc.Block())

        @block.sync
        def _(sp):
            for c, (a, b) in enumerate(CHUNKS):
                sp.dma_start(rec[:, a * QT:b * QT, 0:FE], edge[:, a * QT:b * QT, :]).then_inc(s_edge[c], 16)
            with sp.Fori(1, BODIES) as i:
                for c, (a, b) in enumerate(CHUNKS):
                    sp.wait_ge(s_scat[c], i * full[c])
                    sp.dma_start(rec[:, a * QT:b * QT, 0:FE],
                                 edge[:, ds(i * BODY * QT + a * QT, (b - a) * QT), :]).then_inc(s_edge[c], 16)
            for c in range(4):
                sp.wait_ge(s_scat[c], BODIES * full[c])

        @block.scalar
        def _(act):
            act.wait_ge(s_tr, 1)
            act.copy(OHdT[:, 0, :], ptr[0][:, 0:QT * P]).then_inc(s_trc, 1)
            with act.Fori(0, BODIES) as i:
                for k in range(BODY):
                    g = i * BODY + k
                    if k in [a for a, _ in CHUNKS]:
                        c = chunk_of[k]
                        a, b = CHUNKS[c]
                        act.wait_ge(s_edge[c], (i + 1) * 16)
                        act.copy(rec[:, a * QT:b * QT, FE:REC], t["meta"][:, ds((i * BODY + a) * QT, (b - a) * QT), :]).then_inc(s_meta, 1)
                    act.wait_ge(s_cnt, g + 1 + 1)
                    act.wait_ge(s_g, (g if k < BODY - 1 else g + 1) + 1)
                    act.copy(t["RD"][:, (k + 1) % BODY % 2, 0:NG], cnt[:, :]).then_inc(s_rd, 1)
                    act.wait_ge(s_tr, g + 2)
                    act.wait_ge(s_g, (g if k < BODY - 1 else g + 1) + 1)
                    act.copy(OHdT[:, (k + 1) % BODY % 2, :], ptr[(k + 1) % BODY % 2][:, 0:QT * P]).then_inc(s_trc, 1)

        @block.tensor
        def _(pe):
            def turn(k):
                for q in range(QT):
                    last = pe.transpose(ptr[k % 2][:, q * P:q * P + P], OHd[:, k, q, :], t["idb"][:, :])
                last.then_inc(s_tr, 1)

            def bins(k, g):
                for q in range(QT):
                    at = g * QT + q
                    c = pbin[k % 2][:, q * P:q * P + P]
                    pe.matmul(c, col(t["hd"][:, ds(at, 1)], P), id64[:, :], start=True, stop=False)
                    last = pe.matmul(c, col(t["hs"][:, ds(at, 1)], P), t["idb"][:, :], start=False, stop=True)
                last.then_inc(s_bin, 1)

            for s in (s_in, s_trc, s_g, s_rd, s_v, s_cnt):
                pe.sem_inc(s, 1)
            pe.wait_ge(s_c, 1)
            pe.matmul(cnt[:, :], zb[:, :], zb[:, :], start=True, stop=False, skip_group_check=True)
            pe.wait_ge(s_oh, 1)
            turn(0)
            bins(0, 0)
            with pe.Fori(0, BODIES) as i:
                for k in range(BODY):
                    g = i * BODY + k
                    k1 = (k + 1) % BODY
                    pe.wait_ge(s_trc, g + 1 + 1)
                    pe.wait_ge(s_rd, g + 1)
                    pe.wait_ge(s_v, (6 * g if k == 0 else 6 * (g - 1) if k == 1 else 6 * (g - 2) + 1) + 1)
                    for q in range(QT):
                        last = pe.matmul(pg[k % 2][:, q, :], OHdT[:, k % 2, q * P:q * P + P], t["RD"][:, k % 2, :], start=True, stop=True)
                    last.then_inc(s_g, 1)
                    pe.wait_ge(s_rd, g + 1)
                    for q in range(QT):
                        last = pe.matmul(cnt[:, :], OHd[:, k, q, :], OHs[:, k, q, :], start=False, stop=False, skip_group_check=True)
                    last.then_inc(s_cnt, 1)
                    pe.wait_ge(s_oh, g + 2)
                    pe.wait_ge(s_trc, (g if k1 else g + 1) + 1)
                    apart(pe, t)
                    turn(k1)
                    pe.wait_ge(s_in, (g if k1 else g + 1) + 1)
                    bins(k1, g + 1)

        @block.gpsimd
        def _(pool):
            with pool.Fori(0, BODIES) as i:
                for k in range(BODY):
                    g = i * BODY + k
                    c = chunk_of[k]
                    if k == CHUNKS[c][0]:
                        pool.wait_ge(s_edge[c], (i + 1) * 16)
                        pool.wait_ge(s_meta, i * 4 + c + 1)
                    pool.wait_ge(s_row, g + 1)
                    apart(pool, t)
                    for q in range(QT):
                        e = k * QT + q
                        pool.indirect_dma_start(binned, bass.IndirectOffsetOnAxis(rows[:, e:e + 1], 0),
                                                rec[:, e, :], None).then_inc(s_scat[c], 16)

        @block.vector
        def _(v):
            def onehot(o, a, k, g):
                return v.tensor_tensor(o[:, k, :, :], a[:, ds(g * QT, QT)].rearrange("p (t a) -> p t a", a=1).to_broadcast([P, QT, NG]),
                                       t["rowb"][:, 0:NG].rearrange("p (a n) -> p a n", a=1).to_broadcast([P, QT, NG]), ALU.is_equal)

            def compare(k, g, q):
                n = (q + 1) * P
                return v.scalar_tensor_tensor(junk[:, q, 0:n], pbin[k % 2][:, 0:n], t["bin"][:, ds(g * QT + q, 1)], mask[:, (QT - 1 - q) * P:],
                                              ALU.is_equal, ALU.mult, accum_out=inside[:, k, q:q + 1])

            v.tensor_scalar(id64[:, :], t["idf"][:, :], float(SI), None, ALU.mult)
            v.memset(mask[:, 0:(QT - 1) * P], 1.0)
            v.tensor_scalar(mask[:, (QT - 1) * P:], t["row"][:, :], t["part"][:, 0:1], None, ALU.is_lt)
            v.memset(zb[:, :], 0.0).then_inc(s_c, 1)
            v.wait_ge(s_c, 1)
            for g in range(2):
                onehot(OHs, t["hs"], g, g)
                onehot(OHd, t["hd"], g, g).then_inc(s_oh, 1)
            v.wait_ge(s_oh, 2)
            v.wait_ge(s_bin, 1)
            for q in range(QT):
                last = compare(0, 0, q)
            last.then_inc(s_in, 1)
            with v.Fori(0, BODIES) as i:
                for k in range(BODY):
                    g = i * BODY + k
                    s, k1, k2 = k % 2, (k + 1) % BODY, (k + 2) % BODY
                    v.wait_ge(s_g, g + 1 + 1)
                    v.tensor_tensor(both[:, s, :, :, :], pg[s][:, :, :].rearrange("p t (a n) -> p t a n", a=2),
                                    OHs[:, k, :, :].rearrange("p t (a n) -> p t a n", a=1).to_broadcast([P, QT, 2, NG]), ALU.mult).then_inc(s_v, 1)
                    v.wait_ge(s_cnt, g + 1)
                    onehot(OHs, t["hs"], k2, g + 2)
                    v.wait_ge(s_v, g * 6 + 1 + 1)
                    v.tensor_reduce(found[:, k, :, :], both[:, s, :, :, :], AX.X, ALU.add).then_inc(s_v, 1)
                    onehot(OHd, t["hd"], k2, g + 2).then_inc(s_oh, 1)
                    v.wait_ge(s_v, g * 6 + 2 + 1)
                    v.wait_ge(s_in, g + 1 + 1)
                    v.tensor_tensor(rank[:, k, :], inside[:, k, :], found[:, k, :, 0], ALU.add).then_inc(s_v, 1)
                    v.wait_ge(s_bin, g + 2)
                    compare(k1, g + 1, 0)
                    v.wait_ge(s_v, g * 6 + 3 + 1)
                    v.scalar_tensor_tensor(main[:, k, :], rank[:, k, :], float(P - 1), t["base"][:, ds(g * QT, QT)], ALU.min, ALU.add).then_inc(s_v, 1)
                    v.tensor_tensor(over[:, k, :], rank[:, k, :], found[:, k, :, 1], ALU.add).then_inc(s_v, 1)
                    compare(k1, g + 1, 1)
                    v.wait_ge(s_v, g * 6 + 5 + 1)
                    v.scalar_tensor_tensor(over[:, k, :], rank[:, k, :], P - 0.5, over[:, k, :], ALU.is_gt, ALU.mult).then_inc(s_v, 1)
                    compare(k1, g + 1, 2)
                    v.wait_ge(s_v, g * 6 + 6 + 1)
                    c = chunk_of[k]
                    if k == CHUNKS[c][0]:
                        v.wait_ge(s_edge[c], (i + 1) * 16)
                    v.scalar_tensor_tensor(rows[:, k * QT:k * QT + QT], main[:, k, :], float(SI), over[:, k, :],
                                           ALU.mult, ALU.max).then_inc(s_row, 1)
                    compare(k1, g + 1, 3).then_inc(s_in, 1)


LB = -(-NT // QT)
LAST_K = LB - 1
assert NT == LAST_K * QT + 1 and LAST_K % 2 == 0
LCHUNKS = [(0, 4), (4, 8), (8, LB)]


def tiles(k):
    return range(k * QT, min(k * QT + QT, NT))


def slot(k):
    return 2 if k == LAST_K else k % 2


def before(k):
    return -1 if k == LAST_K else k - 2 if k >= 2 else k - 3


def bank_before(k):
    return k - 2 if k >= 1 else -1


CREDIT = LB


def deep(k):
    return 3 if k == LAST_K else k % 3


def before_deep(k):
    return -1 if k == LAST_K else k - 3 if k >= 3 else k - 4


WIDE = (QT, QT, 1)
DEEP = (QT, QT, QT, 1)
MW = 3 * F + 1


def layer0(nc, t, binned):
    with ExitStack() as ctx:
        sb = lambda n, s, d=F32: ctx.enter_context(nc.sbuf_tensor(n, s, d))
        pb = lambda n, s, d=F32: ctx.enter_context(nc.psum_tensor(n, s, d))
        sem = lambda n: ctx.enter_context(nc.semaphore(n))
        rec = sb("bin_row", [P, NT, REC])
        close = sb("edge_features", [P, NT, FE])
        places = [sb(f"places_spread{n}", [P, w * P], BF16) for n, w in enumerate(WIDE)]
        GT = [sb(f"gather{n}", [P, w * P], BF16) for n, w in enumerate(WIDE)]
        eT = [sb(f"edge_turned{n}", [w * FE, P]) for n, w in enumerate(WIDE)]
        S = [sb(f"scatter{n}", [P, w, P], BF16) for n, w in enumerate(DEEP)]
        msg = [sb(f"messages{n}", [P, w, MW], BF16) for n, w in enumerate(DEEP)]
        rest = [sb(f"rest_of_messages{n}", [P, w * F]) for n, w in enumerate(DEEP)]
        wd = sb("w1b_diagonal", [P, QT, F])
        pid = [pb(f"places{n}", [P, QT * P]) for n in range(2)]
        ptr = [pb(f"edges_turned{n}", [P, P]) for n in range(2)]
        pre = [pb(f"before_relu{n}", [P, QT * F]) for n in range(2)]
        acc = pb("sums", [P, MW])
        s_ld = [sem(f"row_in{c}") for c in range(3)]
        s_c, s_ids, s_pid, s_pl, s_tr, s_gt, s_et, s_pre, s_hi, s_rest, s_mid, s_msg, s_s, s_acc, s_out = (sem(n) for n in (
            "constants", "ids_ready", "places_up", "places_ready", "edges_turned", "gather_ready", "edges_ready", "sums_ready",
            "messages_hi", "rest_ready", "messages_mid", "messages_ready", "scatter_ready", "group_added", "row_kept"))
        block = ctx.enter_context(nc.Block())
        tiled = lambda a, n: a[:, 0:n * F].rearrange("p (t f) -> p t f", f=F)

        def load(sp, c, j):
            a, b = LCHUNKS[c][0] * QT, min(LCHUNKS[c][1] * QT, NT)
            sp.dma_start(rec[:, a:b, :], binned[ds(j * (P * SI), P * SI), :].rearrange("(p i) w -> p i w", i=SI)[:, a:b, :]).then_inc(s_ld[c], 16)

        @block.sync
        def _(sp):
            for c in range(3):
                load(sp, c, 0)
            with sp.Fori(1, NT) as j:
                for c, (a, b) in enumerate(LCHUNKS):
                    sp.wait_ge(s_s, (j - 1) * LB + CREDIT + b)
                    apart(sp, t)
                    sp.wait_ge(s_ids, (j - 1) * 3 + c + 1)
                    apart(sp, t)
                    load(sp, c, j)
            for c in range(2):
                sp.wait_ge(s_s, (NT - 1) * LB + CREDIT + LCHUNKS[c][1])
                sp.wait_ge(s_ids, (NT - 1) * 3 + c + 1)
                load(sp, c, NT)
            for c in range(2):
                sp.wait_ge(s_ld[c], 16 * (NT + 1))

        @block.gpsimd
        def _(pool):
            def keep_ids(c, j):
                a, b = LCHUNKS[c][0] * QT, min(LCHUNKS[c][1] * QT, NT)
                pool.wait_ge(s_ld[c], (j + 1) * 16)
                apart(pool, t)
                pool.tensor_copy(t["ids"][:, :, ds(j * NT + a, b - a)], rec[:, a:b, FE:FE + 2].rearrange("p t c -> p c t"))

            def draw_close(c, half, j):
                a, b = LCHUNKS[c][0] * QT, min(LCHUNKS[c][1] * QT, NT)
                a, b = ((a, a + 2 * QT), (a + 2 * QT, b))[half]
                pool.wait_ge(s_tr, (j - 1) * LB + CREDIT + LCHUNKS[c][1])
                apart(pool, t)
                last = pool.tensor_copy(close[:, a:b, :], rec[:, a:b, 0:FE])
                if half:
                    last.then_inc(s_ids, 1)

            pieces = {1: (2, 0), 2: (2, 1), 3: (2, 2), 5: (0, 0), 6: (0, 1), 7: (0, 2), 8: (1, 0), 9: (1, 1), 10: (1, 2)}

            def piece(c, part, j):
                if part:
                    draw_close(c, part - 1, j)
                else:
                    keep_ids(c, j)

            for c, part in ((0, 0), (0, 1), (0, 2), (1, 0), (1, 1), (1, 2)):
                piece(c, part, 0)
            with pool.Fori(0, NT) as j:
                for k in range(LB):
                    n = len(tiles(k))
                    pool.wait_ge(s_mid, j * LB + k + 1)
                    apart(pool, t)
                    pool.tensor_tensor(msg[deep(k)][:, :, 2 * F:3 * F], tiled(rest[deep(k)], n), msg[deep(k)][:, :, F:2 * F], ALU.subtract).then_inc(s_msg, 1)
                    if k in pieces:
                        piece(*pieces[k], j if k < 5 else j + 1)

        @block.vector
        def _(v):
            v.memset(wd[:, :, :], 0.0).then_inc(s_c, 1)
            for k in (LAST_K - 1, LAST_K):
                v.memset(S[deep(k)][:, :, :], 0.0)
            for m in msg:
                v.memset(m[:, :, 0:3 * F], 0.0)
                last = v.memset(m[:, :, 3 * F:MW], 1.0)
            v.wait_ge(s_c, 1)
            for q in range(QT):
                last = v.tensor_copy(wd[FE * q:FE * q + FE, q, :], t["w1b"][FE * q:FE * q + FE, :])
            last.then_inc(s_c, 1)
            v.wait_ge(s_c, 2)

            def gather(k, n):
                w = len(tiles(k)) * P
                v.wait_ge(s_pl, n + CREDIT + 1)
                v.wait_ge(s_pre, n + CREDIT - k + before(k) + 1)
                v.tensor_scalar(GT[slot(k)][:, 0:w], places[slot(k)][:, 0:w], t["part"][:, 0:1], None, ALU.is_equal).then_inc(s_gt, 1)

            def scatter(k, j):
                q = tiles(k)
                n = len(q)
                for c, (a, _) in enumerate(LCHUNKS):
                    if k == a:
                        v.wait_ge(s_ld[c], (j + 1) * 16)
                v.wait_ge(s_acc, j * LB + CREDIT + before_deep(k) + 1)
                v.tensor_tensor(S[deep(k)][:, 0:n, :], t["row"][:, :].rearrange("p (a n) -> p a n", a=1).to_broadcast([P, n, P]),
                                rec[:, q[0]:q[0] + n, FE + 1:FE + 2].to_broadcast([P, n, P]), ALU.is_equal).then_inc(s_s, 1)

            def keep_row(j):
                v.wait_ge(s_acc, (j + 1) * LB + CREDIT)
                to = t["sum"][:, ds(j + 1, 1), :].rearrange("p a f -> p (a f)")
                v.tensor_copy(to[:, F:F + 1], acc[:, 3 * F:MW])
                v.tensor_reduce(to[:, 0:F], acc[:, 0:3 * F].rearrange("p (c f) -> p f c", c=3), AX.X, ALU.add).then_inc(s_out, 1)

            gather(0, 0)
            with v.Fori(0, NT) as j:
                for k in range(LB):
                    n = len(tiles(k))
                    scatter(k, j)
                    gather((k + 1) % LB, j * LB + k + 1)
                    v.wait_ge(s_hi, j * LB + k + 1)
                    v.scalar_tensor_tensor(tiled(rest[deep(k)], n), tiled(pre[k % 2], n), 0.0, msg[deep(k)][:, :, 0:F], ALU.max, ALU.subtract).then_inc(s_rest, 1)
                    if k == 1:
                        keep_row(j - 1)
            keep_row(NT - 1)

        @block.scalar
        def _(act):
            def spread(k, n):
                w = len(tiles(k)) * P
                act.wait_ge(s_pid, n + 1)
                act.wait_ge(s_gt, n + CREDIT - k + before(k) + 1)
                act.copy(places[slot(k)][:, 0:w], pid[k % 2][:, 0:w]).then_inc(s_pl, 1)

            def edges(k, n):
                w = len(tiles(k)) * FE
                act.wait_ge(s_tr, n + CREDIT + 1)
                act.wait_ge(s_pre, n + CREDIT - k + before(k) + 1)
                act.copy(eT[slot(k)][0:w, :], ptr[k % 2][0:w, :]).then_inc(s_et, 1)

            def middle(k, j):
                n = len(tiles(k))
                act.wait_ge(s_rest, j * LB + CREDIT + k + 1)
                act.copy(msg[deep(k)][:, :, F:2 * F], tiled(rest[deep(k)], n)).then_inc(s_mid, 1)

            spread(0, 0)
            edges(0, 0)
            with act.Fori(0, NT) as j:
                for k in range(LB):
                    n = len(tiles(k))
                    k1 = (k + 1) % LB
                    spread(k1, j * LB + k + 1)
                    if k:
                        middle(k - 1, j)
                    edges(k1, j * LB + k + 1)
                    act.wait_ge(s_pre, j * LB + CREDIT + k + 1)
                    act.wait_ge(s_acc, j * LB + CREDIT + before_deep(k) + 1)
                    act.activation(msg[deep(k)][:, :, 0:F], tiled(pre[k % 2], n), ACT.Relu).then_inc(s_hi, 1)
                middle(LAST_K, j)

        @block.tensor
        def _(pe):
            def ids_up(k, n, j):
                q = tiles(k)
                for c, (a, _) in enumerate(LCHUNKS):
                    if k == a:
                        pe.wait_ge(s_ids, j * 3 + c + 1)
                pe.wait_ge(s_pl, n - k + CREDIT + bank_before(k) + 1)
                for m, i in enumerate(q):
                    last = pe.matmul(pid[k % 2][:, m * P:m * P + P], col(t["ids"][:, 0, ds(j * NT + i, 1)], P), t["idb"][:, :], start=True, stop=True)
                last.then_inc(s_pid, 1)
                pe.wait_ge(s_et, n - k + CREDIT + bank_before(k) + 1)
                pe.transpose(ptr[k % 2][0:len(q) * FE, :], close[:, q[0]:q[0] + len(q), :].rearrange("p t f -> p (t f)"), t["idf"][:, :]).then_inc(s_tr, 1)

            def sums(k, j):
                q = tiles(k)
                g = j * LB + k
                pe.wait_ge(s_et, g + CREDIT + 1)
                pe.wait_ge(s_rest, j * LB + CREDIT + bank_before(k) + 1)
                pe.matmul(pre[k % 2][:, 0:len(q) * F], eT[slot(k)][0:len(q) * FE, :], wd[0:len(q) * FE, 0:len(q), :], start=True, stop=False, skip_group_check=True)
                pe.wait_ge(s_gt, g + CREDIT + 1)
                for m, i in enumerate(q):
                    for part in range(3):
                        last = pe.matmul(pre[k % 2][:, m * F:m * F + F], GT[slot(k)][:, m * P:m * P + P], t["A3"][:, i, part, :],
                                         start=False, stop=(part == 2), skip_group_check=True)
                last.then_inc(s_pre, 1)

            def add(k, j):
                q = tiles(k)
                g = j * LB + k
                pe.wait_ge(s_msg, g + CREDIT + 1)
                pe.wait_ge(s_s, g + CREDIT + 1)
                if k == 0:
                    pe.wait_ge(s_out, j + 1)
                for m, i in enumerate(q):
                    last = pe.matmul(acc[:, :], S[deep(k)][:, m, :], msg[deep(k)][:, m, :], start=(i == 0), stop=(i == NT - 1), skip_group_check=True)
                last.then_inc(s_acc, 1)

            pe.wait_ge(s_c, 2)
            for s in (s_pl, s_tr, s_gt, s_et, s_pre, s_rest, s_msg, s_s):
                pe.sem_inc(s, CREDIT)
            pe.sem_inc(s_acc, CREDIT - 2)
            pe.matmul(acc[:, :], S[3][:, 0, :], msg[3][:, 0, :], start=True, stop=False, skip_group_check=True)
            ids_up(0, 0, 0)
            with pe.Fori(0, NT) as j:
                for k in range(LB):
                    k1 = (k + 1) % LB
                    ids_up(k1, j * LB + k + 1, j if k1 else j + 1)
                    sums(k, j)
                    add((k - 2) % LB, j if k >= 2 else j - 1)
            add(LAST_K - 1, NT - 1)
            add(LAST_K, NT - 1)

    beyond0(nc, t, binned)


def steps_beyond(eng, t):
    return eng.value_load(t["nover"][0:1, 0:1], min_val=1, max_val=EO // STEP)


def beyond_rows(binned, o, b, columns):
    return binned[ds(o * (STEP * P) + (MAIN + b * QT * P), QT * P), columns].rearrange("(q p) w -> p q w", p=P)


def beyond0(nc, t, binned):
    with ExitStack() as ctx:
        sb = lambda n, s, d=F32: [ctx.enter_context(nc.sbuf_tensor(f"beyond_{n}{b}", s, d)) for b in range(QB)]
        pb = lambda n, w: [ctx.enter_context(nc.psum_tensor(f"beyond_{n}{b}", [P, w], F32)) for b in range(QB)]
        sem = lambda n: ctx.enter_context(nc.semaphore(n))
        rec = sb("records", [P, QT, REC])
        close = sb("features", [P, QT * FE])
        ids = sb("places", [P, QT], BF16)
        at = sb("tiles", [1, QT, 2], I32)
        GT = sb("gather", [P, QT * P], BF16)
        S = sb("scatter", [P, QT, P])
        eT = sb("edges_turned", [P, P])
        msg = sb("messages", [P, QT, F + 1])
        wd = ctx.enter_context(nc.sbuf_tensor("beyond_w1b", [P, QT, F], F32))
        pid, ptr, pre, acc = pb("places_up", QT * P), pb("edges_up", P), pb("before_relu", QT * F), pb("sums", QT * (F + 1))
        s_ld = [sem(f"beyond_in{b}") for b in range(QB)]
        s_c, s_close, s_ids, s_at, s_pid, s_tr, s_gt, s_et, s_pre, s_msg, s_s, s_acc, s_out = (sem(n) for n in (
            "constants", "features_ready", "ids_ready", "tiles_known", "places_up", "edges_turned", "gather_ready", "edges_ready",
            "sums_ready", "messages_ready", "scatter_ready", "group_added", "group_kept"))
        block = ctx.enter_context(nc.Block())

        @block.sync
        def _(sp):
            with sp.Fori(0, steps_beyond(sp, t)) as o:
                for b in range(QB):
                    sp.wait_ge(s_s, o * QB + b + 1)
                    apart(sp, t)
                    sp.wait_ge(s_close, o * QB + b + 1)
                    apart(sp, t)
                    sp.dma_start(rec[b][:, :, :], beyond_rows(binned, o, b, slice(0, REC))).then_inc(s_ld[b], 16)

        @block.gpsimd
        def _(pool):
            with pool.Fori(0, steps_beyond(pool, t)) as o:
                for b in range(QB):
                    pool.wait_ge(s_ld[b], (o + 1) * 16)
                    pool.wait_ge(s_tr, o * QB + b + 1)
                    apart(pool, t)
                    pool.tensor_copy(close[b][:, :].rearrange("p (t f) -> p t f", f=FE), rec[b][:, :, 0:FE]).then_inc(s_close, 1)

        @block.vector
        def _(v):
            v.memset(wd[:, :, :], 0.0).then_inc(s_c, 1)
            for m in msg:
                v.memset(m[:, :, F:F + 1], 1.0)
            v.wait_ge(s_c, 1)
            for q in range(QT):
                last = v.tensor_copy(wd[FE * q:FE * q + FE, q, :], t["w1b"][FE * q:FE * q + FE, :])
            last.then_inc(s_c, 1)
            with v.Fori(0, steps_beyond(v, t)) as o:
                for b in range(QB):
                    v.wait_ge(s_ld[b], (o + 1) * 16)
                    v.tensor_copy(ids[b][:, :], rec[b][:, :, FE]).then_inc(s_ids, 1)
                    v.tensor_scalar(at[b][:, :, :], rec[b][0:1, :, FE + 2:FE + 4], 0.0, None, ALU.max).then_inc(s_at, 1)
                    v.tensor_tensor(S[b][:, :, :], t["row"][:, :].rearrange("p (a n) -> p a n", a=1).to_broadcast([P, QT, P]),
                                    rec[b][:, :, FE + 1:FE + 2].to_broadcast([P, QT, P]), ALU.is_equal).then_inc(s_s, 1)
                for b in range(QB):
                    v.wait_ge(s_pid, o * QB + b + 1)
                    v.tensor_scalar(GT[b][:, :], pid[b][:, :], t["part"][:, 0:1], None, ALU.is_equal).then_inc(s_gt, 1)
                v.wait_ge(s_at, (o + 1) * QB)
                apart(v, t)
                to = [[v.value_load(at[b][0:1, q, 1:2], min_val=0, max_val=NT - 1) for q in range(QT)] for b in range(QB)]
                for b in range(QB):
                    v.wait_ge(s_acc, o * QB + b + 1)
                    for q in range(QT):
                        row = t["sum"][:, ds(to[b][q] + 1, 1), :].rearrange("p a f -> p (a f)")
                        v.wait_ge(s_out, (o * QB + b) * QT + q + 1)
                        v.tensor_tensor(row, row, acc[b][:, q * (F + 1):(q + 1) * (F + 1)], ALU.add).then_inc(s_out, 1)

        @block.scalar
        def _(act):
            with act.Fori(0, steps_beyond(act, t)) as o:
                for b in range(QB):
                    act.wait_ge(s_tr, (o + 1) * QB + b + 1)
                    act.copy(eT[b][:, :], ptr[b][:, :]).then_inc(s_et, 1)
                for b in range(QB):
                    act.wait_ge(s_pre, o * QB + b + 1)
                    act.activation(msg[b][:, :, 0:F], pre[b][:, :].rearrange("p (t f) -> p t f", f=F), ACT.Relu).then_inc(s_msg, 1)

        @block.tensor
        def _(pe):
            pe.wait_ge(s_c, 2)
            pe.sem_inc(s_out, 1)
            for s in (s_s, s_close, s_tr):
                pe.sem_inc(s, QB)
            with pe.Fori(0, steps_beyond(pe, t)) as o:
                for b in range(QB):
                    pe.wait_ge(s_ids, o * QB + b + 1)
                    for q in range(QT):
                        last = pe.matmul(pid[b][:, q * P:q * P + P], col(ids[b][:, q:q + 1], P), t["idb"][:, :], start=True, stop=True)
                    last.then_inc(s_pid, 1)
                    pe.wait_ge(s_close, (o + 1) * QB + b + 1)
                    pe.transpose(ptr[b][:, :], close[b][:, :], t["idf"][:, :]).then_inc(s_tr, 1)
                for b in range(QB):
                    pe.wait_ge(s_at, o * QB + b + 1)
                    apart(pe, t)
                    of = [pe.value_load(at[b][0:1, q, 0:1], min_val=0, max_val=NT - 1) for q in range(QT)]
                    pe.wait_ge(s_et, o * QB + b + 1)
                    pe.matmul(pre[b][:, :], eT[b][:, :], wd[:, :, :], start=True, stop=False, skip_group_check=True)
                    pe.wait_ge(s_gt, o * QB + b + 1)
                    for q in range(QT):
                        for part in range(3):
                            last = pe.matmul(pre[b][:, q * F:q * F + F], GT[b][:, q * P:q * P + P],
                                             t["A3"][:, ds(of[q], 1), part, :].rearrange("p a f -> p (a f)"),
                                             start=False, stop=(part == 2), skip_group_check=True)
                    last.then_inc(s_pre, 1)
                for b in range(QB):
                    pe.wait_ge(s_msg, o * QB + b + 1)
                    pe.wait_ge(s_s, (o + 1) * QB + b + 1)
                    for q in range(QT):
                        last = pe.matmul(acc[b][:, q * (F + 1):(q + 1) * (F + 1)], S[b][:, q, :], msg[b][:, q, :], start=True, stop=True)
                    last.then_inc(s_acc, 1)


def nodes(nc, t):
    with ExitStack() as ctx:
        sb = lambda n, s, d=F32: ctx.enter_context(nc.sbuf_tensor(n, s, d))
        pb = lambda n, s, d=F32: ctx.enter_context(nc.psum_tensor(n, s, d))
        sem = lambda n: ctx.enter_context(nc.semaphore(n))
        sq = sb("sq2", [P, NT, F])
        y = sb("y", [P, NT, F])
        st = sb("st2", [P, 3, NT])
        deg = sb("degree", [P, NT])
        mT = sb("sums_turned", [F + 1, 2, QT * P])
        hT = sb("h_turned2", [F, 2, QT * P])
        rest = sb("rest2", [P, 2, 2, 3 * F])
        ptr = [pb(f"turned2_{i}", [P, QT * P]) for i in range(2)]
        pm = [pb(f"times_w2_{i}", [P, QT * F]) for i in range(2)]
        pq = [pb(f"qkv_sum{i}", [P, 2 * 3 * F]) for i in range(2)]
        s_v, s_tr, s_mT, s_pm, s_y, s_h, s_sqrt, s_tr2, s_hT, s_pq, s_hi, s_rest, s_mid, s_q = (sem(n) for n in (
            "v", "sums_turned", "sums_copied", "times_w2", "y_ready", "h_ready", "rooted", "h_turned", "h_copied", "qkv_up", "qkv_hi",
            "qkv_rest", "qkv_mid", "qkv_done"))
        block = ctx.enter_context(nc.Block())
        GB = -(-NT // QT)
        GQ = -(-NT // 2)

        @block.tensor
        def _(pe):
            for g in range(GB + 1):
                if g < GB:
                    m = min(QT, NT - QT * g)
                    if g >= 2:
                        pe.wait_ge(s_mT, g - 1)
                    for k in range(m):
                        last = pe.transpose(ptr[g % 2][0:F + 1, k * P:k * P + P], t["sum"][:, QT * g + k + 1, :], t["idf"][:, :])
                    last.then_inc(s_tr, 1)
                if g >= 1:
                    q = g - 1
                    m = min(QT, NT - QT * q)
                    pe.wait_ge(s_mT, q + 1)
                    if q >= 2:
                        pe.wait_ge(s_y, q - 1)
                    for k in range(m):
                        last = pe.matmul(pm[q % 2][:, k * F:k * F + F], mT[:, q % 2, k * P:k * P + P], t["w2"][:, :], start=True, stop=True)
                    last.then_inc(s_pm, 1)
            pe.wait_ge(s_h, 9)
            for g in range(GQ + 1):
                if g < GQ:
                    m = min(2, NT - 2 * g)
                    if g >= 2:
                        pe.wait_ge(s_hT, g - 1)
                    for k in range(m):
                        last = pe.transpose(ptr[g % 2][0:F, k * P:k * P + P], t["h"][:, 2 * g + k, :], t["idf"][:, :])
                    last.then_inc(s_tr2, 1)
                if g >= 1:
                    q = g - 1
                    m = min(2, NT - 2 * q)
                    pe.wait_ge(s_hT, q + 1)
                    if q >= 2:
                        pe.wait_ge(s_rest, q - 1)
                    for k in range(m):
                        last = pe.matmul(pq[q % 2][:, k * 3 * F:(k + 1) * 3 * F], hT[:, q % 2, k * P:k * P + P], t["wqkv"][:, :], start=True, stop=True)
                    last.then_inc(s_pq, 1)

        @block.scalar
        def _(act):
            for g in range(GB):
                n = min(QT, NT - QT * g)
                act.wait_ge(s_tr, g + 1)
                if g >= 2:
                    act.wait_ge(s_pm, g - 1)
                act.copy(mT[:, g % 2, 0:n * P], ptr[g % 2][0:F + 1, 0:n * P]).then_inc(s_mT, 1)
            for r in range(2):
                act.wait_ge(s_h, 4 * (r + 1))
                act.activation(st[:, 2, :], st[:, 1, :], ACT.Sqrt, bias=t["eps"][:, 0:1], scale=1.0 / F).then_inc(s_sqrt, 1)
            for g in range(GQ + 2):
                if g < GQ:
                    n = min(2, NT - 2 * g)
                    act.wait_ge(s_tr2, g + 1)
                    if g >= 2:
                        act.wait_ge(s_pq, g - 1)
                    act.copy(hT[:, g % 2, 0:n * P], ptr[g % 2][0:F, 0:n * P]).then_inc(s_hT, 1)
                if 1 <= g <= GQ:
                    q = g - 1
                    n = min(2, NT - 2 * q)
                    act.wait_ge(s_pq, q + 1)
                    act.copy(t["qkv"][:, 2 * q:2 * q + n, 0, :], pq[q % 2][:, 0:n * 3 * F].rearrange("p (t f) -> p t f", t=n)).then_inc(s_hi, 1)
                if g >= 2:
                    q = g - 2
                    n = min(2, NT - 2 * q)
                    act.wait_ge(s_rest, q + 1)
                    act.copy(t["qkv"][:, 2 * q:2 * q + n, 1, :], rest[:, q % 2, 0:n, :]).then_inc(s_mid, 1)

        @block.gpsimd
        def _(pool):
            pool.memset(t["qkv"][:, NT, :, :], 0.0)

        @block.vector
        def _(v):
            n = [0]

            def link(ins):
                n[0] += 1
                ins.then_inc(s_v, 1)
                v.wait_ge(s_v, n[0])

            b = lambda a: a.rearrange("p (t a) -> p t a", a=1).to_broadcast([P, NT, F])
            w = lambda a: a.rearrange("p (a f) -> p a f", a=1).to_broadcast([P, NT, F])
            link(v.tensor_scalar(deg[:, :], t["sum"][:, 1:NT + 1, F], 1.0, None, ALU.max))
            link(v.reciprocal(deg[:, :], deg[:, :]))
            for g in range(GB):
                m = min(QT, NT - QT * g)
                at = slice(QT * g, QT * g + m)
                v.wait_ge(s_pm, g + 1)
                v.tensor_tensor(y[:, at, :], pm[g % 2][:, 0:m * F].rearrange("p (t f) -> p t f", f=F),
                                deg[:, at].rearrange("p (t a) -> p t a", a=1).to_broadcast([P, m, F]), ALU.mult).then_inc(s_y, 1)
            v.wait_ge(s_y, GB)
            link(v.tensor_tensor(y[:, :, :], y[:, :, :], t["h"][:, 0:NT, :], ALU.add))
            layer_norm(v, link, y, y, sq, st, s_h, s_sqrt, 1)
            link(v.tensor_tensor(y[:, :, :], y[:, :, :], w(t["gb"][:, 0, :]), ALU.mult))
            link(v.tensor_tensor(y[:, :, :], y[:, :, :], w(t["gb"][:, 1, :]), ALU.add))
            link(v.tensor_tensor(t["x"][:, :, :], t["x"][:, :, :], y[:, :, :], ALU.add))
            layer_norm(v, link, t["x"], t["h"], sq, st, s_h, s_sqrt, 2)
            v.tensor_scalar(t["h"][:, 0:NT, :], t["h"][:, 0:NT, :], 0.0, None, ALU.max).then_inc(s_h, 1)
            for g in range(GQ + 1):
                if g < GQ:
                    m = min(2, NT - 2 * g)
                    v.wait_ge(s_hi, g + 1)
                    if g >= 2:
                        v.wait_ge(s_q, g - 1)
                    v.tensor_tensor(rest[:, g % 2, 0:m, :], pq[g % 2][:, 0:m * 3 * F].rearrange("p (t f) -> p t f", t=m),
                                    t["qkv"][:, 2 * g:2 * g + m, 0, :], ALU.subtract).then_inc(s_rest, 1)
                if g >= 1:
                    q = g - 1
                    m = min(2, NT - 2 * q)
                    v.wait_ge(s_mid, q + 1)
                    v.tensor_tensor(t["qkv"][:, 2 * q:2 * q + m, 2, :], rest[:, q % 2, 0:m, :], t["qkv"][:, 2 * q:2 * q + m, 1, :], ALU.subtract).then_inc(s_q, 1)


W = F + HEADS


def layer1(nc, t, binned, out):
    with ExitStack() as ctx:
        sb = lambda n, s, d=F32: ctx.enter_context(nc.sbuf_tensor(n, s, d))
        pb = lambda n, s, d=F32: ctx.enter_context(nc.psum_tensor(n, s, d))
        sem = lambda n: ctx.enter_context(nc.semaphore(n))
        wide = (QT, QT, 1)
        GTs = [sb(f"gather_src{n}", [P, w * P], BF16) for n, w in enumerate(wide)]
        GTd = [sb(f"gather_dst{n}", [P, w * P], BF16) for n, w in enumerate(wide)]
        away = [sb(f"away{n}", [P, w * P]) for n, w in enumerate(wide)]
        S = [sb(f"scatter1_{n}", [P, w, P]) for n, w in enumerate(wide)]
        qs = [sb(f"queries{n}", [P, w, F]) for n, w in enumerate(wide)]
        prod = [sb(f"products{n}", [P, w, F]) for n, w in enumerate(wide)]
        att = [sb(f"scores{n}", [P, w, HEADS]) for n, w in enumerate(wide)]
        msg = [sb(f"messages1_{n}", [P, w, W]) for n, w in enumerate(wide)]
        idf = sb("src_places", [P, NT * NT + 1])
        minus = sb("minus_part", [P, 1])
        row = sb("row_places", [P, NT])
        pis, pid = pb("src_places_up", [P, QT * P]), pb("dst_places_up", [P, QT * P])
        pq = [pb(f"q_up{n}", [P, QT * F]) for n in range(2)]
        pkv = [pb(f"kv_up{n}", [P, w * 2 * F]) for n, w in enumerate(wide)]
        acc = pb("sums1", [P, W])
        names = ("constants", "src_up", "dst_up", "src_gather", "away_ready", "dst_gather", "scatter_part", "scatter_ready", "q_up", "kv_up",
                 "q_ready", "products_ready", "scores_ready", "clipped", "exp_ready", "messages_ready", "group_added", "row_kept")
        s_c, s_is, s_id, s_gs, s_aw, s_gd, s_sp, s_s, s_pq, s_kv, s_q, s_pr, s_sc, s_cl, s_ex, s_msg, s_acc, s_out = (sem(n) for n in names)
        block = ctx.enter_context(nc.Block())
        POOLED = 3

        @block.gpsimd
        def _(pool):
            pool.wait_ge(s_c, 1)
            with pool.Fori(0, NT) as i:
                pool.wait_ge(s_sp, i * (LAST_K + 1) + 1)
                apart(pool, t)
                pool.tensor_copy(row[:, :], idf[:, 0:NT * NT].rearrange("p (j i) -> p i j", i=NT)[:, ds(i, 1), :].rearrange("p a j -> p (a j)")).then_inc(s_sp, 1)
                pool.wait_ge(s_sp, i * (LAST_K + 1) + 2)
                apart(pool, t)
                for k in range(LAST_K):
                    q = tiles(k)
                    pool.wait_ge(s_acc, i * LB + CREDIT + before(k) + 1)
                    apart(pool, t)
                    for m, j in enumerate(q[:POOLED]):
                        last = pool.tensor_scalar(S[slot(k)][:, m, :], t["row"][:, :], row[:, j:j + 1], None, ALU.is_equal)
                    last.then_inc(s_sp, 1)

        @block.vector
        def _(v):
            v.tensor_scalar(minus[:, :], t["part"][:, :], -1.0, None, ALU.mult)
            v.tensor_copy(idf[:, :], t["ids"][:, 0, 0:NT * NT + 1]).then_inc(s_c, 1)
            v.wait_ge(s_c, 1)

            def gather(k, n):
                w = len(tiles(k)) * P
                v.wait_ge(s_is, n + 1)
                v.wait_ge(s_kv, n + CREDIT - k + before(k) + 1)
                v.tensor_scalar(GTs[slot(k)][:, 0:w], pis[:, 0:w], t["part"][:, 0:1], None, ALU.is_equal).then_inc(s_gs, 1)

            def scatter(k, i):
                v.wait_ge(s_acc, i * LB + CREDIT + before(k) + 1)
                m = min(POOLED, len(tiles(k)) - 1)
                v.tensor_scalar(S[slot(k)][:, m, :], t["row"][:, :], idf[:, ds(i + tiles(k)[-1] * NT, 1)], None, ALU.is_equal).then_inc(s_s, 1)

            gather(0, 0)
            gather(1, 1)
            with v.Fori(0, NT) as i:
                for k in range(LB):
                    n = len(tiles(k))
                    g = i * LB + k
                    o = slot(k)
                    kv = pkv[o][:, :].rearrange("p (t f) -> p t f", f=2 * F)
                    heads = lambda a: a.rearrange("p t (h d) -> p t h d", h=HEADS)
                    v.wait_ge(s_q, g + CREDIT + 1)
                    v.wait_ge(s_kv, g + CREDIT + 1)
                    v.tensor_tensor(prod[o][:, :, :], qs[o][:, :, :], kv[:, :, 0:F], ALU.mult).then_inc(s_pr, 1)
                    gather((k + 2) % LB, g + 2)
                    v.wait_ge(s_pr, g + 1)
                    v.tensor_reduce(att[o][:, :, :], heads(prod[o][:, :, :]), AX.X, ALU.add).then_inc(s_sc, 1)
                    scatter(k, i)
                    v.wait_ge(s_sc, g + 1)
                    v.tensor_scalar(att[o][:, :, :], att[o][:, :, :], 10.0, -10.0, ALU.min, ALU.max).then_inc(s_cl, 1)
                    v.wait_ge(s_ex, g + 1)
                    v.tensor_tensor(heads(msg[o][:, :, 0:F]), heads(kv[:, :, F:2 * F]),
                                    msg[o][:, :, F:W].rearrange("p t (h a) -> p t h a", a=1).to_broadcast([P, n, HEADS, HD]), ALU.mult).then_inc(s_msg, 1)
                v.wait_ge(s_acc, (i + 1) * LB + CREDIT)
                v.tensor_copy(t["out"][:, ds(i, 1), :].rearrange("p a f -> p (a f)"), acc[:, :]).then_inc(s_out, 1)

        @block.scalar
        def _(act):
            def gather(k, n):
                w = len(tiles(k)) * P
                act.wait_ge(s_id, n + 1)
                act.activation(away[slot(k)][:, 0:w], pid[:, 0:w], ACT.Abs, bias=minus[:, 0:1]).then_inc(s_aw, 1)
                act.wait_ge(s_kv, n + CREDIT - k + before(k) + 1)
                act.wait_ge(s_aw, n + 1)
                act.activation(GTd[slot(k)][:, 0:w], away[slot(k)][:, 0:w], ACT.Relu, bias=1.0, scale=-1.0).then_inc(s_gd, 1)

            act.wait_ge(s_c, 1)
            gather(0, 0)
            gather(1, 1)
            with act.Fori(0, NT) as i:
                for k in range(LB):
                    n = len(tiles(k))
                    o = slot(k)
                    g = i * LB + k
                    act.wait_ge(s_pq, g + 1)
                    act.wait_ge(s_msg, i * LB + CREDIT + before(k) + 1)
                    act.copy(qs[o][:, :, :], pq[k % 2][:, 0:n * F].rearrange("p (t f) -> p t f", f=F)).then_inc(s_q, 1)
                    gather((k + 2) % LB, g + 2)
                    act.wait_ge(s_cl, g + 1)
                    act.wait_ge(s_acc, i * LB + CREDIT + before(k) + 1)
                    act.activation(msg[o][:, :, F:W], att[o][:, :, :], ACT.Exp).then_inc(s_ex, 1)

        @block.tensor
        def _(pe):
            def ids_up(k, n, i):
                w = len(tiles(k)) * P
                for side, bank, made, up in ((0, pis, s_gs, s_is), (1, pid, s_aw, s_id)):
                    if not isinstance(n, int) or n:
                        pe.wait_ge(made, n)
                    for m, j in enumerate(tiles(k)):
                        last = pe.matmul(bank[:, m * P:m * P + P], col(t["ids"][:, side, ds(i + j * NT, 1)], P), t["idb"][:, :], start=True, stop=True)
                    last.then_inc(up, 1)

            def gathered(k, g, i):
                n = len(tiles(k))
                pe.wait_ge(s_gs, g + 1)
                pe.wait_ge(s_q, g - k + CREDIT + bank_before(k) + 1)
                for m in range(n):
                    for part in range(3):
                        last = pe.matmul(pq[k % 2][:, m * F:m * F + F], GTs[slot(k)][:, m * P:m * P + P],
                                         t["qkv"][:, ds(i, 1), part, 0:F].rearrange("p a f -> p (a f)"), start=(part == 0), stop=(part == 2))
                last.then_inc(s_pq, 1)
                pe.wait_ge(s_gd, g + 1)
                pe.wait_ge(s_msg, g - k + CREDIT + before(k) + 1)
                for m, j in enumerate(tiles(k)):
                    for part in range(3):
                        last = pe.matmul(pkv[slot(k)][:, m * 2 * F:(m + 1) * 2 * F], GTd[slot(k)][:, m * P:m * P + P], t["qkv"][:, j, part, F:3 * F],
                                         start=(part == 0), stop=(part == 2))
                last.then_inc(s_kv, 1)

            def add(k, i):
                g = i * LB + k
                pe.wait_ge(s_msg, g + CREDIT + 1)
                pe.wait_ge(s_s, g + 1)
                if k != LAST_K:
                    pe.wait_ge(s_sp, i * (LAST_K + 1) + k + 3)
                if k == 0:
                    pe.wait_ge(s_out, i + 1)
                for m, j in enumerate(tiles(k)):
                    last = pe.matmul(acc[:, :], S[slot(k)][:, m, :], msg[slot(k)][:, m, :], start=(j == 0), stop=(j == NT - 1), skip_group_check=True)
                last.then_inc(s_acc, 1)

            for s in (s_kv, s_q, s_msg, s_acc):
                pe.sem_inc(s, CREDIT)
            pe.sem_inc(s_out, 1)
            pe.sem_inc(s_sp, 1)
            pe.wait_ge(s_c, 1)
            ids_up(0, 0, 0)
            ids_up(1, 1, 0)
            gathered(0, 0, 0)
            with pe.Fori(0, NT) as i:
                for k in range(LB):
                    k1, k2 = (k + 1) % LB, (k + 2) % LB
                    g = i * LB + k
                    ids_up(k2, g + 2, i if k2 == k + 2 else i + 1)
                    gathered(k1, g + 1, i if k1 else i + 1)
                    if k:
                        add(k - 1, i)
                add(LAST_K, i)

    beyond1(nc, t, binned)
    finish(nc, t, out)


def beyond1(nc, t, binned):
    with ExitStack() as ctx:
        sb = lambda n, s, d=F32: [ctx.enter_context(nc.sbuf_tensor(f"beyond1_{n}{b}", s, d)) for b in range(QB)]
        pb = lambda n, w, k=QB: [ctx.enter_context(nc.psum_tensor(f"beyond1_{n}{b}", [P, w], F32)) for b in range(k)]
        sem = lambda n: ctx.enter_context(nc.semaphore(n))
        rec = sb("records", [P, QT, 4])
        ids = sb("places", [P, 2, QT], BF16)
        at = sb("tiles", [1, QT, 2], I32)
        GT = sb("gather", [P, 2, QT * P], BF16)
        S = sb("scatter", [P, QT, P])
        qs = sb("queries", [P, QT, F])
        prod = sb("products", [P, QT, F])
        att = sb("scores", [P, QT, HEADS])
        msg = sb("messages", [P, QT, W])
        (pis, pid), pq, pkv, acc = pb("places_up", QT * P), pb("q_up", QT * F), pb("kv_up", QT * 2 * F), pb("sums", QT * W)
        s_ld = [sem(f"beyond1_in{b}") for b in range(QB)]
        names = ("ids_ready1", "tiles_known1", "places_up1", "gathers_ready", "scatter_ready1", "q_up1", "kv_up1", "q_ready1",
                 "products_ready1", "scores_ready1", "clipped1", "exp_ready1", "messages_ready1", "group_added1", "group_kept1")
        s_ids, s_at, s_up, s_gt, s_s, s_pq, s_kv, s_q, s_pr, s_sc, s_cl, s_ex, s_msg, s_acc, s_out = (sem(n) for n in names)
        block = ctx.enter_context(nc.Block())
        heads = lambda a: a.rearrange("p t (h d) -> p t h d", h=HEADS)

        @block.sync
        def _(sp):
            with sp.Fori(0, steps_beyond(sp, t)) as o:
                for b in range(QB):
                    sp.wait_ge(s_s, o * QB + b + 1)
                    apart(sp, t)
                    sp.dma_start(rec[b][:, :, :], beyond_rows(binned, o, b, slice(FE, REC))).then_inc(s_ld[b], 16)

        @block.vector
        def _(v):
            with v.Fori(0, steps_beyond(v, t)) as o:
                for b in range(QB):
                    v.wait_ge(s_ld[b], (o + 1) * 16)
                    v.tensor_copy(ids[b][:, :, :], rec[b][:, :, 0:2].rearrange("p t c -> p c t")).then_inc(s_ids, 1)
                    v.tensor_scalar(at[b][:, :, :], rec[b][0:1, :, 2:4], 0.0, None, ALU.max).then_inc(s_at, 1)
                    v.tensor_tensor(S[b][:, :, :], t["row"][:, :].rearrange("p (a n) -> p a n", a=1).to_broadcast([P, QT, P]),
                                    rec[b][:, :, 0:1].to_broadcast([P, QT, P]), ALU.is_equal).then_inc(s_s, 1)
                to = []
                for b in range(QB):
                    v.wait_ge(s_up, o * QB + b + 1)
                    v.tensor_scalar(GT[b][:, 0, :], pis[:, :], t["part"][:, 0:1], None, ALU.is_equal)
                    v.tensor_scalar(GT[b][:, 1, :], pid[:, :], t["part"][:, 0:1], None, ALU.is_equal).then_inc(s_gt, 1)
                    v.wait_ge(s_at, o * QB + b + 1)
                    apart(v, t)
                    to.append([v.value_load(at[b][0:1, q, 0:1], min_val=0, max_val=NT - 1) for q in range(QT)])
                for b in range(QB):
                    g = o * QB + b
                    kv = pkv[b][:, :].rearrange("p (t f) -> p t f", f=2 * F)
                    v.wait_ge(s_q, g + 1)
                    v.wait_ge(s_kv, g + 1)
                    v.tensor_tensor(prod[b][:, :, :], qs[b][:, :, :], kv[:, :, 0:F], ALU.mult).then_inc(s_pr, 1)
                    v.wait_ge(s_pr, g + 1)
                    v.tensor_reduce(att[b][:, :, :], heads(prod[b][:, :, :]), AX.X, ALU.add).then_inc(s_sc, 1)
                    v.wait_ge(s_sc, g + 1)
                    v.tensor_scalar(att[b][:, :, :], att[b][:, :, :], 10.0, -10.0, ALU.min, ALU.max).then_inc(s_cl, 1)
                    v.wait_ge(s_ex, g + 1)
                    v.tensor_tensor(heads(msg[b][:, :, 0:F]), heads(kv[:, :, F:2 * F]),
                                    msg[b][:, :, F:W].rearrange("p t (h a) -> p t h a", a=1).to_broadcast([P, QT, HEADS, HD]), ALU.mult).then_inc(s_msg, 1)
                for b in range(QB):
                    v.wait_ge(s_acc, o * QB + b + 1)
                    for q in range(QT):
                        row = t["out"][:, ds(to[b][q], 1), :].rearrange("p a f -> p (a f)")
                        v.wait_ge(s_out, (o * QB + b) * QT + q + 1)
                        v.tensor_tensor(row, row, acc[b][:, q * W:(q + 1) * W], ALU.add).then_inc(s_out, 1)

        @block.scalar
        def _(act):
            with act.Fori(0, steps_beyond(act, t)) as o:
                for b in range(QB):
                    act.wait_ge(s_pq, o * QB + b + 1)
                    act.copy(qs[b][:, :, :], pq[b][:, :].rearrange("p (t f) -> p t f", f=F)).then_inc(s_q, 1)
                    act.wait_ge(s_cl, o * QB + b + 1)
                    act.activation(msg[b][:, :, F:W], att[b][:, :, :], ACT.Exp).then_inc(s_ex, 1)

        @block.tensor
        def _(pe):
            def places(b, o):
                pe.wait_ge(s_ids, o * QB + b + 1)
                for side, bank in ((0, pis), (1, pid)):
                    for q in range(QT):
                        last = pe.matmul(bank[:, q * P:q * P + P], col(ids[b][:, side, q:q + 1], P), t["idb"][:, :], start=True, stop=True)
                last.then_inc(s_up, 1)

            def known(b, o):
                pe.wait_ge(s_at, o * QB + b + 1)
                apart(pe, t)
                return [[pe.value_load(at[b][0:1, q, s:s + 1], min_val=0, max_val=NT - 1) for q in range(QT)] for s in range(2)]

            def gathered(b, o, tile):
                pe.wait_ge(s_gt, o * QB + b + 1)
                for side, bank, first, end, up in ((0, pq[b], 0, F, s_pq), (1, pkv[b], F, 3 * F, s_kv)):
                    for q in range(QT):
                        for part in range(3):
                            last = pe.matmul(bank[:, q * (end - first):(q + 1) * (end - first)], GT[b][:, side, q * P:q * P + P],
                                             t["qkv"][:, ds(tile[side][q], 1), part, first:end].rearrange("p a f -> p (a f)"),
                                             start=(part == 0), stop=(part == 2))
                    last.then_inc(up, 1)

            pe.sem_inc(s_out, 1)
            pe.sem_inc(s_s, QB)
            with pe.Fori(0, steps_beyond(pe, t)) as o:
                places(0, o)
                tile = known(0, o)
                pe.wait_ge(s_gt, o * QB + 1)
                places(1, o)
                gathered(0, o, tile)
                tile = known(1, o)
                gathered(1, o, tile)
                for b in range(QB):
                    pe.wait_ge(s_msg, o * QB + b + 1)
                    pe.wait_ge(s_s, (o + 1) * QB + b + 1)
                    for q in range(QT):
                        last = pe.matmul(acc[b][:, q * W:(q + 1) * W], S[b][:, q, :], msg[b][:, q, :], start=True, stop=True)
                    last.then_inc(s_acc, 1)


def finish(nc, t, out):
    with ExitStack() as ctx:
        den = ctx.enter_context(nc.sbuf_tensor("denominators", [P, NT, HEADS], F32))
        s_v, s_o = (ctx.enter_context(nc.semaphore(n)) for n in ("v_out", "written"))
        block = ctx.enter_context(nc.Block())

        @block.vector
        def _(v):
            n = [0]

            def link(ins):
                n[0] += 1
                ins.then_inc(s_v, 1)
                v.wait_ge(s_v, n[0])

            link(v.tensor_scalar(den[:, :, :], t["out"][:, :, F:W], 1e-8, None, ALU.add))
            link(v.reciprocal(den[:, :, :], den[:, :, :]))
            for h in range(HEADS):
                a = t["out"][:, :, h * HD:(h + 1) * HD]
                last = v.tensor_tensor(a, a, den[:, :, h:h + 1].to_broadcast([P, NT, HD]), ALU.mult)
            link(last)
            v.tensor_tensor(t["x"][:, :, :], t["x"][:, :, :], t["out"][:, :, 0:F], ALU.add).then_inc(s_v, 1)

        @block.sync
        def _(sp):
            sp.wait_ge(s_v, 4)
            sp.dma_start(out[0:(NT - 1) * P, :].rearrange("(t p) f -> p t f", p=P), t["x"][:, 0:NT - 1, :]).then_inc(s_o, 16)
            sp.dma_start(out[(NT - 1) * P:N_NODES, :], t["x"][0:LAST, NT - 1, :]).then_inc(s_o, 16)
            sp.wait_ge(s_o, 32)


def kernel(x, src, dst, edge_attr_32, L0_gnn_W1, L0_gnn_b1, L0_gnn_W2, L0_gnn_b2, L0_gnn_gamma, L0_gnn_beta,
           L1_gnn_qTrans, L1_gnn_kTrans, L1_gnn_vTrans):
    import numpy as np
    import concourse.bacc as bacc
    from concourse.bass_utils import run_bass_kernel_spmd

    pad = ET * P - N_EDGES
    across = lambda a: np.ascontiguousarray(a.reshape(ET, P, *a.shape[1:]).swapaxes(0, 1))

    def node_ids(a):
        a = np.asarray(a)
        return across(np.concatenate([a, np.full(pad, NT * P, a.dtype)]))

    arrays = {
        "x_in": np.asarray(x), "src": node_ids(src), "dst": node_ids(dst),
        "edge": across(np.concatenate([np.asarray(edge_attr_32), np.zeros((pad, FE), np.float32)])),
        "w1": np.asarray(L0_gnn_W1), "b1": np.asarray(L0_gnn_b1), "w2": np.asarray(L0_gnn_W2), "b2": np.asarray(L0_gnn_b2),
        "gamma": np.asarray(L0_gnn_gamma), "beta": np.asarray(L0_gnn_beta),
        "wq": np.asarray(L1_gnn_qTrans), "wk": np.asarray(L1_gnn_kTrans), "wv": np.asarray(L1_gnn_vTrans),
    }
    nc = bacc.Bacc("TRN2", target_bir_lowering=False, num_devices=1)
    args = [nc.dram_tensor(n, a.shape, mybir.dt.from_np(a.dtype), kind="ExternalInput").ap() for n, a in arrays.items()]
    out = nc.dram_tensor("out", (N_NODES, F), F32, kind="ExternalOutput").ap()
    gnn(nc, *args, out)
    r = run_bass_kernel_spmd(nc, [arrays], core_ids=[0])
    return r.results[0]["out"]
```

```python
from contextlib import ExitStack

import concourse.bass as bass
from concourse import mybir

F32 = mybir.dt.float32
BF16 = mybir.dt.bfloat16
I32 = mybir.dt.int32
ALU = mybir.AluOpType
ACT = mybir.ActivationFunctionType
AX = mybir.AxisListType
ds = bass.ds

P = 128
N_NODES = 6250
N_EDGES = 206250
F = 64
FE = 32
HEADS = 4
HD = F // HEADS
NT = -(-N_NODES // P)
LAST = N_NODES - (NT - 1) * P
NG = NT + 1
SI = 64

QT = 4
BODY = 13
ET = -(-N_EDGES // P)
GROUPS = ET // QT
BODIES = GROUPS // BODY
assert GROUPS * QT == ET and BODIES * BODY == GROUPS
EP = ET + 2 * QT
CHUNKS = [(0, 3), (3, 6), (6, 9), (9, 13)]

REC = FE + 4
MAIN = NG * P * SI
QB = 2
STEP = QB * QT
EO = -(-ET // STEP) * STEP
ROWS = MAIN + EO * P
LN_EPS = 1e-5
NA = -(-NT // QT)
HB = 31
HU = 4
assert NA * HU * HB == ET
BY_POOL = 7


def col(ap, n):
    return ap.to_broadcast([P, n])


def apart(eng, t):
    eng.sem_inc(t["passed"], 1)


def gnn(nc, x, src, dst, edge, w1, b1, w2, b2, gamma, beta, wq, wk, wv, out):
    binned = nc.dram_tensor("binned", [ROWS, REC], F32).ap()
    with ExitStack() as keep:
        def sb(name, shape, dt=F32, at=keep):
            return at.enter_context(nc.sbuf_tensor(name, shape, dt))

        t = {"passed": keep.enter_context(nc.semaphore("passed"))}
        t["x"] = sb("x_nodes", [P, NT, F])
        t["h"] = sb("h_nodes", [P, NA * QT, F])
        t["row"] = sb("iota_row", [P, P])
        t["rowb"] = sb("iota_rowb", [P, P], BF16)
        t["part"] = sb("iota_part", [P, 1])
        t["idf"] = sb("identity_f32", [P, P])
        t["idb"] = sb("identity_bf16", [P, P], BF16)
        t["w1a"] = sb("w1a_b1", [F + 1, F])
        t["w1b"] = sb("w1b", [P, F])
        t["w2"] = sb("w2_b2", [F + 1, F])
        t["wqkv"] = sb("wqkv", [F, 3 * F])
        t["gb"] = sb("gamma_beta", [P, 2, F])
        t["eps"] = sb("eps", [P, 1])
        t["nover"] = sb("steps_over", [1, 1], I32)
        t["A3"] = sb("a_parts", [P, NA * QT, 3, F], BF16)
        with ExitStack() as ctx:
            t["hs"] = sb("src_tile", [P, EP], BF16, ctx)
            t["hd"] = sb("dst_tile", [P, EP], BF16, ctx)
            t["bin"] = sb("bin", [P, EP], F32, ctx)
            t["base"] = sb("bin_base", [P, ET], F32, ctx)
            t["meta"] = sb("meta", [P, ET, 4], F32, ctx)
            t["RD"] = sb("counts_over", [NG, 2, 2 * NG], F32, ctx)
            prepare(nc, t, x, src, dst, w1, b1, w2, b2, gamma, beta, wq, wk, wv, binned)
            place(nc, t, edge, binned)
        t["sum"] = sb("node_sums", [P, NT + 1, F + 1])
        t["ids"] = sb("places", [P, 2, NG * NT], BF16)
        layer0(nc, t, binned)
        t["qkv"] = sb("qkv_parts", [P, NG, 3, 3 * F], BF16)
        nodes(nc, t)
        t["out"] = sb("attention_sums", [P, NT + 1, F + HEADS])
        layer1(nc, t, binned)
        finish(nc, t, out)


def prepare(nc, t, x, src, dst, w1, b1, w2, b2, gamma, beta, wq, wk, wv, binned):
    with ExitStack() as ctx:
        sb = lambda n, s, d=F32: ctx.enter_context(nc.sbuf_tensor(n, s, d))
        pb = lambda n, s, d=F32: ctx.enter_context(nc.psum_tensor(n, s, d))
        sem = lambda n: ctx.enter_context(nc.semaphore(n))
        fill = sb("fill", [P, NT * REC])
        ids = sb("ids", [P, 2, ET], I32)
        hi = sb("hi", [P, 2, ET], I32)
        lo = sb("lo", [P, 2, ET], I32)
        OH = sb("tile_onehots", [P, 2, 2, HB, NG], BF16)
        hdf = sb("dst_tiles", [P, HU * HB])
        hist = pb("hist", [NG, NG])
        pref = pb("pref", [NG, 1])
        tot = pb("tot", [1, 1])
        tr = pb("h_turned", [F, QT * P])
        pa = pb("a_sum", [P, QT * F])
        close = sb("h_group", [P, QT, F])
        hT = sb("hT", [F + 1, QT * P])
        ni = sb("ni", [NG, NG], I32)
        nf = sb("nf", [NG, NG])
        n0 = sb("n0", [NG, NG])
        z = sb("zeros", [NG, NG])
        inc = sb("inc", [NG, NG])
        upper = sb("upper", [NG, NG])
        ones = sb("ones", [NG, 1])
        prefs = sb("prefs", [NG, 1])
        sq = sb("sq", [P, NT, F])
        st = sb("st", [P, 3, NT])
        rest = sb("rest", [P, QT * F])
        s_fillset, s_fill, s_ids, s_x, s_w = (sem(n) for n in ("fill_set", "filled", "ids_in", "x_in", "weights_in"))
        s_iota, s_v, s_c, s_oh, s_hist, s_tab, s_t = (sem(n) for n in ("iotas", "v", "constants", "onehots", "counted", "table", "tab"))
        s_sqrt, s_h, s_tr, s_hT, s_pa, s_hi, s_rest, s_mid, s_a = (sem(n) for n in ("rooted", "h_ready", "turned", "hT_ready", "a_summed", "a_hi", "a_rest", "a_mid", "a_done"))
        s_xz, s_close, s_steps = (sem(n) for n in ("x_zeroed", "h_drawn", "steps_known"))
        s_over, s_lo, s_meta, s_hs, s_ohp, s_hd = (sem(n) for n in (
            "filled_beyond", "tiles_and_places", "meta_ready", "tiles_ready", "onehots_by_pool", "dst_tiles_ready"))
        block = ctx.enter_context(nc.Block())

        @block.sync
        def _(sp):
            sp.dma_start(ids[:, 0, :], src).then_inc(s_ids, 16)
            sp.dma_start(ids[:, 1, :], dst).then_inc(s_ids, 16)
            sp.wait_ge(s_xz, 1)
            sp.dma_start(t["x"][:, 0:NT - 1, :], x[0:(NT - 1) * P, :].rearrange("(t p) f -> p t f", p=P)).then_inc(s_x, 16)
            sp.dma_start(t["x"][0:LAST, NT - 1, :], x[(NT - 1) * P:N_NODES, :]).then_inc(s_x, 16)
            sp.wait_ge(s_fillset, 1)
            for j in range(NG):
                sp.dma_start(binned[j * P * SI:(j + 1) * P * SI, :].rearrange("(p i) w -> p (i w)", i=SI)[:, 0:NT * REC],
                             fill[:, :]).then_inc(s_fill, 16)
            sp.wait_ge(s_fill, 16 * NG)
            sp.wait_ge(s_steps, 1)
            apart(sp, t)
            steps = steps_beyond(sp, t)
            with sp.Fori(0, steps) as o:
                sp.dma_start(binned[ds(o * (STEP * P) + MAIN, STEP * P), :].rearrange("(p i) w -> p (i w)", p=P),
                             fill[:, 0:STEP * REC]).then_inc(s_over, 16)
            sp.wait_ge(s_over, steps * 16)
            apart(sp, t)

        @block.scalar
        def _(act):
            one = lambda v: v.rearrange("(a f) -> a f", a=1)
            act.dma_start(t["w1a"][0:F, :], w1[0:F, :]).then_inc(s_w, 16)
            act.dma_start(t["w1a"][F:F + 1, :], one(b1)).then_inc(s_w, 16)
            for k in range(4):
                act.dma_start(t["w1b"][FE * k:FE * k + FE, :], w1[F:F + FE, :]).then_inc(s_w, 16)
            act.dma_start(t["w2"][0:F, :], w2).then_inc(s_w, 16)
            act.dma_start(t["w2"][F:F + 1, :], one(b2)).then_inc(s_w, 16)
            for k, w in enumerate((wq, wk, wv)):
                act.dma_start(t["wqkv"][:, F * k:F * k + F], w).then_inc(s_w, 16)
            act.dma_start(t["gb"][:, 0, :], one(gamma).to_broadcast([P, F])).then_inc(s_w, 16)
            act.dma_start(t["gb"][:, 1, :], one(beta).to_broadcast([P, F])).then_inc(s_w, 16)
            act.wait_ge(s_lo, 1)
            for k, a in enumerate((hi[:, 0, :], hi[:, 1, :], lo[:, 0, :], lo[:, 1, :])):
                last = act.copy(t["meta"][:, :, (k + 2) % 4], a)
            last.then_inc(s_meta, 1)
            act.wait_ge(s_h, 4)
            act.activation(st[:, 2, :], st[:, 1, :], ACT.Sqrt, bias=t["eps"][:, 0:1], scale=1.0 / F).then_inc(s_sqrt, 1)
            act.wait_ge(s_h, 5)
            with act.Fori(0, NA) as g:
                act.wait_ge(s_tr, g + 1)
                act.copy(close[:, :, :], t["h"][:, ds(g * QT, QT), :]).then_inc(s_close, 1)
                act.wait_ge(s_tr, g + 2)
                act.wait_ge(s_pa, g + 1)
                act.copy(hT[0:F, :], tr[:, :]).then_inc(s_hT, 1)
                act.wait_ge(s_pa, g + 2)
                act.copy(t["A3"][:, ds(g * QT, QT), 0, :], pa[:, :].rearrange("p (t f) -> p t f", f=F)).then_inc(s_hi, 1)
                act.wait_ge(s_rest, g + 2)
                act.copy(t["A3"][:, ds(g * QT, QT), 1, :], rest[:, :].rearrange("p (t f) -> p t f", f=F)).then_inc(s_mid, 1)
            act.wait_ge(s_w, 16 * 13)

        @block.gpsimd
        def _(pool):
            pool.memset(t["x"][:, NT - 1, :], 0.0).then_inc(s_xz, 1)
            pool.iota(t["row"][:, :], [[1, P]], base=0, channel_multiplier=0, allow_small_or_imprecise_dtypes=True).then_inc(s_iota, 1)
            pool.iota(t["part"][:, :], [[1, 1]], base=0, channel_multiplier=1, allow_small_or_imprecise_dtypes=True).then_inc(s_iota, 1)
            pool.memset(fill[:, :], -1.0).then_inc(s_fillset, 1)
            pool.memset(t["h"][:, NT:NA * QT, :], 0.0).then_inc(s_iota, 1)
            pool.memset(t["eps"][:, :], LN_EPS).then_inc(s_iota, 1)
            pool.memset(t["hs"][:, ET:EP], float(NT)).then_inc(s_iota, 1)
            pool.memset(t["hd"][:, ET:EP], float(NT)).then_inc(s_iota, 1)
            pool.wait_ge(s_hs, 1)
            apart(pool, t)
            with pool.Fori(0, NA) as g:
                pool.wait_ge(s_ohp, g * HU + 1)
                apart(pool, t)
                pool.tensor_copy(hdf[:, :], t["hd"][:, ds(g * (HU * HB), HU * HB)]).then_inc(s_hd, 1)
                pool.wait_ge(s_hd, g + 1)
                apart(pool, t)
                for b in range(HU):
                    pool.wait_ge(s_hist, g * HU + b + 1)
                    apart(pool, t)
                    for m in range(HB - BY_POOL, HB):
                        last = pool.tensor_scalar(OH[:, b % 2, 1, m, :], t["rowb"][:, 0:NG], hdf[:, b * HB + m:b * HB + m + 1], None, ALU.is_equal)
                    last.then_inc(s_ohp, 1)

        @block.vector
        def _(v):
            n = [0]

            def link(ins):
                n[0] += 1
                ins.then_inc(s_v, 1)
                v.wait_ge(s_v, n[0])

            v.memset(z[:, :], 0.0)
            v.memset(t["bin"][:, ET:EP], 0.0)
            v.memset(ones[:, :], 1.0)
            v.memset(hT[F:F + 1, :], 1.0)
            v.wait_ge(s_iota, 6)
            v.tensor_copy(t["rowb"][:, :], t["row"][:, :])
            v.tensor_scalar(t["idf"][:, :], t["row"][:, :], t["part"][:, 0:1], None, ALU.is_equal)
            v.tensor_scalar(upper[:, :], t["row"][0:NG, 0:NG], t["part"][0:NG, 0:1], None, ALU.is_gt)
            v.tensor_scalar(t["idb"][:, :], t["row"][:, :], t["part"][:, 0:1], None, ALU.is_equal).then_inc(s_c, 1)
            v.wait_ge(s_ids, 32)
            v.tensor_scalar(hi[:, :, :], ids[:, :, :], 7, None, ALU.logical_shift_right)
            v.tensor_scalar(lo[:, :, :], ids[:, :, :], P - 1, None, ALU.bitwise_and).then_inc(s_lo, 1)
            v.wait_ge(s_lo, 1)
            v.tensor_copy(t["hs"][:, 0:ET], hi[:, 0, :])
            v.tensor_copy(t["hd"][:, 0:ET], hi[:, 1, :]).then_inc(s_hs, 1)
            v.wait_ge(s_x, 32)
            layer_norm(v, link, t["x"], t["h"], sq, st, s_h, s_sqrt, 1)
            v.tensor_scalar(t["h"][:, 0:NT, :], t["h"][:, 0:NT, :], 0.0, None, ALU.max).then_inc(s_h, 1)
            v.wait_ge(s_meta, 1)
            v.scalar_tensor_tensor(t["bin"][:, 0:ET], t["meta"][:, :, 3], float(SI), t["meta"][:, :, 2], ALU.mult, ALU.add)
            link(v.tensor_scalar(t["base"][:, :], t["meta"][:, :, 2], 1.0 / SI, None, ALU.mult))
            link(v.scalar_tensor_tensor(t["base"][:, :], t["meta"][:, :, 3], float(P), t["base"][:, :], ALU.mult, ALU.add))
            with v.Fori(0, NA) as g:
                for b in range(HU):
                    v.wait_ge(s_hist, g * HU + b + 1)
                    for k, (a, w) in enumerate(((t["hs"], HB), (t["hd"], HB - BY_POOL))):
                        last = v.tensor_tensor(OH[:, b % 2, k, 0:w, :],
                                               a[:, ds((g * HU + b) * HB, w)].rearrange("p (t a) -> p t a", a=1).to_broadcast([P, w, NG]),
                                               t["rowb"][:, 0:NG].rearrange("p (a n) -> p a n", a=1).to_broadcast([P, w, NG]), ALU.is_equal)
                    last.then_inc(s_oh, 1)
                    if b == 2:
                        v.wait_ge(s_hi, g + 1)
                        v.tensor_tensor(rest[:, :].rearrange("p (t f) -> p t f", f=F), pa[:, :].rearrange("p (t f) -> p t f", f=F),
                                        t["A3"][:, ds(g * QT, QT), 0, :], ALU.subtract).then_inc(s_rest, 1)
                    if b == 3:
                        v.wait_ge(s_mid, g + 1)
                        v.tensor_tensor(t["A3"][:, ds(g * QT, QT), 2, :], rest[:, :].rearrange("p (t f) -> p t f", f=F),
                                        t["A3"][:, ds(g * QT, QT), 1, :], ALU.subtract).then_inc(s_a, 1)
            v.wait_ge(s_hist, NA * HU + 2)
            v.tensor_scalar(n0[:, :], hist[:, :], -1.0, 0.0, ALU.add, ALU.max)
            link(v.tensor_scalar(ni[:, :], hist[:, :], -1.0, 0.0, ALU.add, ALU.max))
            link(v.tensor_scalar(ni[:, :], ni[:, :], 7, None, ALU.logical_shift_right))
            link(v.tensor_copy(nf[:, :], ni[:, :]))
            link(v.tensor_tensor_scan(inc[:, :], nf[:, :], z[:, :], 0.0, ALU.add, ALU.add))
            v.tensor_tensor(n0[:, :], inc[:, :], nf[:, :], ALU.subtract).then_inc(s_tab, 1)
            v.wait_ge(s_t, 1)
            link(v.tensor_copy(prefs[:, :], pref[:, :]))
            link(v.tensor_scalar(n0[:, :], n0[:, :], prefs[:, 0:1], float(P), ALU.add, ALU.mult))
            for b in range(2):
                v.tensor_scalar(t["RD"][:, b, NG:], n0[:, :], float(MAIN - P), None, ALU.add)
                v.memset(t["RD"][:, b, 0:NG], 0.0)
            link(v.tensor_scalar(t["nover"][:, :], tot[:, :], float(STEP - 1), float(STEP), ALU.add, ALU.max))
            v.tensor_scalar(t["nover"][:, :], t["nover"][:, :], 3, None, ALU.logical_shift_right).then_inc(s_steps, 1)

        @block.tensor
        def _(pe):
            pe.wait_ge(s_c, 1)
            pe.matmul(hist[:, :], z[:, :], z[:, :], start=True, stop=False, skip_group_check=True).then_inc(s_hist, 2)
            pe.sem_inc(s_ohp, 1)
            pe.sem_inc(s_tr, 1)
            pe.sem_inc(s_pa, 1)
            pe.sem_inc(s_rest, 1)
            pe.wait_ge(s_w, 16 * 13)
            with pe.Fori(0, NA) as g:
                for b in range(HU):
                    pe.wait_ge(s_oh, g * HU + b + 1)
                    pe.wait_ge(s_ohp, g * HU + b + 2)
                    for k in range(HB):
                        last = pe.matmul(hist[:, :], OH[:, b % 2, 1, k, :], OH[:, b % 2, 0, k, :], start=False, stop=False, skip_group_check=True)
                    last.then_inc(s_hist, 1)
                    if b == 0:
                        pe.wait_ge(s_close, g + 1)
                        apart(pe, t)
                        for k in range(QT):
                            last = pe.transpose(tr[:, k * P:k * P + P], close[:, k, :], t["idf"][:, :])
                        last.then_inc(s_tr, 1)
                    if b == 1:
                        pe.wait_ge(s_hT, g + 1)
                        pe.wait_ge(s_rest, g + 1)
                        for k in range(QT):
                            last = pe.matmul(pa[:, k * F:k * F + F], hT[:, k * P:k * P + P], t["w1a"][:, :], start=True, stop=True)
                        last.then_inc(s_pa, 1)
            pe.wait_ge(s_tab, 1)
            pe.matmul(pref[:, :], upper[:, :], inc[:, NG - 1:NG], start=True, stop=True)
            pe.matmul(tot[:, :], ones[:, :], inc[:, NG - 1:NG], start=True, stop=True).then_inc(s_t, 1)


def layer_norm(v, link, x, y, sq, st, s_h, s_sqrt, roots):
    full = [P, NT, F]
    b = lambda a: a.rearrange("p (t a) -> p t a", a=1).to_broadcast(full)
    link(v.tensor_reduce(st[:, 0, :], x[:, :, :], AX.X, ALU.add))
    link(v.tensor_scalar(st[:, 0, :], st[:, 0, :], 1.0 / F, None, ALU.mult))
    link(v.tensor_tensor(y[:, 0:NT, :], x[:, :, :], b(st[:, 0, :]), ALU.subtract))
    link(v.tensor_tensor(sq[:, :, :], y[:, 0:NT, :], y[:, 0:NT, :], ALU.mult))
    v.tensor_reduce(st[:, 1, :], sq[:, :, :], AX.X, ALU.add).then_inc(s_h, 4)
    v.wait_ge(s_sqrt, roots)
    link(v.reciprocal(st[:, 0, :], st[:, 2, :]))
    link(v.tensor_tensor(y[:, 0:NT, :], y[:, 0:NT, :], b(st[:, 0, :]), ALU.mult))


def place(nc, t, edge, binned):
    with ExitStack() as ctx:
        sb = lambda n, s, d=F32: ctx.enter_context(nc.sbuf_tensor(n, s, d))
        pb = lambda n, s, d=F32: ctx.enter_context(nc.psum_tensor(n, s, d))
        sem = lambda n: ctx.enter_context(nc.semaphore(n))
        rec = sb("records", [P, BODY * QT, REC])
        rows = sb("rows", [P, BODY * QT], I32)
        OHs = sb("src_onehots", [P, BODY, QT, NG], BF16)
        OHd = sb("dst_onehots", [P, BODY, QT, NG], BF16)
        OHdT = sb("dst_onehots_turned", [NG, 2, QT * P])
        mask = sb("earlier", [P, QT * P])
        junk = sb("junk", [P, QT, QT * P], BF16)
        both = sb("both", [P, 2, QT, 2, NG])
        found = sb("found", [P, BODY, QT, 2])
        inside = sb("inside", [P, BODY, QT])
        rank = sb("rank", [P, BODY, QT])
        main = sb("main", [P, BODY, QT])
        over = sb("over", [P, BODY, QT])
        id64 = sb("id64", [P, P], BF16)
        zb = sb("zb", [P, NG], BF16)
        pbin = [pb(f"bins{i}", [P, QT * P]) for i in range(2)]
        ptr = [pb(f"turned{i}", [NG, 2 * QT * P], BF16) for i in range(2)]
        pg = [pb(f"gathered{i}", [P, QT, 2 * NG]) for i in range(2)]
        cnt = pb("counts", [NG, NG])
        s_c, s_oh, s_bin, s_tr, s_trc, s_g, s_cnt, s_rd, s_in, s_v, s_row, s_meta = (sem(n) for n in (
            "constants", "onehots_ready", "bins_ready", "turned_ready", "turned_copied", "gathered_ready", "group_counted",
            "counts_copied", "inside_ready", "v", "rows_ready", "meta_ready"))
        s_edge = [sem(f"edge_in{c}") for c in range(4)]
        s_scat = [sem(f"scattered{c}") for c in range(4)]
        full = [16 * QT * (b - a) for a, b in CHUNKS]
        chunk_of = [c for c, (a, b) in enumerate(CHUNKS) for _ in range(a, b)]
        block = ctx.enter_context(nc.Block())

        @block.sync
        def _(sp):
            for c, (a, b) in enumerate(CHUNKS):
                sp.dma_start(rec[:, a * QT:b * QT, 0:FE], edge[:, a * QT:b * QT, :]).then_inc(s_edge[c], 16)
            with sp.Fori(1, BODIES) as i:
                for c, (a, b) in enumerate(CHUNKS):
                    sp.wait_ge(s_scat[c], i * full[c])
                    sp.dma_start(rec[:, a * QT:b * QT, 0:FE],
                                 edge[:, ds(i * BODY * QT + a * QT, (b - a) * QT), :]).then_inc(s_edge[c], 16)
            for c in range(4):
                sp.wait_ge(s_scat[c], BODIES * full[c])

        @block.scalar
        def _(act):
            act.wait_ge(s_tr, 1)
            act.copy(OHdT[:, 0, :], ptr[0][:, 0:QT * P]).then_inc(s_trc, 1)
            with act.Fori(0, BODIES) as i:
                for k in range(BODY):
                    g = i * BODY + k
                    if k in [a for a, _ in CHUNKS]:
                        c = chunk_of[k]
                        a, b = CHUNKS[c]
                        act.wait_ge(s_edge[c], (i + 1) * 16)
                        act.copy(rec[:, a * QT:b * QT, FE:REC], t["meta"][:, ds((i * BODY + a) * QT, (b - a) * QT), :]).then_inc(s_meta, 1)
                    act.wait_ge(s_cnt, g + 1 + 1)
                    act.wait_ge(s_g, (g if k < BODY - 1 else g + 1) + 1)
                    act.copy(t["RD"][:, (k + 1) % BODY % 2, 0:NG], cnt[:, :]).then_inc(s_rd, 1)
                    act.wait_ge(s_tr, g + 2)
                    act.wait_ge(s_g, (g if k < BODY - 1 else g + 1) + 1)
                    act.copy(OHdT[:, (k + 1) % BODY % 2, :], ptr[(k + 1) % BODY % 2][:, 0:QT * P]).then_inc(s_trc, 1)

        @block.tensor
        def _(pe):
            def turn(k):
                for q in range(QT):
                    last = pe.transpose(ptr[k % 2][:, q * P:q * P + P], OHd[:, k, q, :], t["idb"][:, :])
                last.then_inc(s_tr, 1)

            def bins(k, g):
                for q in range(QT):
                    at = g * QT + q
                    c = pbin[k % 2][:, q * P:q * P + P]
                    pe.matmul(c, col(t["hd"][:, ds(at, 1)], P), id64[:, :], start=True, stop=False)
                    last = pe.matmul(c, col(t["hs"][:, ds(at, 1)], P), t["idb"][:, :], start=False, stop=True)
                last.then_inc(s_bin, 1)

            for s in (s_in, s_trc, s_g, s_rd, s_v, s_cnt):
                pe.sem_inc(s, 1)
            pe.wait_ge(s_c, 1)
            pe.matmul(cnt[:, :], zb[:, :], zb[:, :], start=True, stop=False, skip_group_check=True)
            pe.wait_ge(s_oh, 1)
            turn(0)
            bins(0, 0)
            with pe.Fori(0, BODIES) as i:
                for k in range(BODY):
                    g = i * BODY + k
                    k1 = (k + 1) % BODY
                    pe.wait_ge(s_trc, g + 1 + 1)
                    pe.wait_ge(s_rd, g + 1)
                    pe.wait_ge(s_v, (6 * g if k == 0 else 6 * (g - 1) if k == 1 else 6 * (g - 2) + 1) + 1)
                    for q in range(QT):
                        last = pe.matmul(pg[k % 2][:, q, :], OHdT[:, k % 2, q * P:q * P + P], t["RD"][:, k % 2, :], start=True, stop=True)
                    last.then_inc(s_g, 1)
                    pe.wait_ge(s_rd, g + 1)
                    for q in range(QT):
                        last = pe.matmul(cnt[:, :], OHd[:, k, q, :], OHs[:, k, q, :], start=False, stop=False, skip_group_check=True)
                    last.then_inc(s_cnt, 1)
                    pe.wait_ge(s_oh, g + 2)
                    pe.wait_ge(s_trc, (g if k1 else g + 1) + 1)
                    apart(pe, t)
                    turn(k1)
                    pe.wait_ge(s_in, (g if k1 else g + 1) + 1)
                    bins(k1, g + 1)

        @block.gpsimd
        def _(pool):
            with pool.Fori(0, BODIES) as i:
                for k in range(BODY):
                    g = i * BODY + k
                    c = chunk_of[k]
                    if k == CHUNKS[c][0]:
                        pool.wait_ge(s_edge[c], (i + 1) * 16)
                        pool.wait_ge(s_meta, i * 4 + c + 1)
                    pool.wait_ge(s_row, g + 1)
                    apart(pool, t)
                    for q in range(QT):
                        e = k * QT + q
                        pool.indirect_dma_start(binned, bass.IndirectOffsetOnAxis(rows[:, e:e + 1], 0),
                                                rec[:, e, :], None).then_inc(s_scat[c], 16)

        @block.vector
        def _(v):
            def onehot(o, a, k, g):
                return v.tensor_tensor(o[:, k, :, :], a[:, ds(g * QT, QT)].rearrange("p (t a) -> p t a", a=1).to_broadcast([P, QT, NG]),
                                       t["rowb"][:, 0:NG].rearrange("p (a n) -> p a n", a=1).to_broadcast([P, QT, NG]), ALU.is_equal)

            def compare(k, g, q):
                n = (q + 1) * P
                return v.scalar_tensor_tensor(junk[:, q, 0:n], pbin[k % 2][:, 0:n], t["bin"][:, ds(g * QT + q, 1)], mask[:, (QT - 1 - q) * P:],
                                              ALU.is_equal, ALU.mult, accum_out=inside[:, k, q:q + 1])

            v.tensor_scalar(id64[:, :], t["idf"][:, :], float(SI), None, ALU.mult)
            v.memset(mask[:, 0:(QT - 1) * P], 1.0)
            v.tensor_scalar(mask[:, (QT - 1) * P:], t["row"][:, :], t["part"][:, 0:1], None, ALU.is_lt)
            v.memset(zb[:, :], 0.0).then_inc(s_c, 1)
            v.wait_ge(s_c, 1)
            for g in range(2):
                onehot(OHs, t["hs"], g, g)
                onehot(OHd, t["hd"], g, g).then_inc(s_oh, 1)
            v.wait_ge(s_oh, 2)
            v.wait_ge(s_bin, 1)
            for q in range(QT):
                last = compare(0, 0, q)
            last.then_inc(s_in, 1)
            with v.Fori(0, BODIES) as i:
                for k in range(BODY):
                    g = i * BODY + k
                    s, k1, k2 = k % 2, (k + 1) % BODY, (k + 2) % BODY
                    v.wait_ge(s_g, g + 1 + 1)
                    v.tensor_tensor(both[:, s, :, :, :], pg[s][:, :, :].rearrange("p t (a n) -> p t a n", a=2),
                                    OHs[:, k, :, :].rearrange("p t (a n) -> p t a n", a=1).to_broadcast([P, QT, 2, NG]), ALU.mult).then_inc(s_v, 1)
                    v.wait_ge(s_cnt, g + 1)
                    onehot(OHs, t["hs"], k2, g + 2)
                    v.wait_ge(s_v, g * 6 + 1 + 1)
                    v.tensor_reduce(found[:, k, :, :], both[:, s, :, :, :], AX.X, ALU.add).then_inc(s_v, 1)
                    onehot(OHd, t["hd"], k2, g + 2).then_inc(s_oh, 1)
                    v.wait_ge(s_v, g * 6 + 2 + 1)
                    v.wait_ge(s_in, g + 1 + 1)
                    v.tensor_tensor(rank[:, k, :], inside[:, k, :], found[:, k, :, 0], ALU.add).then_inc(s_v, 1)
                    v.wait_ge(s_bin, g + 2)
                    compare(k1, g + 1, 0)
                    v.wait_ge(s_v, g * 6 + 3 + 1)
                    v.scalar_tensor_tensor(main[:, k, :], rank[:, k, :], float(P - 1), t["base"][:, ds(g * QT, QT)], ALU.min, ALU.add).then_inc(s_v, 1)
                    v.tensor_tensor(over[:, k, :], rank[:, k, :], found[:, k, :, 1], ALU.add).then_inc(s_v, 1)
                    compare(k1, g + 1, 1)
                    v.wait_ge(s_v, g * 6 + 5 + 1)
                    v.scalar_tensor_tensor(over[:, k, :], rank[:, k, :], P - 0.5, over[:, k, :], ALU.is_gt, ALU.mult).then_inc(s_v, 1)
                    compare(k1, g + 1, 2)
                    v.wait_ge(s_v, g * 6 + 6 + 1)
                    c = chunk_of[k]
                    if k == CHUNKS[c][0]:
                        v.wait_ge(s_edge[c], (i + 1) * 16)
                    v.scalar_tensor_tensor(rows[:, k * QT:k * QT + QT], main[:, k, :], float(SI), over[:, k, :],
                                           ALU.mult, ALU.max).then_inc(s_row, 1)
                    compare(k1, g + 1, 3).then_inc(s_in, 1)


LB = -(-NT // QT)
LAST_K = LB - 1
assert NT == LAST_K * QT + 1 and LAST_K % 2 == 0
LCHUNKS = [(0, 4), (4, 8), (8, LB)]


def tiles(k):
    return range(k * QT, min(k * QT + QT, NT))


def slot(k):
    return 2 if k == LAST_K else k % 2


def before(k):
    return -1 if k == LAST_K else k - 2 if k >= 2 else k - 3


def bank_before(k):
    return k - 2 if k >= 1 else -1


CREDIT = 2 * LB


def deep(k):
    return 3 if k == LAST_K else k % 3


def before_deep(k):
    return -1 if k == LAST_K else k - 3 if k >= 3 else k - 4


WIDE = (QT, QT, 1)
DEEP = (QT, QT, QT, 1)
MW = 3 * F + 1


def layer0(nc, t, binned):
    with ExitStack() as ctx:
        sb = lambda n, s, d=F32: ctx.enter_context(nc.sbuf_tensor(n, s, d))
        pb = lambda n, s, d=F32: ctx.enter_context(nc.psum_tensor(n, s, d))
        sem = lambda n: ctx.enter_context(nc.semaphore(n))
        rec = sb("bin_row", [P, NT, REC])
        close = sb("edge_features", [P, NT, FE])
        places = [sb(f"places_spread{n}", [P, w * P], BF16) for n, w in enumerate(WIDE)]
        GT = [sb(f"gather{n}", [P, w * P], BF16) for n, w in enumerate(WIDE)]
        eT = [sb(f"edge_turned{n}", [w * FE, P]) for n, w in enumerate(WIDE)]
        S = [sb(f"scatter{n}", [P, w, P], BF16) for n, w in enumerate(DEEP)]
        msg = [sb(f"messages{n}", [P, w, MW], BF16) for n, w in enumerate(DEEP)]
        rest = [sb(f"rest_of_messages{n}", [P, w * F]) for n, w in enumerate(DEEP)]
        wd = sb("w1b_diagonal", [P, QT, F])
        pid = [pb(f"places{n}", [P, QT * P]) for n in range(2)]
        ptr = [pb(f"edges_turned{n}", [P, P]) for n in range(2)]
        pre = [pb(f"before_relu{n}", [P, QT * F]) for n in range(2)]
        acc = pb("sums", [P, MW])
        s_ld = [sem(f"row_in{c}") for c in range(3)]
        s_c, s_ids, s_pid, s_pl, s_tr, s_gt, s_et, s_pre, s_hi, s_rest, s_mid, s_msg, s_s, s_acc, s_out = (sem(n) for n in (
            "constants", "ids_ready", "places_up", "places_ready", "edges_turned", "gather_ready", "edges_ready", "sums_ready",
            "messages_hi", "rest_ready", "messages_mid", "messages_ready", "scatter_ready", "group_added", "row_kept"))
        block = ctx.enter_context(nc.Block())
        tiled = lambda a, n: a[:, 0:n * F].rearrange("p (t f) -> p t f", f=F)

        def load(sp, c, j):
            a, b = LCHUNKS[c][0] * QT, min(LCHUNKS[c][1] * QT, NT)
            sp.dma_start(rec[:, a:b, :], binned[ds(j * (P * SI), P * SI), :].rearrange("(p i) w -> p i w", i=SI)[:, a:b, :]).then_inc(s_ld[c], 16)

        @block.sync
        def _(sp):
            for c in range(3):
                load(sp, c, 0)
            with sp.Fori(1, NT) as j:
                for c, (a, b) in enumerate(LCHUNKS):
                    sp.wait_ge(s_s, (j - 1) * LB + CREDIT + b)
                    apart(sp, t)
                    sp.wait_ge(s_ids, (j - 1) * 3 + c + 1)
                    apart(sp, t)
                    load(sp, c, j)
            for c in range(2):
                sp.wait_ge(s_s, (NT - 1) * LB + CREDIT + LCHUNKS[c][1])
                sp.wait_ge(s_ids, (NT - 1) * 3 + c + 1)
                load(sp, c, NT)
            for c in range(2):
                sp.wait_ge(s_ld[c], 16 * (NT + 1))

        @block.gpsimd
        def _(pool):
            def keep_ids(c, j):
                a, b = LCHUNKS[c][0] * QT, min(LCHUNKS[c][1] * QT, NT)
                pool.wait_ge(s_ld[c], (j + 1) * 16)
                apart(pool, t)
                pool.tensor_copy(t["ids"][:, :, ds(j * NT + a, b - a)], rec[:, a:b, FE:FE + 2].rearrange("p t c -> p c t"))

            def draw_close(c, half, j):
                a, b = LCHUNKS[c][0] * QT, min(LCHUNKS[c][1] * QT, NT)
                a, b = ((a, a + 2 * QT), (a + 2 * QT, b))[half]
                pool.wait_ge(s_tr, (j - 1) * LB + CREDIT + LCHUNKS[c][1])
                apart(pool, t)
                last = pool.tensor_copy(close[:, a:b, :], rec[:, a:b, 0:FE])
                if half:
                    last.then_inc(s_ids, 1)

            pieces = {1: (2, 0), 2: (2, 1), 3: (2, 2), 5: (0, 0), 6: (0, 1), 7: (0, 2), 8: (1, 0), 9: (1, 1), 10: (1, 2)}

            def piece(c, part, j):
                if part:
                    draw_close(c, part - 1, j)
                else:
                    keep_ids(c, j)

            for c, part in ((0, 0), (0, 1), (0, 2), (1, 0), (1, 1), (1, 2)):
                piece(c, part, 0)
            with pool.Fori(0, NT) as j:
                for k in range(LB):
                    n = len(tiles(k))
                    pool.wait_ge(s_mid, j * LB + k + 1)
                    apart(pool, t)
                    pool.tensor_tensor(msg[deep(k)][:, :, 2 * F:3 * F], tiled(rest[deep(k)], n), msg[deep(k)][:, :, F:2 * F], ALU.subtract).then_inc(s_msg, 1)
                    if k in pieces:
                        piece(*pieces[k], j if k < 5 else j + 1)

        @block.vector
        def _(v):
            v.memset(wd[:, :, :], 0.0).then_inc(s_c, 1)
            for k in (LAST_K - 1, LAST_K):
                v.memset(S[deep(k)][:, :, :], 0.0)
            for m in msg:
                v.memset(m[:, :, 0:3 * F], 0.0)
                last = v.memset(m[:, :, 3 * F:MW], 1.0)
            v.wait_ge(s_c, 1)
            for q in range(QT):
                last = v.tensor_copy(wd[FE * q:FE * q + FE, q, :], t["w1b"][FE * q:FE * q + FE, :])
            last.then_inc(s_c, 1)
            v.wait_ge(s_c, 2)

            def gather(k, n):
                w = len(tiles(k)) * P
                v.wait_ge(s_pl, n + CREDIT + 1)
                v.wait_ge(s_pre, n + CREDIT - k + before(k) + 1)
                v.tensor_scalar(GT[slot(k)][:, 0:w], places[slot(k)][:, 0:w], t["part"][:, 0:1], None, ALU.is_equal).then_inc(s_gt, 1)

            def scatter(k, j):
                q = tiles(k)
                n = len(q)
                for c, (a, _) in enumerate(LCHUNKS):
                    if k == a:
                        v.wait_ge(s_ld[c], (j + 1) * 16)
                v.wait_ge(s_acc, j * LB + CREDIT + before_deep(k) + 1)
                v.tensor_tensor(S[deep(k)][:, 0:n, :], t["row"][:, :].rearrange("p (a n) -> p a n", a=1).to_broadcast([P, n, P]),
                                rec[:, q[0]:q[0] + n, FE + 1:FE + 2].to_broadcast([P, n, P]), ALU.is_equal).then_inc(s_s, 1)

            def keep_row(j):
                v.wait_ge(s_acc, (j + 1) * LB + CREDIT)
                to = t["sum"][:, ds(j + 1, 1), :].rearrange("p a f -> p (a f)")
                v.tensor_copy(to[:, F:F + 1], acc[:, 3 * F:MW])
                v.tensor_reduce(to[:, 0:F], acc[:, 0:3 * F].rearrange("p (c f) -> p f c", c=3), AX.X, ALU.add).then_inc(s_out, 1)

            gather(0, 0)
            with v.Fori(0, NT) as j:
                for k in range(LB):
                    n = len(tiles(k))
                    scatter(k, j)
                    gather((k + 1) % LB, j * LB + k + 1)
                    v.wait_ge(s_hi, j * LB + k + 1)
                    v.scalar_tensor_tensor(tiled(rest[deep(k)], n), tiled(pre[k % 2], n), 0.0, msg[deep(k)][:, :, 0:F], ALU.max, ALU.subtract).then_inc(s_rest, 1)
                    if k == 1:
                        keep_row(j - 1)
            keep_row(NT - 1)

        @block.scalar
        def _(act):
            def spread(k, n):
                w = len(tiles(k)) * P
                act.wait_ge(s_pid, n + 1)
                act.wait_ge(s_gt, n + CREDIT - k + before(k) + 1)
                act.copy(places[slot(k)][:, 0:w], pid[k % 2][:, 0:w]).then_inc(s_pl, 1)

            def edges(k, n):
                w = len(tiles(k)) * FE
                act.wait_ge(s_tr, n + CREDIT + 1)
                act.wait_ge(s_pre, n + CREDIT - k + before(k) + 1)
                act.copy(eT[slot(k)][0:w, :], ptr[k % 2][0:w, :]).then_inc(s_et, 1)

            def middle(k, j):
                n = len(tiles(k))
                act.wait_ge(s_rest, j * LB + CREDIT + k + 1)
                act.copy(msg[deep(k)][:, :, F:2 * F], tiled(rest[deep(k)], n)).then_inc(s_mid, 1)

            spread(0, 0)
            edges(0, 0)
            with act.Fori(0, NT) as j:
                for k in range(LB):
                    n = len(tiles(k))
                    k1 = (k + 1) % LB
                    spread(k1, j * LB + k + 1)
                    if k:
                        middle(k - 1, j)
                    edges(k1, j * LB + k + 1)
                    act.wait_ge(s_pre, j * LB + CREDIT + k + 1)
                    act.wait_ge(s_acc, j * LB + CREDIT + before_deep(k) + 1)
                    act.activation(msg[deep(k)][:, :, 0:F], tiled(pre[k % 2], n), ACT.Relu).then_inc(s_hi, 1)
                middle(LAST_K, j)

        @block.tensor
        def _(pe):
            def ids_up(k, n, j):
                q = tiles(k)
                for c, (a, _) in enumerate(LCHUNKS):
                    if k == a:
                        pe.wait_ge(s_ids, j * 3 + c + 1)
                pe.wait_ge(s_pl, n - k + CREDIT + bank_before(k) + 1)
                for m, i in enumerate(q):
                    last = pe.matmul(pid[k % 2][:, m * P:m * P + P], col(t["ids"][:, 0, ds(j * NT + i, 1)], P), t["idb"][:, :], start=True, stop=True)
                last.then_inc(s_pid, 1)
                pe.wait_ge(s_et, n - k + CREDIT + bank_before(k) + 1)
                pe.transpose(ptr[k % 2][0:len(q) * FE, :], close[:, q[0]:q[0] + len(q), :].rearrange("p t f -> p (t f)"), t["idf"][:, :]).then_inc(s_tr, 1)

            def sums(k, j):
                q = tiles(k)
                g = j * LB + k
                pe.wait_ge(s_et, g + CREDIT + 1)
                pe.wait_ge(s_rest, j * LB + CREDIT + bank_before(k) + 1)
                pe.matmul(pre[k % 2][:, 0:len(q) * F], eT[slot(k)][0:len(q) * FE, :], wd[0:len(q) * FE, 0:len(q), :], start=True, stop=False, skip_group_check=True)
                pe.wait_ge(s_gt, g + CREDIT + 1)
                for m, i in enumerate(q):
                    for part in range(3):
                        last = pe.matmul(pre[k % 2][:, m * F:m * F + F], GT[slot(k)][:, m * P:m * P + P], t["A3"][:, i, part, :],
                                         start=False, stop=(part == 2), skip_group_check=True)
                last.then_inc(s_pre, 1)

            def add(k, j):
                q = tiles(k)
                g = j * LB + k
                pe.wait_ge(s_msg, g + CREDIT + 1)
                pe.wait_ge(s_s, g + CREDIT + 1)
                if k == 0:
                    pe.wait_ge(s_out, j + 1)
                for m, i in enumerate(q):
                    last = pe.matmul(acc[:, :], S[deep(k)][:, m, :], msg[deep(k)][:, m, :], start=(i == 0), stop=(i == NT - 1), skip_group_check=True)
                last.then_inc(s_acc, 1)

            pe.wait_ge(s_c, 2)
            for s in (s_pl, s_tr, s_gt, s_et, s_pre, s_rest, s_msg, s_s):
                pe.sem_inc(s, CREDIT)
            pe.sem_inc(s_acc, CREDIT - 2)
            pe.matmul(acc[:, :], S[3][:, 0, :], msg[3][:, 0, :], start=True, stop=False, skip_group_check=True)
            ids_up(0, 0, 0)
            with pe.Fori(0, NT) as j:
                for k in range(LB):
                    k1 = (k + 1) % LB
                    ids_up(k1, j * LB + k + 1, j if k1 else j + 1)
                    sums(k, j)
                    add((k - 2) % LB, j if k >= 2 else j - 1)
            add(LAST_K - 1, NT - 1)
            add(LAST_K, NT - 1)

    beyond0(nc, t, binned)


def steps_beyond(eng, t):
    return eng.value_load(t["nover"][0:1, 0:1], min_val=1, max_val=EO // STEP)


def beyond_rows(binned, o, b, columns):
    return binned[ds(o * (STEP * P) + (MAIN + b * QT * P), QT * P), columns].rearrange("(q p) w -> p q w", p=P)


def beyond0(nc, t, binned):
    with ExitStack() as ctx:
        sb = lambda n, s, d=F32: [ctx.enter_context(nc.sbuf_tensor(f"beyond_{n}{b}", s, d)) for b in range(QB)]
        pb = lambda n, w: [ctx.enter_context(nc.psum_tensor(f"beyond_{n}{b}", [P, w], F32)) for b in range(QB)]
        sem = lambda n: ctx.enter_context(nc.semaphore(n))
        rec = sb("records", [P, QT, REC])
        close = sb("features", [P, QT * FE])
        ids = sb("places", [P, QT], BF16)
        at = sb("tiles", [1, QT, 2], I32)
        GT = sb("gather", [P, QT * P], BF16)
        S = sb("scatter", [P, QT, P])
        eT = sb("edges_turned", [P, P])
        msg = sb("messages", [P, QT, F + 1])
        wd = ctx.enter_context(nc.sbuf_tensor("beyond_w1b", [P, QT, F], F32))
        pid, ptr, pre, acc = pb("places_up", QT * P), pb("edges_up", P), pb("before_relu", QT * F), pb("sums", QT * (F + 1))
        s_ld = [sem(f"beyond_in{b}") for b in range(QB)]
        s_c, s_close, s_ids, s_at, s_pid, s_tr, s_gt, s_et, s_pre, s_msg, s_s, s_acc, s_out = (sem(n) for n in (
            "constants", "features_ready", "ids_ready", "tiles_known", "places_up", "edges_turned", "gather_ready", "edges_ready",
            "sums_ready", "messages_ready", "scatter_ready", "group_added", "group_kept"))
        block = ctx.enter_context(nc.Block())

        @block.sync
        def _(sp):
            with sp.Fori(0, steps_beyond(sp, t)) as o:
                for b in range(QB):
                    sp.wait_ge(s_s, o * QB + b + 1)
                    apart(sp, t)
                    sp.wait_ge(s_close, o * QB + b + 1)
                    apart(sp, t)
                    sp.dma_start(rec[b][:, :, :], beyond_rows(binned, o, b, slice(0, REC))).then_inc(s_ld[b], 16)

        @block.gpsimd
        def _(pool):
            with pool.Fori(0, steps_beyond(pool, t)) as o:
                for b in range(QB):
                    pool.wait_ge(s_ld[b], (o + 1) * 16)
                    pool.wait_ge(s_tr, o * QB + b + 1)
                    apart(pool, t)
                    pool.tensor_copy(close[b][:, :].rearrange("p (t f) -> p t f", f=FE), rec[b][:, :, 0:FE]).then_inc(s_close, 1)

        @block.vector
        def _(v):
            v.memset(wd[:, :, :], 0.0).then_inc(s_c, 1)
            for m in msg:
                v.memset(m[:, :, F:F + 1], 1.0)
            v.wait_ge(s_c, 1)
            for q in range(QT):
                last = v.tensor_copy(wd[FE * q:FE * q + FE, q, :], t["w1b"][FE * q:FE * q + FE, :])
            last.then_inc(s_c, 1)
            with v.Fori(0, steps_beyond(v, t)) as o:
                for b in range(QB):
                    v.wait_ge(s_ld[b], (o + 1) * 16)
                    v.tensor_copy(ids[b][:, :], rec[b][:, :, FE]).then_inc(s_ids, 1)
                    v.tensor_scalar(at[b][:, :, :], rec[b][0:1, :, FE + 2:FE + 4], 0.0, None, ALU.max).then_inc(s_at, 1)
                    v.tensor_tensor(S[b][:, :, :], t["row"][:, :].rearrange("p (a n) -> p a n", a=1).to_broadcast([P, QT, P]),
                                    rec[b][:, :, FE + 1:FE + 2].to_broadcast([P, QT, P]), ALU.is_equal).then_inc(s_s, 1)
                for b in range(QB):
                    v.wait_ge(s_pid, o * QB + b + 1)
                    v.tensor_scalar(GT[b][:, :], pid[b][:, :], t["part"][:, 0:1], None, ALU.is_equal).then_inc(s_gt, 1)
                v.wait_ge(s_at, (o + 1) * QB)
                apart(v, t)
                to = [[v.value_load(at[b][0:1, q, 1:2], min_val=0, max_val=NT - 1) for q in range(QT)] for b in range(QB)]
                for b in range(QB):
                    v.wait_ge(s_acc, o * QB + b + 1)
                    for q in range(QT):
                        row = t["sum"][:, ds(to[b][q] + 1, 1), :].rearrange("p a f -> p (a f)")
                        v.wait_ge(s_out, (o * QB + b) * QT + q + 1)
                        v.tensor_tensor(row, row, acc[b][:, q * (F + 1):(q + 1) * (F + 1)], ALU.add).then_inc(s_out, 1)

        @block.scalar
        def _(act):
            with act.Fori(0, steps_beyond(act, t)) as o:
                for b in range(QB):
                    act.wait_ge(s_tr, (o + 1) * QB + b + 1)
                    act.copy(eT[b][:, :], ptr[b][:, :]).then_inc(s_et, 1)
                for b in range(QB):
                    act.wait_ge(s_pre, o * QB + b + 1)
                    act.activation(msg[b][:, :, 0:F], pre[b][:, :].rearrange("p (t f) -> p t f", f=F), ACT.Relu).then_inc(s_msg, 1)

        @block.tensor
        def _(pe):
            pe.wait_ge(s_c, 2)
            pe.sem_inc(s_out, 1)
            for s in (s_s, s_close, s_tr):
                pe.sem_inc(s, QB)
            with pe.Fori(0, steps_beyond(pe, t)) as o:
                for b in range(QB):
                    pe.wait_ge(s_ids, o * QB + b + 1)
                    for q in range(QT):
                        last = pe.matmul(pid[b][:, q * P:q * P + P], col(ids[b][:, q:q + 1], P), t["idb"][:, :], start=True, stop=True)
                    last.then_inc(s_pid, 1)
                    pe.wait_ge(s_close, (o + 1) * QB + b + 1)
                    pe.transpose(ptr[b][:, :], close[b][:, :], t["idf"][:, :]).then_inc(s_tr, 1)
                for b in range(QB):
                    pe.wait_ge(s_at, o * QB + b + 1)
                    apart(pe, t)
                    of = [pe.value_load(at[b][0:1, q, 0:1], min_val=0, max_val=NT - 1) for q in range(QT)]
                    pe.wait_ge(s_et, o * QB + b + 1)
                    pe.matmul(pre[b][:, :], eT[b][:, :], wd[:, :, :], start=True, stop=False, skip_group_check=True)
                    pe.wait_ge(s_gt, o * QB + b + 1)
                    for q in range(QT):
                        for part in range(3):
                            last = pe.matmul(pre[b][:, q * F:q * F + F], GT[b][:, q * P:q * P + P],
                                             t["A3"][:, ds(of[q], 1), part, :].rearrange("p a f -> p (a f)"),
                                             start=False, stop=(part == 2), skip_group_check=True)
                    last.then_inc(s_pre, 1)
                for b in range(QB):
                    pe.wait_ge(s_msg, o * QB + b + 1)
                    pe.wait_ge(s_s, (o + 1) * QB + b + 1)
                    for q in range(QT):
                        last = pe.matmul(acc[b][:, q * (F + 1):(q + 1) * (F + 1)], S[b][:, q, :], msg[b][:, q, :], start=True, stop=True)
                    last.then_inc(s_acc, 1)


def nodes(nc, t):
    with ExitStack() as ctx:
        sb = lambda n, s, d=F32: ctx.enter_context(nc.sbuf_tensor(n, s, d))
        pb = lambda n, s, d=F32: ctx.enter_context(nc.psum_tensor(n, s, d))
        sem = lambda n: ctx.enter_context(nc.semaphore(n))
        sq = sb("sq2", [P, NT, F])
        y = sb("y", [P, NT, F])
        st = sb("st2", [P, 3, NT])
        deg = sb("degree", [P, NT])
        mT = sb("sums_turned", [F + 1, 2, QT * P])
        hT = sb("h_turned2", [F, 2, QT * P])
        rest = sb("rest2", [P, 2, 2, 3 * F])
        ptr = [pb(f"turned2_{i}", [P, QT * P]) for i in range(2)]
        pm = [pb(f"times_w2_{i}", [P, QT * F]) for i in range(2)]
        pq = [pb(f"qkv_sum{i}", [P, 2 * 3 * F]) for i in range(2)]
        s_v, s_tr, s_mT, s_pm, s_y, s_h, s_sqrt, s_tr2, s_hT, s_pq, s_hi, s_rest, s_mid, s_q = (sem(n) for n in (
            "v", "sums_turned", "sums_copied", "times_w2", "y_ready", "h_ready", "rooted", "h_turned", "h_copied", "qkv_up", "qkv_hi",
            "qkv_rest", "qkv_mid", "qkv_done"))
        block = ctx.enter_context(nc.Block())
        GB = -(-NT // QT)
        GQ = -(-NT // 2)

        @block.tensor
        def _(pe):
            for g in range(GB + 1):
                if g < GB:
                    m = min(QT, NT - QT * g)
                    if g >= 2:
                        pe.wait_ge(s_mT, g - 1)
                    for k in range(m):
                        last = pe.transpose(ptr[g % 2][0:F + 1, k * P:k * P + P], t["sum"][:, QT * g + k + 1, :], t["idf"][:, :])
                    last.then_inc(s_tr, 1)
                if g >= 1:
                    q = g - 1
                    m = min(QT, NT - QT * q)
                    pe.wait_ge(s_mT, q + 1)
                    if q >= 2:
                        pe.wait_ge(s_y, q - 1)
                    for k in range(m):
                        last = pe.matmul(pm[q % 2][:, k * F:k * F + F], mT[:, q % 2, k * P:k * P + P], t["w2"][:, :], start=True, stop=True)
                    last.then_inc(s_pm, 1)
            pe.wait_ge(s_h, 9)
            for g in range(GQ + 1):
                if g < GQ:
                    m = min(2, NT - 2 * g)
                    if g >= 2:
                        pe.wait_ge(s_hT, g - 1)
                    for k in range(m):
                        last = pe.transpose(ptr[g % 2][0:F, k * P:k * P + P], t["h"][:, 2 * g + k, :], t["idf"][:, :])
                    last.then_inc(s_tr2, 1)
                if g >= 1:
                    q = g - 1
                    m = min(2, NT - 2 * q)
                    pe.wait_ge(s_hT, q + 1)
                    if q >= 2:
                        pe.wait_ge(s_rest, q - 1)
                    for k in range(m):
                        last = pe.matmul(pq[q % 2][:, k * 3 * F:(k + 1) * 3 * F], hT[:, q % 2, k * P:k * P + P], t["wqkv"][:, :], start=True, stop=True)
                    last.then_inc(s_pq, 1)

        @block.scalar
        def _(act):
            for g in range(GB):
                n = min(QT, NT - QT * g)
                act.wait_ge(s_tr, g + 1)
                if g >= 2:
                    act.wait_ge(s_pm, g - 1)
                act.copy(mT[:, g % 2, 0:n * P], ptr[g % 2][0:F + 1, 0:n * P]).then_inc(s_mT, 1)
            for r in range(2):
                act.wait_ge(s_h, 4 * (r + 1))
                act.activation(st[:, 2, :], st[:, 1, :], ACT.Sqrt, bias=t["eps"][:, 0:1], scale=1.0 / F).then_inc(s_sqrt, 1)
            for g in range(GQ + 2):
                if g < GQ:
                    n = min(2, NT - 2 * g)
                    act.wait_ge(s_tr2, g + 1)
                    if g >= 2:
                        act.wait_ge(s_pq, g - 1)
                    act.copy(hT[:, g % 2, 0:n * P], ptr[g % 2][0:F, 0:n * P]).then_inc(s_hT, 1)
                if 1 <= g <= GQ:
                    q = g - 1
                    n = min(2, NT - 2 * q)
                    act.wait_ge(s_pq, q + 1)
                    act.copy(t["qkv"][:, 2 * q:2 * q + n, 0, :], pq[q % 2][:, 0:n * 3 * F].rearrange("p (t f) -> p t f", t=n)).then_inc(s_hi, 1)
                if g >= 2:
                    q = g - 2
                    n = min(2, NT - 2 * q)
                    act.wait_ge(s_rest, q + 1)
                    act.copy(t["qkv"][:, 2 * q:2 * q + n, 1, :], rest[:, q % 2, 0:n, :]).then_inc(s_mid, 1)

        @block.gpsimd
        def _(pool):
            pool.memset(t["qkv"][:, NT, :, :], 0.0)

        @block.vector
        def _(v):
            n = [0]

            def link(ins):
                n[0] += 1
                ins.then_inc(s_v, 1)
                v.wait_ge(s_v, n[0])

            b = lambda a: a.rearrange("p (t a) -> p t a", a=1).to_broadcast([P, NT, F])
            w = lambda a: a.rearrange("p (a f) -> p a f", a=1).to_broadcast([P, NT, F])
            link(v.tensor_scalar(deg[:, :], t["sum"][:, 1:NT + 1, F], 1.0, None, ALU.max))
            link(v.reciprocal(deg[:, :], deg[:, :]))
            for g in range(GB):
                m = min(QT, NT - QT * g)
                at = slice(QT * g, QT * g + m)
                v.wait_ge(s_pm, g + 1)
                v.tensor_tensor(y[:, at, :], pm[g % 2][:, 0:m * F].rearrange("p (t f) -> p t f", f=F),
                                deg[:, at].rearrange("p (t a) -> p t a", a=1).to_broadcast([P, m, F]), ALU.mult).then_inc(s_y, 1)
            v.wait_ge(s_y, GB)
            link(v.tensor_tensor(y[:, :, :], y[:, :, :], t["h"][:, 0:NT, :], ALU.add))
            layer_norm(v, link, y, y, sq, st, s_h, s_sqrt, 1)
            link(v.tensor_tensor(y[:, :, :], y[:, :, :], w(t["gb"][:, 0, :]), ALU.mult))
            link(v.tensor_tensor(y[:, :, :], y[:, :, :], w(t["gb"][:, 1, :]), ALU.add))
            link(v.tensor_tensor(t["x"][:, :, :], t["x"][:, :, :], y[:, :, :], ALU.add))
            layer_norm(v, link, t["x"], t["h"], sq, st, s_h, s_sqrt, 2)
            v.tensor_scalar(t["h"][:, 0:NT, :], t["h"][:, 0:NT, :], 0.0, None, ALU.max).then_inc(s_h, 1)
            for g in range(GQ + 1):
                if g < GQ:
                    m = min(2, NT - 2 * g)
                    v.wait_ge(s_hi, g + 1)
                    if g >= 2:
                        v.wait_ge(s_q, g - 1)
                    v.tensor_tensor(rest[:, g % 2, 0:m, :], pq[g % 2][:, 0:m * 3 * F].rearrange("p (t f) -> p t f", t=m),
                                    t["qkv"][:, 2 * g:2 * g + m, 0, :], ALU.subtract).then_inc(s_rest, 1)
                if g >= 1:
                    q = g - 1
                    m = min(2, NT - 2 * q)
                    v.wait_ge(s_mid, q + 1)
                    v.tensor_tensor(t["qkv"][:, 2 * q:2 * q + m, 2, :], rest[:, q % 2, 0:m, :], t["qkv"][:, 2 * q:2 * q + m, 1, :], ALU.subtract).then_inc(s_q, 1)


W = F + HEADS


def lasting(k):
    return 6 if k == LAST_K else k % 6


def before_lasting(k):
    return -1 if k == LAST_K else k - 6 if k >= 6 else k - 7


def layer1(nc, t, binned):
    with ExitStack() as ctx:
        sb = lambda n, s, d=F32: ctx.enter_context(nc.sbuf_tensor(n, s, d))
        pb = lambda n, s, d=F32: ctx.enter_context(nc.psum_tensor(n, s, d))
        sem = lambda n: ctx.enter_context(nc.semaphore(n))
        warm = sb("warm", [1, 1])
        GTs = [sb(f"gather_src{n}", [P, w * P], BF16) for n, w in enumerate(WIDE)]
        places = [sb(f"dst_places{n}", [P, w * P], BF16) for n, w in enumerate(WIDE)]
        GTd = [sb(f"gather_dst{n}", [P, w * P], BF16) for n, w in enumerate(WIDE)]
        S = [sb(f"scatter1_{n}", [P, w, P], BF16) for n, w in enumerate((QT,) * 6 + (1,))]
        qs = [sb(f"queries{n}", [P, w, F]) for n, w in enumerate(WIDE)]
        prod = [sb(f"products{n}", [P, w, F]) for n, w in enumerate(WIDE)]
        att = [sb(f"scores{n}", [P, w, HEADS]) for n, w in enumerate(WIDE)]
        msg = [sb(f"messages1_{n}", [P, w, W]) for n, w in enumerate(DEEP)]
        rest = [sb(f"rest_of_messages1_{n}", [P, w, W]) for n, w in enumerate(DEEP)]
        parts = [sb(f"message_parts{n}", [P, w, 3, W], BF16) for n, w in enumerate(DEEP)]
        pst, pid = pb("scatter_turned", [P, QT * P], BF16), pb("dst_places_up", [P, QT * P])
        pq = [pb(f"q_up{n}", [P, QT * F]) for n in range(2)]
        pkv = [pb(f"kv_up{n}", [P, w * 2 * F]) for n, w in enumerate(WIDE)]
        acc = pb("sums1", [P, 3 * W])
        names = ("constants", "dst_up", "places_ready", "src_turned", "src_gather", "dst_gather", "scatter_ready", "q_up", "kv_up",
                 "q_ready", "products_ready", "scores_ready", "clipped", "exp_ready", "messages_ready", "part_hi", "rest_ready",
                 "part_mid", "parts_ready", "group_added", "row_kept")
        (s_c, s_id, s_pl, s_t, s_gs, s_gd, s_s, s_pq, s_kv, s_q, s_pr, s_sc, s_cl, s_ex, s_msg, s_hi, s_rest, s_mid, s_mb, s_acc,
         s_out) = (sem(n) for n in names)
        block = ctx.enter_context(nc.Block())

        @block.gpsimd
        def _(pool):
            def after_first(k, n):
                o = deep(k)
                pool.wait_ge(s_hi, n + CREDIT + 1)
                apart(pool, t)
                pool.tensor_tensor(rest[o][:, :, :], msg[o][:, :, :], parts[o][:, :, 0, :], ALU.subtract).then_inc(s_rest, 1)

            def third_part(k, n):
                o = deep(k)
                pool.wait_ge(s_mid, n + CREDIT + 1)
                apart(pool, t)
                pool.tensor_tensor(parts[o][:, :, 2, :], rest[o][:, :, :], parts[o][:, :, 1, :], ALU.subtract).then_inc(s_mb, 1)

            pool.wait_ge(s_c, 1)
            apart(pool, t)
            with pool.Fori(0, NT) as i:
                for k in range(LB):
                    g = i * LB + k
                    pool.wait_ge(s_sc, g + 1)
                    apart(pool, t)
                    pool.tensor_scalar(att[slot(k)][:, :, :], att[slot(k)][:, :, :], 10.0, -10.0, ALU.min, ALU.max).then_inc(s_cl, 1)
                    third_part((k - 2) % LB, g - 2)
                    after_first((k - 1) % LB, g - 1)
            third_part(LAST_K - 1, NT * LB - 2)
            after_first(LAST_K, NT * LB - 1)
            third_part(LAST_K, NT * LB - 1)

        @block.vector
        def _(v):
            def scatter(k, n, i):
                q = tiles(k)
                w = len(q)
                v.wait_ge(s_acc, n - k + CREDIT + before_lasting(k) + 1)
                at = t["ids"][:, 0, ds(i + q[0] * NT, w * NT)].rearrange("p (t i) -> p t i", i=NT)[:, :, 0:1]
                v.tensor_tensor(S[lasting(k)][:, :, :], t["rowb"][:, :].rearrange("p (a n) -> p a n", a=1).to_broadcast([P, w, P]),
                                at.to_broadcast([P, w, P]), ALU.is_equal).then_inc(s_s, 1)

            def gather(k, n):
                w = len(tiles(k)) * P
                v.wait_ge(s_pl, n + 1)
                v.wait_ge(s_kv, n - k + CREDIT + before(k) + 1)
                v.tensor_scalar(GTd[slot(k)][:, 0:w], places[slot(k)][:, 0:w], t["part"][:, 0:1], None, ALU.is_equal).then_inc(s_gd, 1)

            def keep_row(i):
                v.wait_ge(s_acc, (i + 1) * LB + CREDIT)
                v.tensor_reduce(t["out"][:, ds(i + 1, 1), :].rearrange("p a f -> p (a f)"), acc[:, :].rearrange("p (c f) -> p f c", c=3),
                                AX.X, ALU.add).then_inc(s_out, 1)

            for k in range(LAST_K - 2, LB):
                v.memset(S[lasting(k)][:, :, :], 0.0)
                v.memset(parts[deep(k)][:, :, :, :], 0.0)
            v.memset(msg[deep(LAST_K)][:, :, :], 0.0)
            for k in (LAST_K - 1, LAST_K):
                last = v.memset(rest[deep(k)][:, :, :], 0.0)
            last.then_inc(s_c, 1)
            for k in range(2):
                scatter(k, k, 0)
            gather(0, 0)
            with v.Fori(0, NT) as i:
                for k in range(LB):
                    n = len(tiles(k))
                    g = i * LB + k
                    o = slot(k)
                    k1, k2 = (k + 1) % LB, (k + 2) % LB
                    kv = pkv[o][:, :].rearrange("p (t f) -> p t f", f=2 * F)
                    heads = lambda a: a.rearrange("p t (h d) -> p t h d", h=HEADS)
                    v.wait_ge(s_q, g + CREDIT + 1)
                    v.wait_ge(s_kv, g + CREDIT + 1)
                    v.tensor_tensor(prod[o][:, :, :], qs[o][:, :, :], kv[:, :, 0:F], ALU.mult).then_inc(s_pr, 1)
                    gather(k1, g + 1)
                    v.wait_ge(s_pr, g + CREDIT + 1)
                    v.tensor_reduce(att[o][:, :, :], heads(prod[o][:, :, :]), AX.X, ALU.add).then_inc(s_sc, 1)
                    scatter(k2, g + 2, i if k2 == k + 2 else i + 1)
                    v.wait_ge(s_ex, g + 1)
                    to = msg[deep(k)]
                    v.tensor_tensor(heads(to[:, :, 0:F]), heads(kv[:, :, F:2 * F]),
                                    to[:, :, F:W].rearrange("p t (h a) -> p t h a", a=1).to_broadcast([P, n, HEADS, HD]), ALU.mult).then_inc(s_msg, 1)
                    if k == 2:
                        keep_row(i - 1)
            keep_row(NT - 1)

        @block.scalar
        def _(act):
            def spread(k, n):
                w = len(tiles(k)) * P
                act.wait_ge(s_id, n + 1)
                act.wait_ge(s_gd, n - k + CREDIT + before(k) + 1)
                act.copy(places[slot(k)][:, 0:w], pid[:, 0:w]).then_inc(s_pl, 1)

            def turned(k, n):
                w = len(tiles(k)) * P
                act.wait_ge(s_t, n + 1)
                act.wait_ge(s_pq, n - k + CREDIT + before(k) + 1)
                act.copy(GTs[slot(k)][:, 0:w], pst[:, 0:w]).then_inc(s_gs, 1)

            def queries(k, n):
                w = len(tiles(k))
                act.wait_ge(s_pq, n + CREDIT + 1)
                act.wait_ge(s_pr, n - k + CREDIT + before(k) + 1)
                act.copy(qs[slot(k)][:, :, :], pq[k % 2][:, 0:w * F].rearrange("p (t f) -> p t f", f=F)).then_inc(s_q, 1)

            def first_part(k, n):
                act.wait_ge(s_msg, n + CREDIT + 1)
                act.wait_ge(s_acc, n - k + CREDIT + before_deep(k) + 1)
                act.copy(parts[deep(k)][:, :, 0, :], msg[deep(k)][:, :, :]).then_inc(s_hi, 1)

            def second_part(k, n):
                act.wait_ge(s_rest, n + CREDIT + 1)
                act.copy(parts[deep(k)][:, :, 1, :], rest[deep(k)][:, :, :]).then_inc(s_mid, 1)

            act.wait_ge(s_c, 1)
            act.activation(warm[:, :], t["eps"][0:1, 0:1], ACT.Exp)
            for k in range(2):
                spread(k, k)
                turned(k, k)
            queries(0, 0)
            with act.Fori(0, NT) as i:
                for k in range(LB):
                    g = i * LB + k
                    k1, k2 = (k + 1) % LB, (k + 2) % LB
                    first_part((k - 1) % LB, g - 1)
                    second_part((k - 2) % LB, g - 2)
                    spread(k2, g + 2)
                    act.wait_ge(s_cl, g + 1)
                    act.wait_ge(s_rest, g - k + CREDIT + before_deep(k) + 1)
                    act.activation(msg[deep(k)][:, :, F:W], att[slot(k)][:, :, :], ACT.Exp).then_inc(s_ex, 1)
                    queries(k1, g + 1)
                    turned(k2, g + 2)
            second_part(LAST_K - 1, NT * LB - 2)
            first_part(LAST_K, NT * LB - 1)
            second_part(LAST_K, NT * LB - 1)

        @block.tensor
        def _(pe):
            def places_up(k, n, i):
                if not isinstance(n, int) or n:
                    pe.wait_ge(s_pl, n)
                for m, j in enumerate(tiles(k)):
                    last = pe.matmul(pid[:, m * P:m * P + P], col(t["ids"][:, 1, ds(i + j * NT, 1)], P), t["idb"][:, :], start=True, stop=True)
                last.then_inc(s_id, 1)

            def turn(k, n):
                if not isinstance(n, int) or n:
                    pe.wait_ge(s_gs, n)
                pe.wait_ge(s_s, n + 1)
                for m in range(len(tiles(k))):
                    last = pe.transpose(pst[:, m * P:m * P + P], S[lasting(k)][:, m, :], t["idb"][:, :])
                last.then_inc(s_t, 1)

            def queries_up(k, n, i):
                pe.wait_ge(s_gs, n + 1)
                pe.wait_ge(s_q, n - k + CREDIT + bank_before(k) + 1)
                for m in range(len(tiles(k))):
                    for part in range(3):
                        last = pe.matmul(pq[k % 2][:, m * F:m * F + F], GTs[slot(k)][:, m * P:m * P + P],
                                         t["qkv"][:, ds(i, 1), part, 0:F].rearrange("p a f -> p (a f)"), start=(part == 0), stop=(part == 2))
                last.then_inc(s_pq, 1)

            def keys_and_values_up(k, n):
                pe.wait_ge(s_gd, n + CREDIT + 1)
                pe.wait_ge(s_msg, n - k + CREDIT + before(k) + 1)
                for m, j in enumerate(tiles(k)):
                    for part in range(3):
                        last = pe.matmul(pkv[slot(k)][:, m * 2 * F:(m + 1) * 2 * F], GTd[slot(k)][:, m * P:m * P + P], t["qkv"][:, j, part, F:3 * F],
                                         start=(part == 0), stop=(part == 2))
                last.then_inc(s_kv, 1)

            def add(k, n, i):
                pe.wait_ge(s_mb, n + CREDIT + 1)
                if k == 0:
                    pe.wait_ge(s_out, i + 1)
                for m, j in enumerate(tiles(k)):
                    last = pe.matmul(acc[:, :], S[lasting(k)][:, m, :], parts[deep(k)][:, m, :, :].rearrange("p c f -> p (c f)"),
                                     start=(j == 0), stop=(j == NT - 1), skip_group_check=True)
                last.then_inc(s_acc, 1)

            for s in (s_kv, s_pq, s_pr, s_q, s_gd, s_msg):
                pe.sem_inc(s, CREDIT)
            for s in (s_hi, s_rest):
                pe.sem_inc(s, CREDIT - 1)
            for s in (s_mid, s_mb):
                pe.sem_inc(s, CREDIT - 2)
            pe.sem_inc(s_acc, CREDIT - 3)
            pe.wait_ge(s_c, 1)
            last = S[lasting(LAST_K)][:, 0, :]
            pe.matmul(acc[:, 0:P], last, last, start=True, stop=False, skip_group_check=True)
            pe.matmul(acc[:, P:3 * W], last, last[:, 0:3 * W - P], start=True, stop=False, skip_group_check=True)
            for k in range(2):
                places_up(k, k, 0)
                turn(k, k)
            queries_up(0, 0, 0)
            keys_and_values_up(0, 0)
            with pe.Fori(0, NT) as i:
                for k in range(LB):
                    g = i * LB + k
                    k1, k2 = (k + 1) % LB, (k + 2) % LB
                    places_up(k2, g + 2, i if k2 == k + 2 else i + 1)
                    queries_up(k1, g + 1, i if k1 else i + 1)
                    keys_and_values_up(k1, g + 1)
                    turn(k2, g + 2)
                    add((k - 3) % LB, g - 3, i)
            for k in range(LAST_K - 2, LB):
                add(k, (NT - 1) * LB + k, NT)

    beyond1(nc, t, binned)


def beyond1(nc, t, binned):
    with ExitStack() as ctx:
        sb = lambda n, s, d=F32: [ctx.enter_context(nc.sbuf_tensor(f"beyond1_{n}{b}", s, d)) for b in range(QB)]
        pb = lambda n, w, k=QB: [ctx.enter_context(nc.psum_tensor(f"beyond1_{n}{b}", [P, w], F32)) for b in range(k)]
        sem = lambda n: ctx.enter_context(nc.semaphore(n))
        rec = sb("records", [P, QT, 4])
        ids = sb("places", [P, 2, QT], BF16)
        sum_at = sb("tiles_as_one", [1, QT])
        at = sb("tiles", [1, QT], I32)
        GT = sb("gather", [P, 2, QT * P], BF16)
        S = sb("scatter", [P, QT, P])
        qs = sb("queries", [P, QT, F])
        prod = sb("products", [P, QT, F])
        att = sb("scores", [P, QT, HEADS])
        msg = sb("messages", [P, QT, W])
        (pis, pid), pq, pkv, acc = pb("places_up", QT * P), pb("q_up", QT * F), pb("kv_up", QT * 2 * F), pb("sums", QT * W)
        s_ld = [sem(f"beyond1_in{b}") for b in range(QB)]
        names = ("ids_ready1", "tiles_known1", "places_up1", "gathers_ready", "scatter_ready1", "q_up1", "kv_up1", "q_ready1",
                 "products_ready1", "scores_ready1", "clipped1", "exp_ready1", "messages_ready1", "group_added1", "group_kept1")
        s_sum = sem("tiles_summed1")
        s_ids, s_at, s_up, s_gt, s_s, s_pq, s_kv, s_q, s_pr, s_sc, s_cl, s_ex, s_msg, s_acc, s_out = (sem(n) for n in names)
        block = ctx.enter_context(nc.Block())
        heads = lambda a: a.rearrange("p t (h d) -> p t h d", h=HEADS)

        def source_of(v):
            return v // SI

        @block.sync
        def _(sp):
            with sp.Fori(0, steps_beyond(sp, t)) as o:
                for b in range(QB):
                    sp.wait_ge(s_s, o * QB + b + 1)
                    apart(sp, t)
                    sp.dma_start(rec[b][:, :, :], beyond_rows(binned, o, b, slice(FE, REC))).then_inc(s_ld[b], 16)

        @block.vector
        def _(v):
            with v.Fori(0, steps_beyond(v, t)) as o:
                for b in range(QB):
                    v.wait_ge(s_ld[b], (o + 1) * 16)
                    v.tensor_copy(ids[b][:, :, :], rec[b][:, :, 0:2].rearrange("p t c -> p c t")).then_inc(s_ids, 1)
                    v.scalar_tensor_tensor(sum_at[b][:, :], rec[b][0:1, :, 2], float(SI), rec[b][0:1, :, 3], ALU.mult, ALU.add).then_inc(s_sum, 1)
                    v.tensor_tensor(S[b][:, :, :], t["row"][:, :].rearrange("p (a n) -> p a n", a=1).to_broadcast([P, QT, P]),
                                    rec[b][:, :, 0:1].to_broadcast([P, QT, P]), ALU.is_equal).then_inc(s_s, 1)
                    v.wait_ge(s_sum, o * QB + b + 1)
                    v.tensor_scalar(at[b][:, :], sum_at[b][:, :], 0.0, None, ALU.max).then_inc(s_at, 1)
                to = []
                for b in range(QB):
                    v.wait_ge(s_up, o * QB + b + 1)
                    v.tensor_scalar(GT[b][:, 0, :], pis[:, :], t["part"][:, 0:1], None, ALU.is_equal)
                    v.tensor_scalar(GT[b][:, 1, :], pid[:, :], t["part"][:, 0:1], None, ALU.is_equal).then_inc(s_gt, 1)
                    v.wait_ge(s_at, o * QB + b + 1)
                    apart(v, t)
                    to.append([source_of(v.value_load(at[b][0:1, q:q + 1], min_val=0, max_val=SI * NT - 1)) for q in range(QT)])
                for b in range(QB):
                    g = o * QB + b
                    kv = pkv[b][:, :].rearrange("p (t f) -> p t f", f=2 * F)
                    v.wait_ge(s_q, g + 1)
                    v.wait_ge(s_kv, g + 1)
                    v.tensor_tensor(prod[b][:, :, :], qs[b][:, :, :], kv[:, :, 0:F], ALU.mult).then_inc(s_pr, 1)
                    v.wait_ge(s_pr, g + 1)
                    v.tensor_reduce(att[b][:, :, :], heads(prod[b][:, :, :]), AX.X, ALU.add).then_inc(s_sc, 1)
                    v.wait_ge(s_sc, g + 1)
                    v.tensor_scalar(att[b][:, :, :], att[b][:, :, :], 10.0, -10.0, ALU.min, ALU.max).then_inc(s_cl, 1)
                    v.wait_ge(s_ex, g + 1)
                    v.tensor_tensor(heads(msg[b][:, :, 0:F]), heads(kv[:, :, F:2 * F]),
                                    msg[b][:, :, F:W].rearrange("p t (h a) -> p t h a", a=1).to_broadcast([P, QT, HEADS, HD]), ALU.mult).then_inc(s_msg, 1)
                for b in range(QB):
                    v.wait_ge(s_acc, o * QB + b + 1)
                    for q in range(QT):
                        row = t["out"][:, ds(to[b][q] + 1, 1), :].rearrange("p a f -> p (a f)")
                        v.wait_ge(s_out, (o * QB + b) * QT + q + 1)
                        v.tensor_tensor(row, row, acc[b][:, q * W:(q + 1) * W], ALU.add).then_inc(s_out, 1)

        @block.scalar
        def _(act):
            with act.Fori(0, steps_beyond(act, t)) as o:
                for b in range(QB):
                    act.wait_ge(s_pq, o * QB + b + 1)
                    act.copy(qs[b][:, :, :], pq[b][:, :].rearrange("p (t f) -> p t f", f=F)).then_inc(s_q, 1)
                    act.wait_ge(s_cl, o * QB + b + 1)
                    act.activation(msg[b][:, :, F:W], att[b][:, :, :], ACT.Exp).then_inc(s_ex, 1)

        @block.tensor
        def _(pe):
            def places(b, o):
                pe.wait_ge(s_ids, o * QB + b + 1)
                for side, bank in ((0, pis), (1, pid)):
                    for q in range(QT):
                        last = pe.matmul(bank[:, q * P:q * P + P], col(ids[b][:, side, q:q + 1], P), t["idb"][:, :], start=True, stop=True)
                last.then_inc(s_up, 1)

            def known(b, o):
                pe.wait_ge(s_at, o * QB + b + 1)
                apart(pe, t)
                both = [pe.value_load(at[b][0:1, q:q + 1], min_val=0, max_val=SI * NT - 1) for q in range(QT)]
                return [source_of(v) for v in both], [nc.s_assert_within(v % SI, 0, NT - 1, skip_runtime_bounds_check_because="a record holds tiles below NT, and the filler is clamped to 0") for v in both]

            def gathered(b, o, tile):
                pe.wait_ge(s_gt, o * QB + b + 1)
                for side, bank, first, end, up in ((0, pq[b], 0, F, s_pq), (1, pkv[b], F, 3 * F, s_kv)):
                    for q in range(QT):
                        for part in range(3):
                            last = pe.matmul(bank[:, q * (end - first):(q + 1) * (end - first)], GT[b][:, side, q * P:q * P + P],
                                             t["qkv"][:, ds(tile[side][q], 1), part, first:end].rearrange("p a f -> p (a f)"),
                                             start=(part == 0), stop=(part == 2))
                    last.then_inc(up, 1)

            pe.sem_inc(s_out, 1)
            pe.sem_inc(s_s, QB)
            with pe.Fori(0, steps_beyond(pe, t)) as o:
                places(0, o)
                tile = known(0, o)
                pe.wait_ge(s_gt, o * QB + 1)
                places(1, o)
                gathered(0, o, tile)
                tile = known(1, o)
                gathered(1, o, tile)
                for b in range(QB):
                    pe.wait_ge(s_msg, o * QB + b + 1)
                    pe.wait_ge(s_s, (o + 1) * QB + b + 1)
                    for q in range(QT):
                        last = pe.matmul(acc[b][:, q * W:(q + 1) * W], S[b][:, q, :], msg[b][:, q, :], start=True, stop=True)
                    last.then_inc(s_acc, 1)


def finish(nc, t, out):
    with ExitStack() as ctx:
        den = ctx.enter_context(nc.sbuf_tensor("denominators", [P, NT, HEADS], F32))
        s_v, s_o = (ctx.enter_context(nc.semaphore(n)) for n in ("v_out", "written"))
        block = ctx.enter_context(nc.Block())

        @block.vector
        def _(v):
            n = [0]

            def link(ins):
                n[0] += 1
                ins.then_inc(s_v, 1)
                v.wait_ge(s_v, n[0])

            link(v.tensor_scalar(den[:, :, :], t["out"][:, 1:NT + 1, F:W], 1e-8, None, ALU.add))
            link(v.reciprocal(den[:, :, :], den[:, :, :]))
            for h in range(HEADS):
                a = t["out"][:, 1:NT + 1, h * HD:(h + 1) * HD]
                last = v.tensor_tensor(a, a, den[:, :, h:h + 1].to_broadcast([P, NT, HD]), ALU.mult)
            link(last)
            v.tensor_tensor(t["x"][:, :, :], t["x"][:, :, :], t["out"][:, 1:NT + 1, 0:F], ALU.add).then_inc(s_v, 1)

        @block.sync
        def _(sp):
            sp.wait_ge(s_v, 4)
            sp.dma_start(out[0:(NT - 1) * P, :].rearrange("(t p) f -> p t f", p=P), t["x"][:, 0:NT - 1, :]).then_inc(s_o, 16)
            sp.dma_start(out[(NT - 1) * P:N_NODES, :], t["x"][0:LAST, NT - 1, :]).then_inc(s_o, 16)
            sp.wait_ge(s_o, 32)


def kernel(x, src, dst, edge_attr_32, L0_gnn_W1, L0_gnn_b1, L0_gnn_W2, L0_gnn_b2, L0_gnn_gamma, L0_gnn_beta,
           L1_gnn_qTrans, L1_gnn_kTrans, L1_gnn_vTrans):
    import numpy as np
    import concourse.bacc as bacc
    from concourse.bass_utils import run_bass_kernel_spmd

    pad = ET * P - N_EDGES
    across = lambda a: np.ascontiguousarray(a.reshape(ET, P, *a.shape[1:]).swapaxes(0, 1))

    def node_ids(a):
        a = np.asarray(a)
        return across(np.concatenate([a, np.full(pad, NT * P, a.dtype)]))

    arrays = {
        "x_in": np.asarray(x), "src": node_ids(src), "dst": node_ids(dst),
        "edge": across(np.concatenate([np.asarray(edge_attr_32), np.zeros((pad, FE), np.float32)])),
        "w1": np.asarray(L0_gnn_W1), "b1": np.asarray(L0_gnn_b1), "w2": np.asarray(L0_gnn_W2), "b2": np.asarray(L0_gnn_b2),
        "gamma": np.asarray(L0_gnn_gamma), "beta": np.asarray(L0_gnn_beta),
        "wq": np.asarray(L1_gnn_qTrans), "wk": np.asarray(L1_gnn_kTrans), "wv": np.asarray(L1_gnn_vTrans),
    }
    nc = bacc.Bacc("TRN2", target_bir_lowering=False, num_devices=1)
    args = [nc.dram_tensor(n, a.shape, mybir.dt.from_np(a.dtype), kind="ExternalInput").ap() for n, a in arrays.items()]
    out = nc.dram_tensor("out", (N_NODES, F), F32, kind="ExternalOutput").ap()
    gnn(nc, *args, out)
    r = run_bass_kernel_spmd(nc, [arrays], core_ids=[0])
    return r.results[0]["out"]
```
